# Optimizing a Trainium2 kernel written in Bass

```python
import numpy as np
import jax
import jax.numpy as jnp

def _softmax(x, axis=-1):
    return jax.nn.softmax(x, axis=axis)

def _gelu(x):
    return jax.nn.gelu(x, approximate=True)

def _silu(x):
    return jax.nn.silu(x)

def _sigmoid(x):
    return jax.nn.sigmoid(x)

def _layernorm(x, axis=-1, eps=1e-05):
    m = jnp.mean(x, axis=axis, keepdims=True)
    v = jnp.var(x, axis=axis, keepdims=True)
    return (x - m) / jnp.sqrt(v + eps)

def _scatter_add(tgt, idx, src, axis=0):
    return tgt.at[idx].add(src)

def _segment_sum(src, seg, n):
    return jax.ops.segment_sum(src, seg, n)
kernel_name = 'mk_seq_postln_d1_jaxref_r8_bb4353'

def setup_inputs(seed: int=0):
    np.random.seed(seed)
    _w = jnp.asarray

    def _L0_attn_setup():
        import jax, jax.numpy as jnp
        import numpy as np
        HEADS = 16
        KV_HEADS = 4
        DIM_HEAD = 128
        DIM = 256
        ROPE_BASE = 10000.0

        def rotate_half(t):
            t1, t2 = jnp.split(t, 2, axis=-1)
            return jnp.concatenate((-t2, t1), axis=-1)

        def apply_rotary(t, cos, sin):
            return t * cos + rotate_half(t) * sin
        key = jax.random.key(seed)
        ks = jax.random.split(key, 6)
        b, n = (4, 128)
        s = 1.0 / np.sqrt(DIM)
        x = jax.random.normal(ks[0], (b, n, DIM), dtype=jnp.float32)
        Wq = jax.random.normal(ks[1], (DIM, HEADS * DIM_HEAD), dtype=jnp.float32) * s
        Wk = jax.random.normal(ks[2], (DIM, KV_HEADS * DIM_HEAD), dtype=jnp.float32) * s
        Wv = jax.random.normal(ks[3], (DIM, KV_HEADS * DIM_HEAD), dtype=jnp.float32) * s
        Wo = jax.random.normal(ks[4], (HEADS * DIM_HEAD, DIM), dtype=jnp.float32) * s
        head_scale = 1.0 + 0.02 * jax.random.normal(ks[5], (1, HEADS, 1, 1), dtype=jnp.float32)
        return {'x': x, 'Wq': Wq, 'Wk': Wk, 'Wv': Wv, 'Wo': Wo, 'head_scale': head_scale}
    _L0_attn_in = _L0_attn_setup()

    def _L0_ffn_setup():
        import jax, jax.numpy as jnp
        import numpy as np
        LN_EPS = 1e-05
        L2_EPS = 1e-12

        def _l2norm(v, axis):
            n = jnp.sqrt(jnp.sum(v * v, axis=axis, keepdims=True))
            return v / jnp.maximum(n, L2_EPS)
        key = jax.random.key(seed)
        ks = jax.random.split(key, 4)
        B, N, D, E, S, H = (8, 256, 256, 16, 128, 64)
        x = jax.random.normal(ks[0], (B, N, D), dtype=jnp.float32)
        mu = jax.random.normal(ks[1], (D, E, S), dtype=jnp.float32) / np.sqrt(D)
        W1 = jax.random.normal(ks[2], (E, D, H), dtype=jnp.float32) * np.sqrt(2.0 / D)
        W2 = jax.random.normal(ks[3], (E, H, D), dtype=jnp.float32) * np.sqrt(2.0 / (H + D))
        return {'x': x, 'gamma': jnp.ones((D,), jnp.float32), 'beta': jnp.zeros((D,), jnp.float32), 'mu': mu, 'scale': jnp.ones((1,), jnp.float32), 'W1': W1, 'b1': jnp.zeros((E, H), jnp.float32), 'W2': W2, 'b2': jnp.zeros((E, D), jnp.float32)}
    _L0_ffn_in = _L0_ffn_setup()
    _d = {'L0_attn_x': _L0_attn_in['x'], 'L0_attn_Wq': _L0_attn_in['Wq'], 'L0_attn_Wk': _L0_attn_in['Wk'], 'L0_attn_Wv': _L0_attn_in['Wv'], 'L0_attn_Wo': _L0_attn_in['Wo'], 'L0_attn_head_scale': _L0_attn_in['head_scale'], 'L0_ffn_gamma': _L0_ffn_in['gamma'], 'L0_ffn_beta': _L0_ffn_in['beta'], 'L0_ffn_mu': _L0_ffn_in['mu'], 'L0_ffn_scale': _L0_ffn_in['scale'], 'L0_ffn_W1': _L0_ffn_in['W1'], 'L0_ffn_b1': _L0_ffn_in['b1'], 'L0_ffn_W2': _L0_ffn_in['W2'], 'L0_ffn_b2': _L0_ffn_in['b2']}
    _x0 = _d['L0_attn_x']
    _d['L0_attn_x'] = jax.random.normal(jax.random.fold_in(jax.random.key(seed), 1), (2, 1024, 256), dtype=_x0.dtype)
    del _x0
    return _d

def reference(L0_attn_x, L0_attn_Wq, L0_attn_Wk, L0_attn_Wv, L0_attn_Wo, L0_attn_head_scale, L0_ffn_gamma, L0_ffn_beta, L0_ffn_mu, L0_ffn_scale, L0_ffn_W1, L0_ffn_b1, L0_ffn_W2, L0_ffn_b2):

    def _L0_attn_ref(x, Wq, Wk, Wv, Wo, head_scale):
        import jax, jax.numpy as jnp
        import numpy as np
        HEADS = 16
        KV_HEADS = 4
        DIM_HEAD = 128
        DIM = 256
        ROPE_BASE = 10000.0

        def rotate_half(t):
            t1, t2 = jnp.split(t, 2, axis=-1)
            return jnp.concatenate((-t2, t1), axis=-1)

        def apply_rotary(t, cos, sin):
            return t * cos + rotate_half(t) * sin
        b, n, _ = x.shape
        q = (x @ Wq).reshape(b, n, HEADS, DIM_HEAD).transpose(0, 2, 1, 3)
        k = (x @ Wk).reshape(b, n, KV_HEADS, DIM_HEAD).transpose(0, 2, 1, 3)
        v = (x @ Wv).reshape(b, n, KV_HEADS, DIM_HEAD).transpose(0, 2, 1, 3)
        inv_freq = 1.0 / ROPE_BASE ** (jnp.arange(0, DIM_HEAD, 2, dtype=jnp.float32) / DIM_HEAD)
        freqs = jnp.arange(n, dtype=jnp.float32)[:, None] * inv_freq[None, :]
        emb = jnp.concatenate((freqs, freqs), axis=-1)
        cos, sin = (jnp.cos(emb), jnp.sin(emb))
        q = apply_rotary(q, cos, sin)
        k = apply_rotary(k, cos, sin)
        rep = HEADS // KV_HEADS
        k = jnp.repeat(k, rep, axis=1)
        v = jnp.repeat(v, rep, axis=1)
        scale = 1.0 / jnp.sqrt(jnp.array(DIM_HEAD, dtype=x.dtype))
        scores = jnp.einsum('bhid,bhjd->bhij', q, k) * scale
        causal = jnp.tril(jnp.ones((n, n), dtype=bool))
        scores = jnp.where(causal, scores, jnp.finfo(scores.dtype).min)
        attn = jax.nn.softmax(scores, axis=-1)
        out = jnp.einsum('bhij,bhjd->bhid', attn, v)
        out = out * head_scale
        out = out.transpose(0, 2, 1, 3).reshape(b, n, HEADS * DIM_HEAD)
        return out @ Wo

    def _L0_ffn_ref(x, gamma, beta, mu, scale, W1, b1, W2, b2):
        import jax, jax.numpy as jnp
        import numpy as np
        LN_EPS = 1e-05
        L2_EPS = 1e-12

        def _l2norm(v, axis):
            n = jnp.sqrt(jnp.sum(v * v, axis=axis, keepdims=True))
            return v / jnp.maximum(n, L2_EPS)
        B, N, D = x.shape
        _, E, S = mu.shape
        mean = jnp.mean(x, axis=-1, keepdims=True)
        var = jnp.mean(jnp.square(x - mean), axis=-1, keepdims=True)
        x_ln = (x - mean) / jnp.sqrt(var + LN_EPS) * gamma + beta
        x_n = _l2norm(x_ln, -1) * scale
        mu_n = _l2norm(mu, 0)
        logits = jnp.einsum('bnd,des->bnes', x_n, mu_n)
        dispatch = jax.nn.softmax(logits, axis=1)
        combine = jax.nn.softmax(logits.reshape(B, N, E * S), axis=-1)
        slot_in = jnp.einsum('bnd,bnes->besd', x_ln, dispatch)
        h = jax.nn.gelu(jnp.einsum('besd,edh->besh', slot_in, W1) + b1[None, :, None, :], approximate=False)
        slot_out = jnp.einsum('besh,ehd->besd', h, W2) + b2[None, :, None, :]
        out = jnp.einsum('bsd,bns->bnd', slot_out.reshape(B, E * S, D), combine)
        return out
    x = L0_attn_x
    x = _layernorm(x + _L0_attn_ref(x, L0_attn_Wq, L0_attn_Wk, L0_attn_Wv, L0_attn_Wo, L0_attn_head_scale), axis=-1)
    x = _layernorm(x + _L0_ffn_ref(x, L0_ffn_gamma, L0_ffn_beta, L0_ffn_mu, L0_ffn_scale, L0_ffn_W1, L0_ffn_b1, L0_ffn_W2, L0_ffn_b2), axis=-1)
    return x

_drawn_inputs = setup_inputs


def setup_inputs(seed=0):
    import zlib

    import numpy as np

    out = dict(_drawn_inputs(seed))
    spreads = {'L0_ffn_gamma': (1.0, 0.6),
     'L0_ffn_beta': (0.0, 0.711),
     'L0_ffn_b1': (0.0, 0.8),
     'L0_ffn_b2': (0.0, 0.318)}
    factors = {'L0_attn_head_scale': 8.0, 'L0_ffn_mu': 8.0, 'L0_ffn_W1': 3.228, 'L0_ffn_W2': 2.916}
    for name, (base, spread) in spreads.items():
        noise = np.random.default_rng([zlib.crc32(name.encode()), seed]).standard_normal(out[name].shape)
        drawn = base * np.exp(spread * noise) if base else spread * noise
        out[name] = jnp.asarray(drawn.astype(out[name].dtype))
    for name, factor in factors.items():
        out[name] = (out[name] * factor).astype(out[name].dtype)
    return out
```

```python
from contextlib import ExitStack

import concourse.bass as bass
import numpy as np
from concourse import mybir

F32 = mybir.dt.float32
F32R = mybir.dt.float32r
BF16 = mybir.dt.bfloat16
ALU = mybir.AluOpType
ACT = mybir.ActivationFunctionType
AX_X = mybir.AxisListType.X

P = 128
BANK = 512
LN_EPS = 1e-5
L2_EPS = 1e-12
HIDDEN = -(2.0 ** 120)
PARTS = ((0, 0), (0, 1), (1, 0))


def plan_group(heads, tiles):
    plan, steps = [], []
    waiting = {"split": None, "weigh": None}

    def rope(which):
        plan.extend([("project", which), ("rotate", which), ("times_cos", which), ("times_sin", which),
                     ("rope_add", which), ("rope_hi", which), ("rope_lo", which)])

    def flush_split():
        if waiting["split"]:
            plan.append(("split", *waiting["split"]))
            waiting["split"] = None

    def flush_weigh():
        step, waiting["weigh"] = waiting["weigh"], None
        if step:
            h, w, j = step
            plan.append(("weigh", *step))
            if j == 4 * w + 3:
                plan.extend([("mixed_hi", h, w), ("mixed_lo", h, w)])

    def turn(step):
        plan.extend([("turn_hi", *step), ("turn_lo", *step), ("turned_hi", *step), ("turned_lo", *step)])
        flush_weigh()
        waiting["weigh"] = step

    def scores(h, i, window_steps=()):
        plan.append(("scores", h, i))
        flush_weigh()
        plan.append(("max", h, i))
        flush_split()
        for step in window_steps[:1]:
            turn(step)
        plan.append(("exp", h, i))
        for step in window_steps[1:]:
            turn(step)
        waiting["split"] = (h, i)

    def output(pair, w):
        plan.extend([("output", pair, w), ("add_output", pair, w)])

    plan.append(("split_weights", "k"))
    plan.append(("split_weights", "v"))
    plan.append(("split_weights", 0))
    rope("k")
    plan.extend([("project", "v"), ("values_hi", "v"), ("values_lo", "v")])
    for half in range(tiles // 4):
        plan.extend([(kind, "v", 0, half) for kind in ("turn_hi", "turn_lo", "turned_hi", "turned_lo")])
    rope(0)
    for h in range(heads):
        if h % 2 == 0:
            plan.append(("split_out_weights", h // 2))
        for i in range(4):
            scores(h, i)
        flush_split()
        if h + 1 < heads:
            plan.append(("split_weights", h + 1))
            plan.extend([("project", h + 1), ("rotate", h + 1), ("times_cos", h + 1), ("times_sin", h + 1),
                         ("rope_add", h + 1)])
        if h % 2 == 1 and h > 1:
            output(h // 2 - 1, 1)
        for j in range(4):
            turn((h, 0, j))
        for i in range(4, 8):
            scores(h, i, [(h - 1, 1, 2 * (i - 4)), (h - 1, 1, 2 * (i - 4) + 1)] if h else ())
            if i == 4 and h % 2 == 1:
                output(h // 2, 0)
            if i == 5 and h + 1 < heads:
                plan.extend([("rope_hi", h + 1), ("rope_lo", h + 1)])
    flush_weigh()
    flush_split()
    for j in range(8):
        turn((heads - 1, 1, j))
    flush_weigh()
    output(heads // 2 - 1, 1)
    return plan


def attention(nc, y_sb, x_d, wq_d, wk_d, wv_d, wo_d, head_scale_d, cos_d, sin_d, ident_d, hidden_d):
    B, N, D = x_d.shape
    DH = P
    HEADS = wq_d.shape[1] // DH
    GROUPS = wk_d.shape[1] // DH
    HPG = HEADS // GROUPS
    TILES = N // P
    KT = D // P
    SCALE = DH ** -0.5
    plan = plan_group(HPG, TILES)

    kinds = {}
    at = {}
    for item in plan:
        at[item] = kinds.get(item[0], 0)
        kinds[item[0]] = at[item] + 1
    entries = [item for item in plan if item[0] in ("project", "scores", "output")]
    assert len(entries) % 2 == 0
    last_reader = {"scores": "exp", "output": "add_output"}
    turns = [item[1:] for item in plan if item[0] == "turn_hi"]
    score_tiles = [item[1:] for item in plan if item[0] == "scores"]

    with ExitStack() as ctx:
        def sb(name, shape, dt=F32):
            return ctx.enter_context(nc.sbuf_tensor(name, shape, dt))

        def psum(name, shape, dt=F32):
            return ctx.enter_context(nc.psum_tensor(name, shape, dt))

        def sem(name):
            return ctx.enter_context(nc.semaphore(name))

        xT = sb("xT", [P, 2, KT, N], F32R)
        qT = sb("qT", [P, 2, 2, N], F32R)
        kT = sb("kT", [P, 2, N], F32R)
        vT = sb("vT", [P, 2, N], F32R)
        v_sb = sb("v_sb", [P, 2, N], F32R)
        probs = sb("probs", [P, 2, N])
        near = sb("near", [P, 2, P * 10], F32R)
        far = sb("far", [P, 2, 2, P * 26], F32R)
        probsT = sb("probsT", [P, 2, 2, BANK], F32R)
        mixed = sb("mixed", [P, 2, 2, N], F32R)
        cos_sb = sb("cos_sb", [P, N])
        sin_sb = sb("sin_sb", [P, N])
        rotated = sb("rotated", [P, N])
        cos_part = sb("cos_part", [P, N])
        raw = {"k": sb("raw_k", [P, KT, DH]), "v": sb("raw_v", [P, KT, DH]), "o": sb("raw_o", [P, 2, D])}
        raw_q = [sb(f"raw_q{i}", [P, KT, DH]) for i in range(2)]
        wk_sb = sb("wk_sb", [P, 2, KT, DH], F32R)
        wv_sb = sb("wv_sb", [P, 2, KT, DH], F32R)
        wq_sb = sb("wq_sb", [P, 2, 2, KT, DH], F32R)
        wo_sb = sb("wo_sb", [P, 2, 2, 2, D], F32R)
        ident = sb("ident", [P, P])
        ident_r = sb("ident_r", [P, P], F32R)
        ident_b = sb("ident_b", [P, P], BF16)
        hidden = sb("hidden", [P, P])
        hidden_b = sb("hidden_b", [P, P], BF16)
        head_scale = sb("head_scale", [P, HEADS])
        unit = sb("unit", [P, 2])
        neg_max = sb("neg_max", [P, 2])
        row_sum = sb("row_sum", [P, 2])
        inv_sum = sb("inv_sum", [P, 2])
        ring = psum("ring", [P, 2, 2 * BANK])
        turned = psum("turned", [P, 2, BANK], F32R)
        mix = psum("mix", [P, 2, BANK])

        done = {kind: sem(f"{kind}_done") for kind in kinds}
        consts_loaded, consts_ready, unit_ready = sem("consts_loaded"), sem("consts_ready"), sem("unit_ready")
        x_loaded, x_turned, xT_hi_done, xT_lo_done = sem("x_loaded"), sem("x_turned"), sem("xT_hi_done"), sem("xT_lo_done")
        y_loaded = sem("y_loaded")
        raw_loaded = {k: sem(f"raw_{k}_loaded") for k in ("k", "v", "o", "q0", "q1")}
        dve_step, pool_step = sem("dve_step"), sem("pool_step")

        def count(group, kind, *which):
            return past(group, kind) + at[(kind, *which)] + 1

        def past(group, kind):
            return group * kinds[kind] + 1

        def start_counts(engine, *own):
            for kind in own:
                engine.sem_inc(done[kind], 1)

        def far_at(i):
            return P * sum(range(5, i + 1))

        def near_at(i):
            return P * (i * (i + 1) // 2)

        def tile_probs(h, i, part, a, b):
            if i < 4:
                return near[:, part, near_at(i) + a:near_at(i) + b]
            return far[:, h % 2, part, far_at(i) + a:far_at(i) + b]

        x_rows = x_d.rearrange("b (t p) d -> b p t d", p=P)
        wq_cols = wq_d.rearrange("(t c) n -> c t n", c=P)
        wk_cols = wk_d.rearrange("(t c) n -> c t n", c=P)
        wv_cols = wv_d.rearrange("(t c) n -> c t n", c=P)
        wo_rows = wo_d.rearrange("(h d) n -> d h n", d=DH)
        x_stage = probs[:, :, :].rearrange("p a (t d) -> p (a t) d", d=D)
        block = ctx.enter_context(nc.Block())

        @block.sync
        def _(sp):
            sp.dma_start(ident[:, :], ident_d).then_inc(consts_loaded, 16)
            sp.dma_start(hidden[:, :], hidden_d).then_inc(consts_loaded, 16)
            sp.dma_start(cos_sb[:, :], cos_d).then_inc(consts_loaded, 16)
            sp.dma_start(sin_sb[:, :], sin_d).then_inc(consts_loaded, 16)
            sp.dma_start(head_scale[:, :], head_scale_d.rearrange("a h b c -> (a b c) h").broadcast_to([P, HEADS])).then_inc(consts_loaded, 16)
            for b in range(B):
                sp.dma_start(y_sb[:, b * TILES:(b + 1) * TILES, :], x_rows[b]).then_inc(y_loaded, 16)
            with sp.Fori(0, B) as b:
                sp.wait_ge(done["split"], past(b * GROUPS, "split"))
                sp.dma_start(x_stage, x_rows[bass.ds(b, 1)].rearrange("a p t d -> p (a t) d")).then_inc(x_loaded, 16)
                with sp.Fori(0, GROUPS) as g:
                    group = b * GROUPS + g
                    for item in plan:
                        if item[0] == "split_weights":
                            h = item[1]
                            if h in ("k", "v"):
                                sp.wait_ge(done["split_weights"], past(group, "split_weights"))
                                sp.dma_start(raw[h][:, :, :], (wk_cols if h == "k" else wv_cols)[:, :, bass.ds(g * DH, DH)]
                                             ).then_inc(raw_loaded[h], 16)
                            else:
                                sp.wait_ge(done["split_weights"],
                                           count(group, "split_weights", h - 2) if h >= 2 else past(group, "split_weights"))
                                sp.dma_start(raw_q[h % 2][:, :, :], wq_cols[:, :, bass.ds((g * HPG + h) * DH, DH)]
                                             ).then_inc(raw_loaded[f"q{h % 2}"], 16)
                        if item[0] == "split_out_weights":
                            pair = item[1]
                            sp.wait_ge(done["split_out_weights"], past(group, "split_out_weights") + pair)
                            sp.dma_start(raw["o"][:, :, :], wo_rows[:, bass.ds(g * HPG + 2 * pair, 2), :]
                                         ).then_inc(raw_loaded["o"], 16)

        @block.tensor
        def _(pe):
            def free_ring(group, e):
                kind, *which = entries[e - 2]
                reader = last_reader.get(kind) or ("values_lo" if which == ["v"] else "times_cos")
                pe.wait_ge(done[reader], count(group, reader, *which) if e >= 2 else past(group, reader))

            start_counts(pe, "project", "scores", "turn_hi", "turn_lo", "weigh", "output")
            pe.wait_ge(consts_ready, 3)
            with pe.Fori(0, B) as b:
                pe.wait_ge(x_loaded, b * 16 + 16)
                pe.wait_ge(done["exp"], past(b * GROUPS, "exp"))
                pe.wait_ge(done["add_output"], past(b * GROUPS, "add_output"))
                for c in range(KT):
                    for t in range(TILES):
                        last = nc.tensor.transpose(ring[:, c, t * P:(t + 1) * P], x_stage[:, t, c * P:(c + 1) * P], ident[:, :])
                    last.then_inc(x_turned, 1)
                with pe.Fori(0, GROUPS) as g:
                    group = b * GROUPS + g
                    e = 0
                    pe.wait_ge(xT_lo_done, b * KT + KT)
                    for kind, *which in plan:
                        if kind == "project":
                            (who,) = which
                            w = wk_sb[:, :, :, :] if who == "k" else wv_sb[:, :, :, :] if who == "v" else wq_sb[:, who % 2, :, :, :]
                            pe.wait_ge(done["split_weights"], count(group, "split_weights", who))
                            free_ring(group, e)
                            passes = [(c, a, m) for c in range(KT) for a, m in PARTS]
                            for half in range(N // BANK):
                                for n, (c, a, m) in enumerate(passes):
                                    last = nc.tensor.matmul(ring[:, e % 2, half * BANK:(half + 1) * BANK], w[:, a, c, :],
                                                            xT[:, m, c, half * BANK:(half + 1) * BANK],
                                                            start=n == 0, stop=n == len(passes) - 1)
                            last.then_inc(done[kind], 1)
                            e += 1
                        if kind == "scores":
                            h, i = which
                            if i == 0:
                                pe.wait_ge(done["rope_lo"], count(group, "rope_lo", h))
                            free_ring(group, e)
                            width = (i + 1) * P
                            q = qT[:, h % 2, :, i * P:(i + 1) * P]
                            for lo in range(0, width, BANK):
                                hi = min(width, lo + BANK)
                                diagonal = hi == width
                                for n, (a, m) in enumerate(PARTS):
                                    last = nc.tensor.matmul(ring[:, e % 2, lo:hi], q[:, a, :], kT[:, m, lo:hi],
                                                            start=n == 0, stop=n == 2 and not diagonal)
                                if diagonal:
                                    last = nc.tensor.matmul(ring[:, e % 2, width - P:width], ident_b[:, :], hidden_b[:, :],
                                                            start=False, stop=True)
                            last.then_inc(done[kind], 1)
                            e += 1
                        if kind in ("turn_hi", "turn_lo"):
                            part = int(kind == "turn_lo")
                            h, w, j = which
                            n = at[(kind, *which)]
                            before = "turned_lo" if part else "turned_hi"
                            pe.wait_ge(done[before], past(group, before) + n)
                            if h == "v":
                                if j == 0:
                                    pe.wait_ge(done["values_lo"], count(group, "values_lo", "v"))
                                for t in range(4):
                                    last = nc.tensor.transpose(turned[:, part, t * P:(t + 1) * P],
                                                               vT[:, part, (4 * j + t) * P:(4 * j + t + 1) * P], ident_r[:, :])
                            else:
                                if j == 0:
                                    pe.wait_ge(done["split"], count(group, "split", h, 4 * w + 3))
                                for i in range(max(4 * w, j), 4 * w + 4):
                                    last = nc.tensor.transpose(turned[:, part, (i - 4 * w) * P:(i - 4 * w + 1) * P],
                                                               tile_probs(h, i, part, j * P, (j + 1) * P), ident_r[:, :])
                            last.then_inc(done[kind], 1)
                        if kind == "weigh":
                            h, w, j = which
                            slot = at[("turn_hi", h, w, j)] % 2
                            first = max(4 * w, j) * P - 4 * w * P
                            pe.wait_ge(done["turned_lo"], count(group, "turned_lo", h, w, j))
                            pe.wait_ge(done["turned_hi"], count(group, "turned_hi", h, w, j))
                            if j == 0:
                                pe.wait_ge(done["mixed_lo"], count(group, "mixed_lo", h - 1, w) if h else past(group, "mixed_lo"))
                            for n, (a, m) in enumerate(PARTS):
                                last = nc.tensor.matmul(mix[:, w, first:BANK], v_sb[:, a, j * P:(j + 1) * P],
                                                        probsT[:, slot, m, first:BANK],
                                                        start=j == 0 and n == 0, stop=j == 4 * w + 3 and n == 2)
                            last.then_inc(done[kind], 1)
                        if kind == "output":
                            pair, w = which
                            pe.wait_ge(done["mixed_lo"], count(group, "mixed_lo", 2 * pair + 1, w))
                            pe.wait_ge(done["split_out_weights"], count(group, "split_out_weights", pair))
                            free_ring(group, e)
                            passes = [(hh, a, m) for hh in range(2) for a, m in PARTS]
                            for t in range(4):
                                for n, (hh, a, m) in enumerate(passes):
                                    last = nc.tensor.matmul(ring[:, e % 2, t * D:(t + 1) * D],
                                                            mixed[:, hh, a, (4 * w + t) * P:(4 * w + t + 1) * P],
                                                            wo_sb[:, pair % 2, m, hh, :],
                                                            start=n == 0, stop=n == len(passes) - 1)
                            last.then_inc(done[kind], 1)
                            e += 1

        @block.scalar
        def _(act):
            start_counts(act, "rotate", "rope_hi", "values_hi", "exp", "turned_hi", "turned_lo", "mixed_hi")
            with act.Fori(0, B) as b:
                for c in range(KT):
                    act.wait_ge(x_turned, b * KT + (c + 1))
                    nc.scalar.activation(xT[:, 0, c, :], ring[:, c, :], ACT.Copy).then_inc(xT_hi_done, 1)
                with act.Fori(0, GROUPS) as g:
                    group = b * GROUPS + g
                    for kind, *which in plan:
                        if kind == "rotate":
                            (who,) = which
                            e = entries.index(("project", who))
                            n = at[(kind, who)]
                            act.wait_ge(done["project"], count(group, "project", who))
                            act.wait_ge(done["rope_add"], past(group, "rope_add") + n)
                            nc.scalar.activation(rotated[0:64, :], ring[64:128, e % 2, :], ACT.Copy)
                            nc.scalar.activation(rotated[64:128, :], ring[0:64, e % 2, :], ACT.Copy).then_inc(done[kind], 1)
                        if kind == "rope_hi":
                            (who,) = which
                            act.wait_ge(done["rope_add"], count(group, "rope_add", who))
                            if who == "k" or who < 2:
                                act.wait_ge(done["scores"], past(group, "scores"))
                            else:
                                act.wait_ge(done["scores"], count(group, "scores", who - 2, TILES - 1))
                            dst = kT[:, 0, :] if who == "k" else qT[:, who % 2, 0, :]
                            nc.scalar.activation(dst, cos_part[:, :], ACT.Copy).then_inc(done[kind], 1)
                        if kind == "values_hi":
                            e = entries.index(("project", "v"))
                            act.wait_ge(done["project"], count(group, "project", "v"))
                            nc.scalar.activation(vT[:, 0, :], ring[:, e % 2, :], ACT.Copy).then_inc(done[kind], 1)
                        if kind == "exp":
                            h, i = which
                            n = at[(kind, h, i)]
                            e = entries.index(("scores", h, i))
                            act.wait_ge(done["max"], count(group, "max", h, i))
                            act.wait_ge(done["split"], count(group, "split", *score_tiles[n - 2]) if n >= 2 else past(group, "split"))
                            nc.scalar.activation(probs[:, n % 2, 0:(i + 1) * P], ring[:, e % 2, 0:(i + 1) * P], ACT.Exp,
                                                 bias=neg_max[:, n % 2:n % 2 + 1],
                                                 accum_out=row_sum[:, n % 2:n % 2 + 1]).then_inc(done[kind], 1)
                        if kind in ("turned_hi", "turned_lo"):
                            part = int(kind == "turned_lo")
                            h, w, j = which
                            n = at[(kind, *which)]
                            source = "turn_lo" if part else "turn_hi"
                            act.wait_ge(done[source], count(group, source, *which))
                            if h == "v":
                                act.wait_ge(done["weigh"], past(group, "weigh"))
                                nc.scalar.activation(v_sb[:, part, j * BANK:(j + 1) * BANK], turned[:, part, :].bitcast(F32),
                                                     ACT.Copy).then_inc(done[kind], 1)
                            else:
                                before = turns[n - 2]
                                act.wait_ge(done["weigh"], count(group, "weigh", *before) if before[0] != "v" else past(group, "weigh"))
                                first = max(4 * w, j) * P - 4 * w * P
                                nc.scalar.activation(probsT[:, n % 2, part, first:BANK], turned[:, part, first:BANK].bitcast(F32),
                                                     ACT.Copy).then_inc(done[kind], 1)
                        if kind == "mixed_hi":
                            h, w = which
                            act.wait_ge(done["weigh"], count(group, "weigh", h, w, 4 * w + 3))
                            act.wait_ge(done["output"], count(group, "output", h // 2 - 1, w) if h >= 2 else past(group, "output"))
                            nc.scalar.activation(mixed[:, h % 2, 0, w * BANK:(w + 1) * BANK], mix[:, w, :], ACT.Copy
                                                 ).then_inc(done[kind], 1)

        @block.vector
        def _(dve):
            start_counts(dve, "times_cos", "times_sin", "values_lo", "max", "split", "mixed_lo", "add_output")
            dve.wait_ge(consts_loaded, 5 * 16)
            nc.vector.tensor_copy(ident_r[:, :], ident[:, :]).then_inc(consts_ready, 1)
            nc.vector.tensor_copy(ident_b[:, :], ident[:, :]).then_inc(consts_ready, 1)
            nc.vector.tensor_copy(hidden_b[:, :], hidden[:, :]).then_inc(consts_ready, 1)
            dve.wait_ge(y_loaded, B * 16)
            with dve.Fori(0, B) as b:
                for c in range(KT):
                    dve.wait_ge(xT_hi_done, b * KT + (c + 1))
                    nc.vector.tensor_tensor(xT[:, 1, c, :], ring[:, c, :], xT[:, 0, c, :].bitcast(F32), ALU.subtract
                                            ).then_inc(xT_lo_done, 1)
                with dve.Fori(0, GROUPS) as g:
                    group = b * GROUPS + g
                    for kind, *which in plan:
                        if kind == "times_cos":
                            (who,) = which
                            n = at[(kind, who)]
                            e = entries.index(("project", who))
                            dve.wait_ge(done["rotate"], count(group, "rotate", who))
                            dve.wait_ge(done["rope_lo"], past(group, "rope_lo") + n)
                            nc.vector.tensor_tensor(cos_part[:, :], ring[:, e % 2, :], cos_sb[:, :], ALU.mult).then_inc(done[kind], 1)
                        if kind == "times_sin":
                            (who,) = which
                            n = at[(kind, who)]
                            nc.vector.tensor_tensor(rotated[:, :], rotated[:, :], sin_sb[:, :], ALU.mult).then_inc(done[kind], 1)
                        if kind == "values_lo":
                            e = entries.index(("project", "v"))
                            dve.wait_ge(done["values_hi"], count(group, "values_hi", "v"))
                            nc.vector.tensor_tensor(vT[:, 1, :], ring[:, e % 2, :], vT[:, 0, :].bitcast(F32), ALU.subtract
                                                    ).then_inc(done[kind], 1)
                        if kind == "max":
                            h, i = which
                            n = at[(kind, h, i)]
                            e = entries.index(("scores", h, i))
                            dve.wait_ge(done["scores"], count(group, "scores", h, i))
                            dve.wait_ge(done["exp"], count(group, "exp", *score_tiles[n - 2]) if n >= 2 else past(group, "exp"))
                            nc.vector.tensor_reduce(neg_max[:, n % 2:n % 2 + 1], ring[:, e % 2, 0:(i + 1) * P], AX_X, ALU.max,
                                                    negate=True).then_inc(done[kind], 1)
                        if kind == "split":
                            h, i = which
                            n = at[(kind, h, i)]
                            width = (i + 1) * P
                            own = group * (2 * kinds["split"]) + 2 * n
                            dve.wait_ge(done["exp"], count(group, "exp", h, i))
                            nc.vector.reciprocal(inv_sum[:, n % 2:n % 2 + 1], row_sum[:, n % 2:n % 2 + 1]).then_inc(dve_step, 1)
                            if i < 4:
                                dve.wait_ge(done["turn_lo"], count(group, "turn_lo", h - 1, 0, 3) if h else past(group, "turn_lo"))
                            else:
                                dve.wait_ge(done["turn_lo"], count(group, "turn_lo", h - 2, 1, 7) if h >= 2 else past(group, "turn_lo"))
                            dve.wait_ge(dve_step, own + 1)
                            nc.vector.tensor_scalar(tile_probs(h, i, 0, 0, width), probs[:, n % 2, 0:width], inv_sum[:, n % 2:n % 2 + 1],
                                                    None, ALU.mult).then_inc(dve_step, 1)
                            dve.wait_ge(dve_step, own + 2)
                            nc.vector.scalar_tensor_tensor(tile_probs(h, i, 1, 0, width), probs[:, n % 2, 0:width],
                                                           inv_sum[:, n % 2:n % 2 + 1], tile_probs(h, i, 0, 0, width).bitcast(F32),
                                                           ALU.mult, ALU.subtract).then_inc(done[kind], 1)
                        if kind == "mixed_lo":
                            h, w = which
                            dve.wait_ge(done["mixed_hi"], count(group, "mixed_hi", h, w))
                            nc.vector.tensor_tensor(mixed[:, h % 2, 1, w * BANK:(w + 1) * BANK], mix[:, w, :],
                                                    mixed[:, h % 2, 0, w * BANK:(w + 1) * BANK].bitcast(F32), ALU.subtract
                                                    ).then_inc(done[kind], 1)
                        if kind == "add_output":
                            pair, w = which
                            e = entries.index(("output", pair, w))
                            dve.wait_ge(done["output"], count(group, "output", pair, w))
                            dve.wait_ge(done["add_output"], past(group, "add_output") + at[(kind, pair, w)])
                            rows = y_sb[:, bass.ds(b * TILES + 4 * w, 4), :].rearrange("p t d -> p (t d)")
                            nc.vector.tensor_tensor(rows, ring[:, e % 2, :], rows, ALU.add).then_inc(done[kind], 1)

        @block.gpsimd
        def _(pool):
            start_counts(pool, "split_weights", "split_out_weights", "rope_add", "rope_lo")
            nc.gpsimd.memset(unit[:, 0:1], 1.0).then_inc(unit_ready, 1)
            nc.gpsimd.memset(unit[:, 1:2], SCALE).then_inc(unit_ready, 1)
            pool.wait_ge(unit_ready, 2)
            pool.wait_ge(consts_loaded, 5 * 16)
            total = 2 + 2 * HPG + 2 * kinds["split_out_weights"]

            def column(one, like):
                return one.rearrange("p (a b) -> p a b", b=1).broadcast_to(list(like.shape))

            with pool.Fori(0, B) as b:
                with pool.Fori(0, GROUPS) as g:
                    group = b * GROUPS + g
                    own = 0
                    for kind, *which in plan:
                        if kind == "split_weights":
                            (who,) = which
                            if who in ("k", "v"):
                                pool.wait_ge(raw_loaded[who], group * 16 + 16)
                                source, dst = raw[who], wk_sb[:, :, :, :] if who == "k" else wv_sb[:, :, :, :]
                                pool.wait_ge(done["project"], past(group, "project"))
                            else:
                                pool.wait_ge(raw_loaded[f"q{who % 2}"], group * (16 * HPG // 2) + 16 * (who // 2 + 1))
                                source, dst = raw_q[who % 2], wq_sb[:, who % 2, :, :, :]
                                pool.wait_ge(done["project"], count(group, "project", who - 2) if who >= 2 else past(group, "project"))
                                nc.gpsimd.tensor_tensor(source[:, :, :], source[:, :, :], column(unit[:, 1:2], source), ALU.mult
                                                        ).then_inc(pool_step, 1)
                                own += 1
                                pool.wait_ge(pool_step, group * total + own)
                            nc.gpsimd.tensor_tensor(dst[:, 0], source[:, :, :], column(unit[:, 0:1], source), ALU.mult).then_inc(pool_step, 1)
                            own += 1
                            pool.wait_ge(pool_step, group * total + own)
                            nc.gpsimd.tensor_tensor(dst[:, 1], source[:, :, :], dst[:, 0].bitcast(F32), ALU.subtract
                                                    ).then_inc(done[kind], 1)
                        if kind == "split_out_weights":
                            (pair,) = which
                            pool.wait_ge(raw_loaded["o"], group * (16 * kinds[kind]) + 16 * (pair + 1))
                            pool.wait_ge(done["output"], past(group, "output"))
                            scales = head_scale[:, bass.ds(g * HPG + 2 * pair, 2)].rearrange("p (h a) -> p h a", a=1)
                            nc.gpsimd.tensor_tensor(raw["o"][:, :, :], raw["o"][:, :, :], scales.broadcast_to([P, 2, D]), ALU.mult
                                                    ).then_inc(pool_step, 1)
                            own += 1
                            pool.wait_ge(pool_step, group * total + own)
                            nc.gpsimd.tensor_tensor(wo_sb[:, pair % 2, 0], raw["o"][:, :, :], column(unit[:, 0:1], raw["o"]), ALU.mult
                                                    ).then_inc(pool_step, 1)
                            own += 1
                            pool.wait_ge(pool_step, group * total + own)
                            nc.gpsimd.tensor_tensor(wo_sb[:, pair % 2, 1], raw["o"][:, :, :], wo_sb[:, pair % 2, 0].bitcast(F32),
                                                    ALU.subtract).then_inc(done[kind], 1)
                        if kind == "rope_add":
                            (who,) = which
                            pool.wait_ge(done["times_cos"], count(group, "times_cos", who))
                            pool.wait_ge(done["times_sin"], count(group, "times_sin", who))
                            nc.gpsimd.tensor_tensor(cos_part[:, :], cos_part[:, :], rotated[:, :], ALU.add).then_inc(done[kind], 1)
                        if kind == "rope_lo":
                            (who,) = which
                            dst = kT[:, :, :] if who == "k" else qT[:, who % 2, :, :]
                            pool.wait_ge(done["rope_hi"], count(group, "rope_hi", who))
                            nc.gpsimd.tensor_tensor(dst[:, 1, :], cos_part[:, :], dst[:, 0, :].bitcast(F32), ALU.subtract
                                                    ).then_inc(done[kind], 1)
                    assert own == total, (own, total)


def plan_experts(experts, tiles):
    plan = [(kind,) for kind in ("stats_1", "std_1", "norm_1", "stats_2", "std_2", "affine", "lengths", "unit_rows",
                                 "rows_hi", "rows_lo")]
    for part in range(2):
        for c in range(2):
            plan.extend([("turn_rows", part, c), ("rows_turned", part, c)])

    def fill(e):
        plan.extend([("slot_logits", e), ("slot_max", e), ("slot_exp", e), ("slot_split", e)])

    def turn(kind, copied, *which):
        plan.extend([(kind, *which, 0), (kind, *which, 1), (copied, *which, 0), (copied, *which, 1)])

    fill(0)
    for e in range(experts):
        if e + 1 < experts:
            fill(e + 1)
        for half in range(tiles // 4):
            turn("turn_dispatch", "dispatch_turned", e, half)
        if e % 4 == 3:
            plan.extend([("gather", e // 4), ("gathered", e // 4)])
    for w in range(experts // 4):
        plan.extend([("hidden_layer", w), ("gelu", w)])
    for w in range(experts // 4):
        plan.extend([("output_layer", w), ("slots_hi", w), ("slots_lo", w)])

    def fill_row(t):
        plan.extend([("row_logits", t), ("row_max", t), ("row_exp", t)])

    fill_row(0)
    plan.append(("row_split", 0))
    for t in range(tiles):
        if t + 1 < tiles:
            fill_row(t + 1)
        for quad in range(experts // 4):
            turn("turn_combine", "combine_turned", t, quad)
        if t + 1 < tiles:
            plan.append(("row_split", t + 1))
        plan.extend([("spread", t), ("add_rows", t)])
    plan.extend([("stats_3",), ("std_3",), ("norm_3",)])
    return plan


def soft_experts(nc, y_sb, gamma_d, beta_d, mu_d, scale_d, w1_d, b1_d, w2_d, b2_d, ident_d, out_d):
    B, N, D = out_d.shape
    _, E, S = mu_d.shape
    H = w1_d.shape[2]
    TILES = N // P
    KT = D // P
    ES = E * S
    assert S == P and KT == 2
    plan = plan_experts(E, TILES)
    kinds, at = {}, {}
    for item in plan:
        at[item] = kinds.get(item[0], 0)
        kinds[item[0]] = at[item] + 1

    with ExitStack() as ctx:
        def sb(name, shape, dt=F32):
            return ctx.enter_context(nc.sbuf_tensor(name, shape, dt))

        def psum(name, shape, dt=F32):
            return ctx.enter_context(nc.psum_tensor(name, shape, dt))

        def sem(name):
            return ctx.enter_context(nc.semaphore(name))

        rows = sb("rows", [P, 2, TILES, D], F32R)
        rowsT = sb("rowsT", [P, 2, KT, N], F32R)
        mu = sb("mu", [P, 2, KT, ES], F32R)
        slots = sb("slots", [P, 2, E, D], F32R)
        exps = sb("exps", [P, 2, ES])
        parts = sb("parts", [P, 2, ES], F32R)
        turned_sb = sb("turned_sb", [P, 2, 2, ES], F32R)
        gathered = sb("gathered", [P, KT, ES])
        hidden = sb("hidden_h", [P, ES])
        w2_sb = exps[0:H + 1, 0, :].rearrange("p (a e d) -> p a e d", a=2, e=4)
        w1_sb = exps[:, 1, :].rearrange("p (c e h) -> p c e h", c=KT, e=E)
        b1_sb = sb("b1_sb", [H, E])
        gamma = sb("gamma", [P, D])
        beta = sb("beta", [P, D])
        scale = sb("scale", [P, 1])
        ident = sb("ident2", [P, P])
        ident_r = sb("ident2_r", [P, P], F32R)
        ones = sb("ones", [P, P])
        moments = sb("moments", [P, TILES, 6])
        mean_var = sb("mean_var", [P, TILES, 2])
        spread_sq = sb("spread_sq", [P, TILES])
        std = sb("std", [P, TILES])
        inv_std = sb("inv_std", [P, TILES])
        neg_max = sb("neg_max2", [P, 2])
        total = sb("total", [P, 2])
        inv_total = sb("inv_total", [P, 2])
        ring = psum("ring2", [P, 4 * BANK])
        turned = psum("turned2", [P, 2, BANK], F32R)
        mix = psum("mix2", [P, 2, BANK])

        done = {kind: sem(f"{kind}_done") for kind in kinds}
        consts_loaded, mu_loaded, w1_loaded = sem("consts2_loaded"), sem("mu_loaded"), sem("w1_loaded")
        w2_loaded = [sem("w2_even_loaded"), sem("w2_odd_loaded")]
        ones_ready, ident_ready, squares_ready, sums_ready, norms_ready, mu_ready = (
            sem("ones_ready"), sem("ident_ready"), sem("squares_ready"), sem("sums_ready"), sem("norms_ready"), sem("mu_ready"))
        ones_row_ready = sem("ones_row_ready")
        dve_step, act_step, stored = sem("dve_step2"), sem("act_step2"), sem("stored")

        def count(b, kind, *which):
            return b * kinds[kind] + at[(kind, *which)] + 1

        block = ctx.enter_context(nc.Block())

        def y_rows(b, t=0, n=TILES):
            return y_sb[:, bass.ds(b * TILES + t, n), :].rearrange("p t d -> p (t d)")

        @block.sync
        def _(sp):
            sp.dma_start(exps[:, :, :], mu_d.rearrange("(c p) e s -> p c (e s)", p=P)).then_inc(mu_loaded, 16)
            sp.dma_start(ident[:, :], ident_d).then_inc(consts_loaded, 16)
            sp.dma_start(gamma[:, :], gamma_d.rearrange("(a d) -> a d", a=1).broadcast_to([P, D])).then_inc(consts_loaded, 16)
            sp.dma_start(beta[:, :], beta_d.rearrange("(a d) -> a d", a=1).broadcast_to([P, D])).then_inc(consts_loaded, 16)
            sp.dma_start(scale[:, :], scale_d.rearrange("(a d) -> a d", a=1).broadcast_to([P, 1])).then_inc(consts_loaded, 16)
            sp.dma_start(b1_sb[:, :], b1_d.rearrange("e h -> h e"), allow_slow_non_contiguous=True).then_inc(consts_loaded, 16)
            for b in range(B):
                sp.wait_ge(done["slot_split"], (b + 1) * kinds["slot_split"])
                for c in range(KT):
                    sp.dma_start(w1_sb[:, c], w1_d[:, c * P:(c + 1) * P, :].rearrange("e p h -> p e h")).then_inc(w1_loaded, 16)
                for w in range(E // 4):
                    if w >= 2:
                        sp.wait_ge(done["output_layer"], count(b, "output_layer", w - 2))
                    else:
                        sp.wait_ge(done["output_layer"], b * kinds["output_layer"])
                    sp.dma_start(w2_sb[0:H, w % 2], w2_d[4 * w:4 * w + 4].rearrange("e h d -> h e d")).then_inc(w2_loaded[w % 2], 16)
                    sp.dma_start(w2_sb[H:H + 1, w % 2], b2_d[4 * w:4 * w + 4].rearrange("(a e) d -> a e d", a=1)
                                 ).then_inc(w2_loaded[w % 2], 16)
                sp.wait_ge(done["norm_3"], b + 1)
                sp.dma_start(out_d[bass.ds(b, 1)].rearrange("a (t p) d -> p (a t) d", p=P),
                             y_sb[:, bass.ds(b * TILES, TILES), :]).then_inc(stored, 16)
            sp.wait_ge(stored, 16 * B)

        @block.tensor
        def _(pe):
            pe.wait_ge(ones_ready, 1)
            pe.wait_ge(squares_ready, 1)
            for q in range(ES // BANK):
                for c in range(KT):
                    last = nc.tensor.matmul(ring[:, q * BANK:(q + 1) * BANK], ones[:, :], gathered[:, c, q * BANK:(q + 1) * BANK],
                                            start=c == 0, stop=c == KT - 1)
            last.then_inc(sums_ready, 1)
            pe.wait_ge(ident_ready, 1)
            pe.wait_ge(mu_ready, 1)
            passes = [(c, a, m) for c in range(KT) for a, m in PARTS]
            for b in range(B):
                for kind, *which in plan:
                    if kind == "turn_rows":
                        part, c = which
                        n = at[(kind, part, c)]
                        if n == 0:
                            pe.wait_ge(done["unit_rows"], b + 1)
                            pe.wait_ge(done["row_exp"], b * kinds["row_exp"])
                        if n >= 2:
                            pe.wait_ge(done["rows_turned"], b * kinds["rows_turned"] + n - 1)
                        unit = parts[:, part, :].rearrange("p (t d) -> p t d", d=D)
                        for t in range(TILES):
                            last = nc.tensor.transpose(ring[:, (n % 2) * N + t * P:(n % 2) * N + (t + 1) * P].bitcast(F32R),
                                                       unit[:, t, c * P:(c + 1) * P], ident_r[:, :])
                        last.then_inc(done[kind], 1)
                    if kind == "slot_logits":
                        (e,) = which
                        if e == 0:
                            pe.wait_ge(done["rows_turned"], (b + 1) * kinds["rows_turned"])
                        if e >= 2:
                            pe.wait_ge(done["slot_exp"], count(b, "slot_exp", e - 2))
                        for half in range(N // BANK):
                            at_col = (e % 2) * N + half * BANK
                            for n, (c, a, m) in enumerate(passes):
                                last = nc.tensor.matmul(ring[:, at_col:at_col + BANK], mu[:, a, c, e * P:(e + 1) * P],
                                                        rowsT[:, m, c, half * BANK:(half + 1) * BANK],
                                                        start=n == 0, stop=n == len(passes) - 1)
                        last.then_inc(done[kind], 1)
                    if kind == "turn_dispatch":
                        e, half, part = which
                        n = at[(kind, *which)]
                        if half == 0 and part == 0:
                            pe.wait_ge(done["slot_split"], count(b, "slot_split", e))
                        if n >= 2:
                            pe.wait_ge(done["dispatch_turned"], b * kinds["dispatch_turned"] + n - 1)
                        else:
                            pe.wait_ge(done["combine_turned"], b * kinds["combine_turned"])
                        for t in range(4):
                            col = (e % 2) * N + (4 * half + t) * P
                            last = nc.tensor.transpose(turned[:, part, t * P:(t + 1) * P], parts[:, part, col:col + P], ident_r[:, :])
                        last.then_inc(done[kind], 1)
                    if kind == "gather":
                        (w,) = which
                        pe.wait_ge(done["dispatch_turned"], count(b, "dispatch_turned", 4 * w + 3, TILES // 4 - 1, 1))
                        pe.wait_ge(done["rows_lo"], b + 1)
                        pe.wait_ge(done["rows_hi"], b + 1)
                        if w:
                            pe.wait_ge(done["gathered"], count(b, "gathered", w - 1))
                        else:
                            pe.wait_ge(done["add_rows"], b * kinds["add_rows"])
                        for c in range(KT):
                            for t in range(TILES):
                                for n, (a, m) in enumerate(PARTS):
                                    last = nc.tensor.matmul(mix[:, c, :], rows[:, a, t, c * P:(c + 1) * P],
                                                            turned_sb[:, 0:2, :, :].rearrange("p a b n -> p a (b n)")[:, m, t * BANK:(t + 1) * BANK],
                                                            start=t == 0 and n == 0, stop=t == TILES - 1 and n == 2)
                        last.then_inc(done[kind], 1)
                    if kind == "hidden_layer":
                        (w,) = which
                        pe.wait_ge(done["gathered"], count(b, "gathered", w))
                        if w == 0:
                            pe.wait_ge(w1_loaded, (b + 1) * (KT * 16))
                            pe.wait_ge(done["slot_exp"], (b + 1) * kinds["slot_exp"])
                        for k in range(4):
                            e = 4 * w + k
                            for c in range(KT):
                                last = nc.tensor.matmul(ring[0:H, e * P:(e + 1) * P], w1_sb[:, c, e, :],
                                                        gathered[:, c, e * P:(e + 1) * P], start=c == 0, stop=c == KT - 1)
                        last.then_inc(done[kind], 1)
                    if kind == "output_layer":
                        (w,) = which
                        pe.wait_ge(done["gelu"], (b + 1) * kinds["gelu"])
                        pe.wait_ge(w2_loaded[w % 2], b * 64 + 32 * (w // 2 + 1))
                        if w >= 2:
                            pe.wait_ge(done["slots_lo"], count(b, "slots_lo", w - 2))
                        for k in range(4):
                            e = 4 * w + k
                            at_col = (w % 2) * 2 * BANK + k * D
                            last = nc.tensor.matmul(ring[:, at_col:at_col + D], hidden[0:H + 1, e * P:(e + 1) * P],
                                                    w2_sb[:, w % 2, k, :], start=True, stop=True)
                        last.then_inc(done[kind], 1)
                    if kind == "row_logits":
                        (t,) = which
                        if t:
                            pe.wait_ge(done["row_exp"], count(b, "row_exp", t - 1))
                        else:
                            pe.wait_ge(done["slots_lo"], (b + 1) * kinds["slots_lo"])
                        for q in range(ES // BANK):
                            for n, (c, a, m) in enumerate(passes):
                                last = nc.tensor.matmul(ring[:, q * BANK:(q + 1) * BANK], rowsT[:, a, c, t * P:(t + 1) * P],
                                                        mu[:, m, c, q * BANK:(q + 1) * BANK], start=n == 0, stop=n == len(passes) - 1)
                        last.then_inc(done[kind], 1)
                    if kind == "turn_combine":
                        t, quad, part = which
                        n = at[(kind, *which)]
                        if quad == 0 and part == 0:
                            pe.wait_ge(done["row_split"], count(b, "row_split", t))
                        if n >= 2:
                            pe.wait_ge(done["combine_turned"], b * kinds["combine_turned"] + n - 1)
                        else:
                            pe.wait_ge(done["dispatch_turned"], (b + 1) * kinds["dispatch_turned"])
                        for k in range(4):
                            col = (4 * quad + k) * P
                            last = nc.tensor.transpose(turned[:, part, k * P:(k + 1) * P], parts[:, part, col:col + P], ident_r[:, :])
                        last.then_inc(done[kind], 1)
                    if kind == "spread":
                        (t,) = which
                        pe.wait_ge(done["combine_turned"], count(b, "combine_turned", t, E // 4 - 1, 1))
                        if t >= 2:
                            pe.wait_ge(done["add_rows"], count(b, "add_rows", t - 2))
                        else:
                            pe.wait_ge(done["gathered"], (b + 1) * kinds["gathered"])
                        for e in range(E):
                            for n, (a, m) in enumerate(PARTS):
                                last = nc.tensor.matmul(mix[:, t % 2, 0:D], turned_sb[:, t % 2, a, e * P:(e + 1) * P],
                                                        slots[:, m, e, :], start=e == 0 and n == 0, stop=e == E - 1 and n == 2)
                        last.then_inc(done[kind], 1)

        @block.scalar
        def _(act):
            act.wait_ge(mu_loaded, 16)
            nc.scalar.activation(gathered[:, :, :], exps[:, :, :], ACT.Square).then_inc(squares_ready, 1)
            act.wait_ge(sums_ready, 1)
            nc.scalar.activation(hidden[:, :], ring[:, :], ACT.Sqrt).then_inc(norms_ready, 1)
            for b in range(B):
                for kind, *which in plan:
                    if kind in ("std_1", "std_2", "std_3"):
                        act.wait_ge(done[kind.replace("std", "stats")], b + 1)
                        nc.scalar.activation(std[:, :], spread_sq[:, :], ACT.Sqrt).then_inc(done[kind], 1)
                    if kind == "lengths":
                        act.wait_ge(done["affine"], b + 1)
                        for t in range(TILES):
                            nc.scalar.activation(exps[:, 1, t * D:(t + 1) * D], exps[:, 0, t * D:(t + 1) * D], ACT.Square,
                                                 accum_out=spread_sq[:, t:t + 1]).then_inc(act_step, 1)
                        act.wait_ge(act_step, (b + 1) * TILES)
                        nc.scalar.activation(std[:, :], spread_sq[:, :], ACT.Sqrt).then_inc(done[kind], 1)
                    if kind == "rows_hi":
                        act.wait_ge(done["gather"], b * kinds["gather"])
                        nc.scalar.activation(rows[:, 0].rearrange("p t d -> p (t d)"), exps[:, 0, :], ACT.Copy).then_inc(done[kind], 1)
                    if kind == "rows_turned":
                        part, c = which
                        n = at[(kind, part, c)]
                        act.wait_ge(done["turn_rows"], count(b, "turn_rows", part, c))
                        nc.scalar.activation(rowsT[:, part, c, :], ring[:, (n % 2) * N:(n % 2 + 1) * N], ACT.Copy).then_inc(done[kind], 1)
                    if kind == "slot_exp":
                        (e,) = which
                        act.wait_ge(done["slot_max"], count(b, "slot_max", e))
                        if e >= 2:
                            act.wait_ge(done["slot_split"], count(b, "slot_split", e - 2))
                        if e == 0:
                            act.wait_ge(done["rows_lo"], b + 1)
                            act.wait_ge(done["unit_rows"], b + 1)
                        nc.scalar.activation(exps[:, e % 2, 0:N], ring[:, (e % 2) * N:(e % 2 + 1) * N], ACT.Exp,
                                             bias=neg_max[:, e % 2:e % 2 + 1], accum_out=total[:, e % 2:e % 2 + 1]
                                             ).then_inc(done[kind], 1)
                    if kind == "dispatch_turned":
                        e, half, part = which
                        act.wait_ge(done["turn_dispatch"], count(b, "turn_dispatch", e, half, part))
                        w = e // 4
                        if e % 4 == 0 and half == 0 and part == 0:
                            if w:
                                act.wait_ge(done["gather"], count(b, "gather", w - 1))
                            else:
                                act.wait_ge(done["spread"], b * kinds["spread"])
                        dst = turned_sb[:, part].rearrange("p a n -> p (a n)").rearrange("p (t n) -> p t n", n=BANK)
                        nc.scalar.activation(dst[:, 4 * half:4 * half + 4, (e % 4) * P:(e % 4 + 1) * P],
                                             turned[:, part, :].bitcast(F32).rearrange("p (t n) -> p t n", n=P),
                                             ACT.Copy).then_inc(done[kind], 1)
                    if kind == "gelu":
                        (w,) = which
                        act.wait_ge(done["hidden_layer"], count(b, "hidden_layer", w))
                        if w == 0:
                            act.wait_ge(ones_row_ready, 1)
                            act.wait_ge(consts_loaded, 5 * 16)
                            act.wait_ge(done["output_layer"], b * kinds["output_layer"])
                        for k in range(4):
                            e = 4 * w + k
                            last = nc.scalar.activation(hidden[0:H, e * P:(e + 1) * P], ring[0:H, e * P:(e + 1) * P], ACT.Gelu,
                                                        bias=b1_sb[:, e:e + 1])
                        last.then_inc(done[kind], 1)
                    if kind == "slots_hi":
                        (w,) = which
                        act.wait_ge(done["output_layer"], count(b, "output_layer", w))
                        if w == 0:
                            act.wait_ge(done["spread"], b * kinds["spread"])
                        nc.scalar.activation(slots[:, 0, 4 * w:4 * w + 4, :].rearrange("p e d -> p (e d)"),
                                             ring[:, (w % 2) * 2 * BANK:(w % 2 + 1) * 2 * BANK], ACT.Copy).then_inc(done[kind], 1)
                    if kind == "row_exp":
                        (t,) = which
                        act.wait_ge(done["row_max"], count(b, "row_max", t))
                        if t >= 2:
                            act.wait_ge(done["row_split"], count(b, "row_split", t - 2))
                            act.wait_ge(done["add_rows"], count(b, "add_rows", t - 2))
                        else:
                            act.wait_ge(done["slot_split"], (b + 1) * kinds["slot_split"])
                        nc.scalar.activation(exps[:, t % 2, :], ring[:, :], ACT.Exp, bias=neg_max[:, t % 2:t % 2 + 1],
                                             accum_out=total[:, t % 2:t % 2 + 1]).then_inc(done[kind], 1)
                    if kind == "combine_turned":
                        t, quad, part = which
                        act.wait_ge(done["turn_combine"], count(b, "turn_combine", t, quad, part))
                        if quad == 0 and part == 0:
                            if t >= 2:
                                act.wait_ge(done["spread"], count(b, "spread", t - 2))
                            else:
                                act.wait_ge(done["gather"], (b + 1) * kinds["gather"])
                        nc.scalar.activation(turned_sb[:, t % 2, part, quad * BANK:(quad + 1) * BANK],
                                             turned[:, part, :].bitcast(F32), ACT.Copy).then_inc(done[kind], 1)

        @block.vector
        def _(dve):
            steps = [0]
            per_sequence = 3 * 2 * TILES + 3 + (TILES + 1) + (3 + TILES) + 2 * E + 2 * TILES

            def step(instruction):
                instruction.then_inc(dve_step, 1)
                steps[0] += 1

            def settle(base):
                dve.wait_ge(dve_step, base + steps[0])

            dve.wait_ge(consts_loaded, 5 * 16)
            nc.vector.tensor_copy(ident_r[:, :], ident[:, :]).then_inc(ident_ready, 1)
            nc.vector.memset(ones[:, :], 1.0).then_inc(ones_ready, 1)
            dve.wait_ge(norms_ready, 1)
            step(nc.vector.tensor_scalar(hidden[:, :], hidden[:, :], L2_EPS, None, ALU.max))
            settle(0)
            step(nc.vector.reciprocal(hidden[:, :], hidden[:, :]))
            settle(0)
            for c in range(KT):
                step(nc.vector.tensor_tensor(exps[:, c, :], exps[:, c, :], hidden[:, :], ALU.mult))
            settle(0)
            step(nc.vector.tensor_copy(mu[:, 0], exps[:, :, :]))
            settle(0)
            nc.vector.tensor_tensor(mu[:, 1], exps[:, :, :], mu[:, 0].bitcast(F32), ALU.subtract).then_inc(mu_ready, 1)
            before = steps[0]
            dve.wait_ge(mu_ready, 1)
            nc.vector.memset(hidden[H:H + 1, :], 1.0).then_inc(ones_row_ready, 1)

            for b in range(B):
                steps[0] = 0
                base = b * per_sequence + before
                for kind, *which in plan:
                    if kind in ("stats_1", "stats_2", "stats_3"):
                        if kind == "stats_1":
                            dve.wait_ge(done["norm_3"], b)
                        elif kind == "stats_2":
                            dve.wait_ge(done["norm_1"], b + 1)
                        else:
                            dve.wait_ge(done["add_rows"], (b + 1) * kinds["add_rows"])
                        for t in range(TILES):
                            step(nc.vector.bn_stats(moments[:, t, :], y_rows(b, t, 1)))
                        settle(base)
                        for t in range(TILES):
                            step(nc.vector.bn_aggr(mean_var[:, t, :], moments[:, t, :]))
                        settle(base)
                        nc.vector.tensor_scalar(spread_sq[:, :], mean_var[:, :, 1:2].rearrange("p t a -> p (t a)"), LN_EPS, None, ALU.add
                                                ).then_inc(done[kind], 1)
                    if kind in ("norm_1", "norm_3"):
                        dve.wait_ge(done["std_1" if kind == "norm_1" else "std_3"], b + 1)
                        step(nc.vector.reciprocal(inv_std[:, :], std[:, :]))
                        settle(base)
                        for t in range(TILES):
                            last = nc.vector.tensor_scalar(y_rows(b, t, 1), y_rows(b, t, 1), mean_var[:, t, 0:1], inv_std[:, t:t + 1],
                                                           ALU.subtract, ALU.mult)
                        last.then_inc(done[kind], 1)
                    if kind == "affine":
                        dve.wait_ge(done["std_2"], b + 1)
                        step(nc.vector.reciprocal(inv_std[:, :], std[:, :]))
                        settle(base)
                        for t in range(TILES):
                            step(nc.vector.tensor_scalar(exps[:, 0, t * D:(t + 1) * D], y_rows(b, t, 1), mean_var[:, t, 0:1],
                                                         inv_std[:, t:t + 1], ALU.subtract, ALU.mult))
                        settle(base)
                        x_ln = exps[:, 0, :].rearrange("p (t d) -> p t d", d=D)
                        every = [P, TILES, D]
                        step(nc.vector.tensor_tensor(x_ln, x_ln, gamma[:, :].rearrange("p (a d) -> p a d", a=1).broadcast_to(every), ALU.mult))
                        settle(base)
                        nc.vector.tensor_tensor(x_ln, x_ln, beta[:, :].rearrange("p (a d) -> p a d", a=1).broadcast_to(every), ALU.add
                                                ).then_inc(done[kind], 1)
                    if kind == "unit_rows":
                        dve.wait_ge(done["lengths"], b + 1)
                        step(nc.vector.tensor_scalar(std[:, :], std[:, :], L2_EPS, None, ALU.max))
                        settle(base)
                        step(nc.vector.reciprocal(inv_std[:, :], std[:, :]))
                        settle(base)
                        step(nc.vector.tensor_scalar(inv_std[:, :], inv_std[:, :], scale[:, 0:1], None, ALU.mult))
                        settle(base)
                        dve.wait_ge(done["turn_combine"], b * kinds["turn_combine"])
                        for t in range(TILES):
                            cols = slice(t * D, (t + 1) * D)
                            step(nc.vector.tensor_scalar(parts[:, 0, cols], exps[:, 0, cols], inv_std[:, t:t + 1], None, ALU.mult))
                        settle(base)
                        for t in range(TILES):
                            cols = slice(t * D, (t + 1) * D)
                            last = nc.vector.scalar_tensor_tensor(parts[:, 1, cols], exps[:, 0, cols], inv_std[:, t:t + 1],
                                                                  parts[:, 0, cols].bitcast(F32), ALU.mult, ALU.subtract)
                        last.then_inc(done[kind], 1)
                    if kind == "rows_lo":
                        dve.wait_ge(done["rows_hi"], b + 1)
                        nc.vector.tensor_tensor(rows[:, 1].rearrange("p t d -> p (t d)"), exps[:, 0, :],
                                                rows[:, 0].rearrange("p t d -> p (t d)").bitcast(F32), ALU.subtract).then_inc(done[kind], 1)
                    if kind == "slot_max":
                        (e,) = which
                        dve.wait_ge(done["slot_logits"], count(b, "slot_logits", e))
                        if e >= 2:
                            dve.wait_ge(done["slot_exp"], count(b, "slot_exp", e - 2))
                        nc.vector.tensor_reduce(neg_max[:, e % 2:e % 2 + 1], ring[:, (e % 2) * N:(e % 2 + 1) * N], AX_X, ALU.max,
                                                negate=True).then_inc(done[kind], 1)
                    if kind == "slot_split":
                        (e,) = which
                        dve.wait_ge(done["slot_exp"], count(b, "slot_exp", e))
                        step(nc.vector.reciprocal(inv_total[:, e % 2:e % 2 + 1], total[:, e % 2:e % 2 + 1]))
                        settle(base)
                        if e >= 2:
                            dve.wait_ge(done["turn_dispatch"], count(b, "turn_dispatch", e - 2, TILES // 4 - 1, 1))
                        else:
                            dve.wait_ge(done["turn_rows"], (b + 1) * kinds["turn_rows"])
                        cols = slice((e % 2) * N, (e % 2 + 1) * N)
                        step(nc.vector.tensor_scalar(parts[:, 0, cols], exps[:, e % 2, 0:N], inv_total[:, e % 2:e % 2 + 1], None, ALU.mult))
                        settle(base)
                        nc.vector.scalar_tensor_tensor(parts[:, 1, cols], exps[:, e % 2, 0:N], inv_total[:, e % 2:e % 2 + 1],
                                                       parts[:, 0, cols].bitcast(F32), ALU.mult, ALU.subtract).then_inc(done[kind], 1)
                    if kind == "gathered":
                        (w,) = which
                        dve.wait_ge(done["gather"], count(b, "gather", w))
                        if w == 0:
                            dve.wait_ge(done["hidden_layer"], b * kinds["hidden_layer"])
                        nc.vector.tensor_copy(gathered[:, :, w * BANK:(w + 1) * BANK], mix[:, :, :]).then_inc(done[kind], 1)
                    if kind == "slots_lo":
                        (w,) = which
                        dve.wait_ge(done["slots_hi"], count(b, "slots_hi", w))
                        nc.vector.tensor_tensor(slots[:, 1, 4 * w:4 * w + 4, :].rearrange("p e d -> p (e d)"),
                                                ring[:, (w % 2) * 2 * BANK:(w % 2 + 1) * 2 * BANK],
                                                slots[:, 0, 4 * w:4 * w + 4, :].rearrange("p e d -> p (e d)").bitcast(F32),
                                                ALU.subtract).then_inc(done[kind], 1)
                    if kind == "row_max":
                        (t,) = which
                        dve.wait_ge(done["row_logits"], count(b, "row_logits", t))
                        if t >= 2:
                            dve.wait_ge(done["row_exp"], count(b, "row_exp", t - 2))
                        else:
                            dve.wait_ge(done["slot_exp"], (b + 1) * kinds["slot_exp"])
                        nc.vector.tensor_reduce(neg_max[:, t % 2:t % 2 + 1], ring[:, :], AX_X, ALU.max, negate=True
                                                ).then_inc(done[kind], 1)
                    if kind == "row_split":
                        (t,) = which
                        dve.wait_ge(done["row_exp"], count(b, "row_exp", t))
                        if t:
                            dve.wait_ge(done["turn_combine"], count(b, "turn_combine", t - 1, E // 4 - 1, 1))
                        else:
                            dve.wait_ge(done["turn_dispatch"], (b + 1) * kinds["turn_dispatch"])
                        step(nc.vector.tensor_copy(parts[:, 0, :], exps[:, t % 2, :]))
                        settle(base)
                        nc.vector.tensor_tensor(parts[:, 1, :], exps[:, t % 2, :], parts[:, 0, :].bitcast(F32), ALU.subtract
                                                ).then_inc(done[kind], 1)
                    if kind == "add_rows":
                        (t,) = which
                        step(nc.vector.reciprocal(inv_total[:, t % 2:t % 2 + 1], total[:, t % 2:t % 2 + 1]))
                        settle(base)
                        dve.wait_ge(done["spread"], count(b, "spread", t))
                        nc.vector.scalar_tensor_tensor(y_rows(b, t, 1), mix[:, t % 2, 0:D], inv_total[:, t % 2:t % 2 + 1],
                                                       y_rows(b, t, 1), ALU.mult, ALU.add).then_inc(done[kind], 1)
                assert steps[0] == per_sequence, (steps[0], per_sequence)


_INS = ["L0_attn_x", "L0_attn_Wq", "L0_attn_Wk", "L0_attn_Wv", "L0_attn_Wo", "L0_attn_head_scale", "L0_ffn_gamma",
        "L0_ffn_beta", "L0_ffn_mu", "L0_ffn_scale", "L0_ffn_W1", "L0_ffn_b1", "L0_ffn_W2", "L0_ffn_b2"]
_OUTS = [((2, 1024, 256), "float32")]


def constants(positions, head, base=10000.0):
    powers = (np.arange(0, head, 2, dtype=np.float32) / np.float32(head)).astype(np.float64)
    inv_freq = (1.0 / np.power(base, powers)).astype(np.float32)
    angles = (inv_freq[:, None] * np.arange(positions, dtype=np.float32)[None, :]).astype(np.float64)
    cos, sin = np.cos(angles).astype(np.float32), np.sin(angles).astype(np.float32)
    later = np.arange(P)[None, :] > np.arange(P)[:, None]
    return {"const_cos": np.concatenate([cos, cos]), "const_sin": np.concatenate([-sin, sin]),
            "const_ident": np.eye(P, dtype=np.float32),
            "const_hidden": np.where(later, np.float32(HIDDEN), np.float32(0.0))}


def program(nc, x, wq, wk, wv, wo, head_scale, gamma, beta, mu, scale, w1, b1, w2, b2, cos, sin, ident, hidden, out):
    B, N, D = x.shape
    with nc.sbuf_tensor("y_sb", [P, B * N // P, D], F32) as y_sb:
        attention(nc, y_sb, x, wq, wk, wv, wo, head_scale, cos, sin, ident, hidden)
        soft_experts(nc, y_sb, gamma, beta, mu, scale, w1, b1, w2, b2, ident, out)


def kernel(**inputs):
    import numpy as _np
    import concourse.bacc as _bacc
    from concourse import mybir as _mybir
    from concourse.bass_utils import run_bass_kernel_spmd as _run

    nc = _bacc.Bacc("TRN2", target_bir_lowering=False, num_devices=1)
    arrays, args = {}, []
    for name in _INS:
        a = _np.ascontiguousarray(inputs[name])
        arrays[f"in_{name}_dram"] = a
        args.append(nc.dram_tensor(f"in_{name}_dram", a.shape, _mybir.dt.from_np(a.dtype), kind="ExternalInput").ap())
    for name, a in constants(1024, 128).items():
        arrays[f"{name}_dram"] = a
        args.append(nc.dram_tensor(f"{name}_dram", a.shape, _mybir.dt.from_np(a.dtype), kind="ExternalInput").ap())
    for i, (shape, dtype) in enumerate(_OUTS):
        dt = _mybir.dt.from_np(_np.dtype(dtype))
        args.append(nc.dram_tensor(f"out_{i}_dram", shape, dt, kind="ExternalOutput").ap())
    program(nc, *args)
    r = _run(nc, [arrays], core_ids=[0])
    got = tuple(r.results[0][f"out_{i}_dram"] for i in range(len(_OUTS)))
    return got[0]
```

```python
from collections import Counter
from contextlib import ExitStack

import concourse.bass as bass
import numpy as np
from concourse import mybir

F32 = mybir.dt.float32
F32R = mybir.dt.float32r
BF16 = mybir.dt.bfloat16
ALU = mybir.AluOpType
ACT = mybir.ActivationFunctionType
AX_X = mybir.AxisListType.X

P = 128
BANK = 512
LN_EPS = 1e-5
L2_EPS = 1e-12
HIDDEN = -(2.0 ** 120)
START = 64
PARTS = ((0, 0), (0, 1), (1, 0))


def plan_heads(part, heads, tiles):
    plan, deferred, later = [], [], []

    def settle():
        plan.extend(deferred)
        deferred[:] = later
        later.clear()

    def rope(who, n):
        plan.append(("project", who, n))
        deferred.extend([("take", who, n), ("swap", who, n)])
        later.extend([(kind, who, n) for kind in ("times_cos", "times_sin", "rope_add")])

    def split_rope(who, n):
        plan.extend([("rope_hi", who, n), ("rope_lo", who, n)])

    def weights(who, n):
        if who == "q":
            plan.extend([(f"load_q{n % 2}", who, n), ("scale_weights", who, n)])
        else:
            plan.append((f"load_{who}", who, n))
        plan.extend([("weights_hi", who, n), ("weights_lo", who, n)])

    def out_weights(pair):
        plan.extend([(kind, pair) for kind in ("load_o", "scale_out", "out_hi", "out_lo")])

    def top(h, i):
        plan.extend([("scores", h, i), ("max", h, i)])
        deferred.append(("sum_exp", h, i))

    def to_columns(h, w):
        plan.extend([(kind, h, w) for kind in ("invert", "columns_hi", "columns_lo")])

    def to_rows(h, w):
        plan.extend([(kind, h, w) for kind in ("turn_columns", "rows_copied")])

    def widen(h, w):
        plan.append(("widen", h, w))
        deferred.append(("widened", h, w))

    def tile(h, w, j):
        plan.extend([(kind, h, w, j) for kind in ("key_scores", "exp", "exp_hi", "exp_lo")])
        settle()

    def weigh(h, w, j):
        plan.append(("weigh", h, w, j))
        if j == 4 * w + 3:
            plan.append(("mixed", h, w))
            deferred.extend([("mixed_hi", h, w), ("mixed_lo", h, w)])

    def output(pair, w):
        plan.extend([("output", pair, w), ("add_output", pair, w)])

    if part == "first":
        for who, n in (("v", 0), ("k", 0), ("q", 0), ("q", 1)):
            weights(who, n)
        plan.extend([(kind, "x", 0, c) for c in range(2) for kind in ("turn_x", "xT_hi", "xT_lo")])
        plan.extend([(kind, "v", 0) for kind in ("project", "take", "turn_v", "v_hi", "v_lo")])
        for who in ("k", "q"):
            rope(who, 0)
            settle()
            settle()
            split_rope(who, 0)
        plan.extend([(kind, "x", 1, c) for c in range(2) for kind in ("turn_x", "xT_hi", "xT_lo")])
        for i in (3, 2, 1, 0, 7, 6, 5, 4):
            top(0, i)
            settle()
            if i == 0:
                rope("q", 1)
            if i == 6:
                to_columns(0, 0)
                to_rows(0, 0)
        split_rope("q", 1)
        return plan

    more = part == "body"
    tops = {1: (3,), 2: (7,), 3: (6,), 4: (2,), 6: (5,), 7: (1,), 8: (0,), 9: (4,)}
    for h in range(heads):
        following = more or h + 1 < heads
        ahead = more or h + 2 < heads
        group_ahead = more or h < 4
        if ahead:
            weights("q", h + 2)
        if h % 4 < 2 and group_ahead:
            weights("kv"[h % 4], h // 4 + 1)
        if h == 0:
            out_weights(0)
        steps = [(0, j) for j in range(4)] + [(1, j) for j in range(8)]
        for n, step in enumerate(steps):
            tile(h, *step)
            if n == 0:
                to_columns(h, 1)
            if n == 10 and following:
                to_columns(h + 1, 0)
            if n == 5 and group_ahead and h % 4 == 2:
                split_rope("k", h // 4 + 1)
            if n == 10 and ahead:
                split_rope("q", h + 2)
            if n == 0 and group_ahead and h % 4 == 3:
                plan.append(("turn_v", "v", h // 4 + 1))
                deferred.extend([(kind, "v", h // 4 + 1) for kind in ("v_hi", "v_lo")])
            if n == 8:
                if h % 2:
                    output(h // 2, 0)
                elif h:
                    output(h // 2 - 1, 1)
                    out_weights(h // 2)
            if following and (h, n) != (heads - 1, 9):
                for i in tops.get(n, ()):
                    top(h + 1, i)
            if n == 2:
                to_rows(h, 1)
                widen(h, 0)
            if n == 5 and ahead:
                rope("q", h + 2)
            if n == 6:
                widen(h, 1)
            if n == 11 and following:
                to_rows(h + 1, 0)
            if n == 10 and group_ahead and h % 4 == 1:
                rope("k", h // 4 + 1)
            if n == 10 and group_ahead and h % 4 == 2:
                plan.append(("project", "v", h // 4 + 1))
                deferred.append(("take", "v", h // 4 + 1))
            if n >= 2:
                weigh(h, *steps[n - 2])
        weigh(h, *steps[-2])
        weigh(h, *steps[-1])
    if more:
        top(heads, 4)
    deferred.reverse()
    settle()
    settle()
    output(heads // 2 - 1, 1)
    return plan


def attention(nc, y_sb, x_d, wq_d, wk_d, wv_d, wo_d, head_scale_d, cos_d, sin_d, ident_d, hidden_d):
    B, N, D = x_d.shape
    DH = P
    HEADS = wq_d.shape[1] // DH
    GROUPS = wk_d.shape[1] // DH
    TILES = N // P
    KT = D // P
    SCALE = DH ** -0.5
    TURN_GROUPS = 2
    TURN_HEADS = TURN_GROUPS * HEADS // GROUPS
    TURNS = B * GROUPS // TURN_GROUPS
    first, body, last_turn = [plan_heads(part, TURN_HEADS, TILES) for part in ("first", "body", "last")]

    def number(plan):
        seen, at = Counter(), {}
        for item in plan:
            at[item] = seen[item[0]]
            seen[item[0]] += 1
        return at, seen

    at_first, in_first = number(first)
    at_body, in_body = number(body)
    at_last, _ = number(last_turn)
    kinds = list(dict.fromkeys(item[0] for item in first + body))
    FILLS = ("turn_x", "project", "turn_v", "scores", "output")
    SMALL_FILLS = ("key_scores", "turn_columns", "widen")
    SMALLS = 3
    HELD = 3
    QUERIES = 4

    def past(it, kind):
        return START if it is None else START + in_first[kind] + it * in_body[kind]

    def count(it, kind, *which):
        at = at_first if it is None else at_last if isinstance(it, int) else at_body
        if (kind, *which) in at:
            return past(it, kind) + at[(kind, *which)] + 1
        if it is None:
            return None
        if which[0] in ("k", "v"):
            item = (kind, which[0], which[1] + TURN_GROUPS, *which[2:])
        elif which[0] == "q":
            item = (kind, "q", which[1] + TURN_HEADS)
        elif "out" in kind:
            item = (kind, which[0] + TURN_HEADS // 2, *which[1:])
        else:
            item = (kind, which[0] + TURN_HEADS, *which[1:])
        return past(it, kind) - in_body[kind] + at_body[item] + 1

    with ExitStack() as ctx:
        def sb(name, shape, dt=F32):
            return ctx.enter_context(nc.sbuf_tensor(name, shape, dt))

        def psum(name, shape, dt=F32):
            return ctx.enter_context(nc.psum_tensor(name, shape, dt))

        def sem(name):
            return ctx.enter_context(nc.semaphore(name))

        xT = sb("xT", [P, 2, B * KT, N], F32R)
        qT = sb("qT", [P, QUERIES, 2, N], F32R)
        kT = sb("kT", [P, 2, 2, N], F32R)
        taken = sb("taken", [P, N])
        v_sb = sb("v_sb", [P, 2, 2, N], F32R)
        exps = sb("exps", [P, 2, BANK])
        exp_parts = sb("exp_parts", [P, HELD, 2, BANK], F32R)
        summed = sb("summed", [P, N])
        mix_sb = sb("mix_sb", [P, BANK])
        inv_wide = sb("inv_wide", [P, 2, BANK])
        mixed = sb("mixed", [P, 2, 2, N], F32R)
        cos_sb = sb("cos_sb", [P, N])
        sin_sb = sb("sin_sb", [P, N])
        rotated = sb("rotated", [P, N])
        cos_part = sb("cos_part", [P, N])
        raw = {"k": sb("raw_k", [P, KT, DH]), "v": sb("raw_v", [P, KT, DH]), "o": sb("raw_o", [P, 2, D])}
        raw_q = [sb(f"raw_q{i}", [P, KT, DH]) for i in range(2)]
        wk_sb = sb("wk_sb", [P, 2, KT, DH], F32R)
        wv_sb = sb("wv_sb", [P, 2, KT, DH], F32R)
        wq_sb = sb("wq_sb", [P, 2, 2, KT, DH], F32R)
        wo_sb = sb("wo_sb", [P, 2, 2, D], F32R)
        ident = sb("ident", [P, P])
        ident_r = sb("ident_r", [P, P], F32R)
        ident_b = sb("ident_b", [P, P], BF16)
        hidden = sb("hidden", [P, P])
        hidden_b = sb("hidden_b", [P, P], BF16)
        head_scale = sb("head_scale", [P, HEADS])
        unit = sb("unit", [P, 2])
        pick_max = sb("pick_max", [4, P], F32R)
        pick_inv = sb("pick_inv", [4, P], F32R)
        neg_max = sb("neg_max", [P, 2, TILES])
        row_sum = sb("row_sum", [P, 2, TILES])
        inv_sum = sb("inv_sum", [P, 2, 4])
        columns = sb("columns", [P, 2, 4, 4], F32R)
        rows = sb("rows4", [4, 2, BANK], F32R)
        ring = psum("ring", [P, 2, 2 * BANK])
        small = psum("small", [P, SMALLS, BANK])
        mix = psum("mix", [P, BANK])

        done = {kind: sem(f"{kind}_done") for kind in kinds}
        consts_loaded, tables_loaded, consts_ready, unit_ready = (
            sem("consts_loaded"), sem("tables_loaded"), sem("consts_ready"), sem("unit_ready"))
        x_loaded = [sem(f"x{b}_loaded") for b in range(B)]

        def loaded(it, kind, *which):
            return (count(it, kind, *which) - START) * (32 if kind == "swap" else 16)

        def start_counts(engine, *own):
            for kind in own:
                engine.sem_inc(done[kind], START)

        def wait_stage(engine, it, kind, *which):
            value = count(it, kind, *which)
            if value is not None:
                engine.wait_ge(done[kind], value)

        def before(plan, item, kind):
            return len([1 for other in plan[:plan.index(item)] if other[0] == kind])

        def wait_before(engine, it, kind, plan, item):
            engine.wait_ge(done[kind], past(it, kind) + before(plan, item, kind))

        def turns(engine, stages):
            stages(None, first)
            with engine.Fori(0, TURNS - 1) as it:
                stages(it, body)
            stages(TURNS - 1, last_turn)

        def sequence(it, who, n):
            if it is None:
                return 0
            per_turn, every = (TURN_HEADS, HEADS) if who == "q" else (TURN_GROUPS, GROUPS)
            return (it * per_turn + n) // every

        def in_sequence(it, who, n):
            if it is None:
                return n
            per_turn, every = (TURN_HEADS, HEADS) if who == "q" else (TURN_GROUPS, GROUPS)
            return (it * per_turn + n) % every

        def slot(plan, item):
            return len([1 for other in plan[:plan.index(item)] if other[0] in FILLS]) % 2

        def small_slot(plan, item):
            return len([1 for other in plan[:plan.index(item)] if other[0] in SMALL_FILLS]) % SMALLS

        def column(one, like):
            return one.rearrange("p (a b) -> p a b", b=1).broadcast_to(list(like.shape))

        def seen(w, j):
            return slice((max(4 * w, j) - 4 * w) * P, BANK)

        x_rows = x_d.rearrange("b (t p) d -> b p t d", p=P)
        wq_cols = wq_d.rearrange("(t c) n -> c t n", c=P)
        wk_cols = wk_d.rearrange("(t c) n -> c t n", c=P)
        wv_cols = wv_d.rearrange("(t c) n -> c t n", c=P)
        wo_rows = wo_d.rearrange("(h d) n -> d h n", d=DH)
        block = ctx.enter_context(nc.Block())

        @block.sync
        def _(sp):
            sp.dma_start(y_sb[:, 0:TILES, :], x_rows[0]).then_inc(x_loaded[0], 16)
            sp.dma_start(ident[:, :], ident_d).then_inc(consts_loaded, 16)
            sp.dma_start(hidden[:, :], hidden_d).then_inc(consts_loaded, 16)

            def stages(it, plan):
                def starts(who, unit):
                    per_turn = TURN_HEADS if who == "q" else TURN_GROUPS
                    if it is None:
                        return (0,)
                    values = [in_sequence(it, who, n) * unit for n in (0, per_turn)]
                    return values if isinstance(it, int) else [sp.snap(value) for value in values]

                columns_at = {who: starts(who, DH) for who in ("q", "k")}
                rows_at = starts("q", 1)

                def columns(who, n):
                    per_turn = TURN_HEADS if who == "q" else TURN_GROUPS
                    return bass.ds(columns_at["q" if who == "q" else "k"][n // per_turn] + n % per_turn * DH, DH)

                for item in plan:
                    kind, *which = item
                    if kind in ("load_k", "load_v"):
                        who, n = which
                        source = (wk_cols if who == "k" else wv_cols)[:, :, columns(who, n)]
                        wait_stage(sp, it, "weights_lo", who, n - 1)
                        sp.dma_start(raw[who][:, :, :], source).then_inc(done[kind], 16)
                    if kind in ("load_q0", "load_q1"):
                        _, n = which
                        source = wq_cols[:, :, columns("q", n)]
                        wait_stage(sp, it, "weights_lo", "q", n - 2)
                        sp.dma_start(raw_q[n % 2][:, :, :], source).then_inc(done[kind], 16)
                    if kind == "swap":
                        sp.wait_ge(done["take"], count(it, "take", *which))
                        sp.dma_start(rotated[0:64, :], taken[64:128, :]).then_inc(done[kind], 16)
                        sp.dma_start(rotated[64:128, :], taken[0:64, :]).then_inc(done[kind], 16)
                    if kind == "load_o":
                        (pair,) = which
                        source = wo_rows[:, bass.ds(rows_at[0] + 2 * pair, 2), :]
                        wait_stage(sp, it, "out_lo", pair - 1)
                        sp.dma_start(raw["o"][:, :, :], source).then_inc(done[kind], 16)

            turns(sp, stages)

        @block.tensor
        def _(pe):
            start_counts(pe, "turn_x", "project", "scores", "turn_v", "turn_columns", "widen", "key_scores", "weigh", "output")
            pe.wait_ge(consts_ready, 5)

            def stages(it, plan):
                entries = [item for item in plan if item[0] in FILLS]
                tiles = [item[1:] for item in plan if item[0] == "exp"]
                small_entries = [item for item in plan if item[0] in SMALL_FILLS]

                def wait_reader(kind, which):
                    reader = {"turn_x": "xT_lo", "project": "take", "turn_v": "v_lo", "scores": "sum_exp", "output": "add_output",
                              "key_scores": "exp", "turn_columns": "rows_copied", "widen": "widened"}[kind]
                    wait_stage(pe, it, reader, *which)

                def free_ring(item):
                    e = entries.index(item)
                    if e >= 2:
                        wait_reader(entries[e - 2][0], entries[e - 2][1:])
                    elif it is not None:
                        pe.wait_ge(done["sum_exp"], past(it, "sum_exp"))
                        pe.wait_ge(done["add_output"], past(it, "add_output"))

                def free_small(item):
                    e = small_entries.index(item)
                    if e >= SMALLS:
                        wait_reader(small_entries[e - SMALLS][0], small_entries[e - SMALLS][1:])
                    elif it is not None:
                        for reader in ("exp", "rows_copied", "widened"):
                            pe.wait_ge(done[reader], past(it, reader))

                for item in plan:
                    kind, *which = item
                    if kind == "turn_x":
                        _, b, c = which
                        pe.wait_ge(x_loaded[b], 16)
                        free_ring(item)
                        for t in range(TILES):
                            last = nc.tensor.transpose(ring[:, slot(plan, item), t * P:(t + 1) * P],
                                                       y_sb[:, b * TILES + t, c * P:(c + 1) * P], ident[:, :])
                        last.then_inc(done[kind], 1)
                    if kind == "project":
                        who, n = which
                        w = wk_sb[:, :, :, :] if who == "k" else wv_sb[:, :, :, :] if who == "v" else wq_sb[:, n % 2, :, :, :]
                        pe.wait_ge(done["weights_lo"], count(it, "weights_lo", who, n))
                        if it is None:
                            pe.wait_ge(done["xT_lo"], count(it, "xT_lo", "x", 0, KT - 1))
                        free_ring(item)
                        passes = [(c, a, m) for c in range(KT) for a, m in PARTS]
                        for half in range(N // BANK):
                            cols = slice(half * BANK, (half + 1) * BANK)
                            for k, (c, a, m) in enumerate(passes):
                                moving = xT[:, m, bass.ds(sequence(it, who, n) * KT + c, 1), cols].rearrange("p a n -> p (a n)")
                                last = nc.tensor.matmul(ring[:, slot(plan, item), cols], w[:, a, c, :], moving,
                                                        start=k == 0, stop=k == len(passes) - 1)
                        last.then_inc(done[kind], 1)
                    if kind == "scores":
                        h, i = which
                        if i == 3:
                            wait_stage(pe, it, "rope_lo", "q", h)
                        free_ring(item)
                        width = (i + 1) * P
                        q = qT[:, h % QUERIES, :, i * P:(i + 1) * P]
                        for lo in range(0, width, BANK):
                            hi = min(width, lo + BANK)
                            diagonal = hi == width
                            for k, (a, m) in enumerate(PARTS):
                                last = nc.tensor.matmul(ring[:, slot(plan, item), lo:hi], q[:, a, :], kT[:, h // 4 % 2, m, lo:hi],
                                                        start=k == 0, stop=k == 2 and not diagonal)
                            if diagonal:
                                last = nc.tensor.matmul(ring[:, slot(plan, item), width - P:width], ident_b[:, :], hidden_b[:, :],
                                                        start=False, stop=True)
                        last.then_inc(done[kind], 1)
                    if kind == "turn_v":
                        pe.wait_ge(done["take"], count(it, "take", *which))
                        free_ring(item)
                        for t in range(TILES):
                            last = nc.tensor.transpose(ring[:, slot(plan, item), t * P:(t + 1) * P], taken[:, t * P:(t + 1) * P], ident[:, :])
                        last.then_inc(done[kind], 1)
                    if kind == "turn_columns":
                        h, w = which
                        pe.wait_ge(done["columns_lo"], count(it, "columns_lo", h, w))
                        free_small(item)
                        for t in range(4):
                            last = nc.tensor.matmul(small[0:4, small_slot(plan, item), t * P:(t + 1) * P], columns[:, w, t, :],
                                                    ident_r[:, :], start=True, stop=True)
                        last.then_inc(done[kind], 1)
                    if kind == "widen":
                        h, w = which
                        pe.wait_ge(done["rows_copied"], count(it, "rows_copied", h, w))
                        free_small(item)
                        nc.tensor.matmul(small[:, small_slot(plan, item), :], pick_inv[:, :], rows[:, w, :], start=True, stop=True
                                         ).then_inc(done[kind], 1)
                    if kind == "key_scores":
                        h, w, j = which
                        if j == 0:
                            pe.wait_ge(done["rows_copied"], count(it, "rows_copied", h, w))
                        free_small(item)
                        bank = small[:, small_slot(plan, item), :]
                        cols = seen(w, j)
                        queries = slice(max(4 * w, j) * P, (4 * w + 4) * P)
                        for k, (a, m) in enumerate(PARTS):
                            nc.tensor.matmul(bank[:, cols], kT[:, h // 4 % 2, a, j * P:(j + 1) * P], qT[:, h % QUERIES, m, queries],
                                             start=k == 0, stop=False)
                        last = nc.tensor.matmul(bank[:, cols], pick_max[:, :], rows[:, w, cols], start=False, stop=j < 4 * w)
                        if j >= 4 * w:
                            last = nc.tensor.matmul(bank[:, cols.start:cols.start + P], hidden_b[:, :], ident_b[:, :],
                                                    start=False, stop=True)
                        last.then_inc(done[kind], 1)
                    if kind == "weigh":
                        h, w, j = which
                        pe.wait_ge(done["exp_lo"], count(it, "exp_lo", h, w, j))
                        if j == 0:
                            wait_stage(pe, it, "mixed", *((h, 0) if w else (h - 1, 1)))
                            wait_stage(pe, it, "v_lo", "v", h // 4)
                        for k, (a, m) in enumerate(PARTS):
                            last = nc.tensor.matmul(mix[:, seen(w, j)], v_sb[:, h // 4 % 2, a, j * P:(j + 1) * P],
                                                    exp_parts[:, tiles.index((h, w, j)) % HELD, m, seen(w, j)],
                                                    start=j == 0 and k == 0, stop=j == 4 * w + 3 and k == 2)
                        last.then_inc(done[kind], 1)
                    if kind == "output":
                        pair, w = which
                        pe.wait_ge(done["mixed_hi"], count(it, "mixed_hi", 2 * pair + 1, w))
                        pe.wait_ge(done["mixed_lo"], count(it, "mixed_lo", 2 * pair + 1, w))
                        pe.wait_ge(done["out_lo"], count(it, "out_lo", pair))
                        free_ring(item)
                        passes = [(hh, a, m) for hh in range(2) for a, m in PARTS]
                        for t in range(4):
                            for k, (hh, a, m) in enumerate(passes):
                                last = nc.tensor.matmul(ring[:, slot(plan, item), t * D:(t + 1) * D],
                                                        mixed[:, hh, a, (4 * w + t) * P:(4 * w + t + 1) * P],
                                                        wo_sb[:, m, hh, :], start=k == 0, stop=k == len(passes) - 1)
                        last.then_inc(done[kind], 1)

            turns(pe, stages)

        @block.scalar
        def _(act):
            act.dma_start(cos_sb[:, :], cos_d).then_inc(tables_loaded, 16)
            act.dma_start(sin_sb[:, :], sin_d).then_inc(tables_loaded, 16)
            act.dma_start(head_scale[:, :], head_scale_d.rearrange("a h b c -> (a b c) h").broadcast_to([P, HEADS])).then_inc(tables_loaded, 16)
            act.dma_start(y_sb[:, TILES:2 * TILES, :], x_rows[1]).then_inc(x_loaded[1], 16)
            start_counts(act, "xT_hi", "take", "rope_hi", "v_hi", "sum_exp", "exp", "exp_hi", "widened", "mixed_hi")

            def stages(it, plan):
                tiles = [item[1:] for item in plan if item[0] == "exp"]
                for item in plan:
                    kind, *which = item
                    if kind == "xT_hi":
                        _, b, c = which
                        act.wait_ge(done["turn_x"], count(it, "turn_x", *which))
                        nc.scalar.activation(xT[:, 0, b * KT + c, :], ring[:, slot(plan, ("turn_x", *which)), :], ACT.Copy
                                             ).then_inc(done[kind], 1)
                    if kind == "take":
                        who, n = which
                        act.wait_ge(done["project"], count(it, "project", *which))
                        wait_before(act, it, "rope_add", plan, item)
                        wait_before(act, it, "turn_v", plan, item)
                        nc.scalar.activation(taken[:, :], ring[:, slot(plan, ("project", *which)), :], ACT.Copy).then_inc(done[kind], 1)
                    if kind == "v_hi":
                        _, g = which
                        act.wait_ge(done["turn_v"], count(it, "turn_v", *which))
                        wait_stage(act, it, "weigh", 4 * g - 5, 1, 7)
                        nc.scalar.activation(v_sb[:, g % 2, 0, :], ring[:, slot(plan, ("turn_v", *which)), :], ACT.Copy
                                             ).then_inc(done[kind], 1)
                    if kind == "rope_hi":
                        who, n = which
                        dst = kT[:, n % 2] if who == "k" else qT[:, n % QUERIES]
                        act.wait_ge(done["rope_add"], count(it, "rope_add", who, n))
                        wait_stage(act, it, "key_scores", 4 * n - 5 if who == "k" else n - QUERIES, 1, 7)
                        nc.scalar.activation(dst[:, 0, :], cos_part[:, :], ACT.Copy).then_inc(done[kind], 1)
                    if kind == "sum_exp":
                        h, i = which
                        act.wait_ge(done["max"], count(it, "max", h, i))
                        if i % 4 == 3:
                            wait_stage(act, it, "invert", h - 2, i // 4)
                        wait_before(act, it, "sum_exp", plan, item)
                        nc.scalar.activation(summed[:, 0:(i + 1) * P], ring[:, slot(plan, ("scores", h, i)), 0:(i + 1) * P], ACT.Exp,
                                             bias=neg_max[:, h % 2, i:i + 1], accum_out=row_sum[:, h % 2, i:i + 1]
                                             ).then_inc(done[kind], 1)
                    if kind == "exp":
                        h, w, j = which
                        n = tiles.index((h, w, j))
                        act.wait_ge(done["key_scores"], count(it, "key_scores", h, w, j))
                        if n >= 2:
                            act.wait_ge(done["exp_lo"], count(it, "exp_lo", *tiles[n - 2]))
                        else:
                            act.wait_ge(done["exp_lo"], past(it, "exp_lo"))
                        nc.scalar.activation(exps[:, n % 2, seen(w, j)], small[:, small_slot(plan, ("key_scores", h, w, j)), seen(w, j)],
                                             ACT.Exp).then_inc(done[kind], 1)
                    if kind == "exp_hi":
                        h, w, j = which
                        n = tiles.index((h, w, j))
                        act.wait_ge(done["exp"], count(it, "exp", h, w, j))
                        if n >= HELD:
                            act.wait_ge(done["weigh"], count(it, "weigh", *tiles[n - HELD]))
                        else:
                            act.wait_ge(done["weigh"], past(it, "weigh"))
                        nc.scalar.activation(exp_parts[:, n % HELD, 0, seen(w, j)], exps[:, n % 2, seen(w, j)], ACT.Copy
                                             ).then_inc(done[kind], 1)
                    if kind == "widened":
                        h, w = which
                        act.wait_ge(done["widen"], count(it, "widen", h, w))
                        wait_stage(act, it, "mixed", h - 1, w)
                        nc.scalar.activation(inv_wide[:, w, :], small[:, small_slot(plan, ("widen", h, w)), :], ACT.Copy
                                             ).then_inc(done[kind], 1)
                    if kind == "mixed_hi":
                        h, w = which
                        act.wait_ge(done["mixed"], count(it, "mixed", h, w))
                        wait_stage(act, it, "output", h // 2 - 1, w)
                        nc.scalar.activation(mixed[:, h % 2, 0, w * BANK:(w + 1) * BANK], mix_sb[:, :], ACT.Copy).then_inc(done[kind], 1)

            turns(act, stages)

        @block.vector
        def _(dve):
            start_counts(dve, "xT_lo", "v_lo", "max", "invert", "columns_hi", "columns_lo", "rows_copied", "exp_lo", "mixed",
                         "times_cos", "rope_lo", "mixed_lo", "add_output")
            dve.wait_ge(consts_loaded, 2 * 16)
            nc.vector.tensor_copy(ident_r[:, :], ident[:, :]).then_inc(consts_ready, 1)
            nc.vector.tensor_copy(ident_b[:, :], ident[:, :]).then_inc(consts_ready, 1)
            nc.vector.tensor_copy(hidden_b[:, :], hidden[:, :]).then_inc(consts_ready, 1)
            for picked, row in ((pick_max, 0), (pick_inv, 2)):
                nc.vector.tensor_tensor(picked[:, :], ident[0:4, row:row + 1].broadcast_to([4, P]),
                                        ident[0:4, row + 1:row + 2].broadcast_to([4, P]), ALU.add).then_inc(consts_ready, 1)

            def stages(it, plan):
                tiles = [item[1:] for item in plan if item[0] == "exp"]
                for item in plan:
                    kind, *which = item
                    if kind == "xT_lo":
                        _, b, c = which
                        dve.wait_ge(done["xT_hi"], count(it, "xT_hi", *which))
                        nc.vector.tensor_tensor(xT[:, 1, b * KT + c, :], ring[:, slot(plan, ("turn_x", *which)), :],
                                                xT[:, 0, b * KT + c, :].bitcast(F32), ALU.subtract).then_inc(done[kind], 1)
                    if kind == "v_lo":
                        _, g = which
                        dve.wait_ge(done["v_hi"], count(it, "v_hi", *which))
                        nc.vector.tensor_tensor(v_sb[:, g % 2, 1, :], ring[:, slot(plan, ("turn_v", *which)), :],
                                                v_sb[:, g % 2, 0, :].bitcast(F32), ALU.subtract).then_inc(done[kind], 1)
                    if kind == "max":
                        h, i = which
                        dve.wait_ge(done["scores"], count(it, "scores", h, i))
                        nc.vector.tensor_reduce(neg_max[:, h % 2, i:i + 1], ring[:, slot(plan, ("scores", h, i)), 0:(i + 1) * P],
                                                AX_X, ALU.max, negate=True).then_inc(done[kind], 1)
                    if kind == "invert":
                        h, w = which
                        dve.wait_ge(done["sum_exp"], count(it, "sum_exp", h, 4 * w))
                        nc.vector.reciprocal(inv_sum[:, w, :], row_sum[:, h % 2, 4 * w:4 * w + 4]).then_inc(done[kind], 1)
                    if kind in ("columns_hi", "columns_lo"):
                        h, w = which
                        values = (neg_max[:, h % 2, 4 * w:4 * w + 4], inv_sum[:, w, :])
                    if kind == "columns_hi":
                        dve.wait_ge(done["invert"], count(it, "invert", h, w))
                        wait_stage(dve, it, "turn_columns", h - 1, w)
                        for k, value in enumerate(values):
                            last = nc.vector.tensor_copy(columns[:, w, :, 2 * k:2 * k + 1], value.rearrange("p (t a) -> p t a", a=1))
                        last.then_inc(done[kind], 1)
                    if kind == "columns_lo":
                        dve.wait_ge(done["columns_hi"], count(it, "columns_hi", h, w))
                        for k, value in enumerate(values):
                            last = nc.vector.tensor_tensor(columns[:, w, :, 2 * k + 1:2 * k + 2], value.rearrange("p (t a) -> p t a", a=1),
                                                           columns[:, w, :, 2 * k:2 * k + 1].bitcast(F32), ALU.subtract)
                        last.then_inc(done[kind], 1)
                    if kind == "rows_copied":
                        h, w = which
                        dve.wait_ge(done["turn_columns"], count(it, "turn_columns", h, w))
                        nc.vector.tensor_copy(rows[:, w, :], small[0:4, small_slot(plan, ("turn_columns", h, w)), :]
                                              ).then_inc(done[kind], 1)
                    if kind == "exp_lo":
                        h, w, j = which
                        n = tiles.index((h, w, j))
                        dve.wait_ge(done["exp_hi"], count(it, "exp_hi", h, w, j))
                        nc.vector.tensor_tensor(exp_parts[:, n % HELD, 1, seen(w, j)], exps[:, n % 2, seen(w, j)],
                                                exp_parts[:, n % HELD, 0, seen(w, j)].bitcast(F32), ALU.subtract).then_inc(done[kind], 1)
                    if kind == "mixed":
                        h, w = which
                        dve.wait_ge(done["weigh"], count(it, "weigh", h, w, 4 * w + 3))
                        dve.wait_ge(done["widened"], count(it, "widened", h, w))
                        wait_before(dve, it, "mixed_lo", plan, item)
                        nc.vector.tensor_tensor(mix_sb[:, :], mix[:, :], inv_wide[:, w, :], ALU.mult).then_inc(done[kind], 1)
                    if kind == "times_cos":
                        dve.wait_ge(done["take"], count(it, "take", *which))
                        if it is None:
                            dve.wait_ge(tables_loaded, 3 * 16)
                        wait_before(dve, it, "rope_lo", plan, item)
                        nc.vector.tensor_tensor(cos_part[:, :], taken[:, :], cos_sb[:, :], ALU.mult).then_inc(done[kind], 1)
                    if kind == "rope_lo":
                        who, n = which
                        dst = kT[:, n % 2] if who == "k" else qT[:, n % QUERIES]
                        dve.wait_ge(done["rope_hi"], count(it, "rope_hi", who, n))
                        nc.vector.tensor_tensor(dst[:, 1, :], cos_part[:, :], dst[:, 0, :].bitcast(F32), ALU.subtract
                                                ).then_inc(done[kind], 1)

                    if kind == "mixed_lo":
                        h, w = which
                        cols = slice(w * BANK, (w + 1) * BANK)
                        dve.wait_ge(done["mixed_hi"], count(it, "mixed_hi", h, w))
                        nc.vector.tensor_tensor(mixed[:, h % 2, 1, cols], mix_sb[:, :], mixed[:, h % 2, 0, cols].bitcast(F32), ALU.subtract
                                                ).then_inc(done[kind], 1)
                    if kind == "add_output":
                        pair, w = which
                        dve.wait_ge(done["output"], count(it, "output", pair, w))
                        wait_before(dve, it, "add_output", plan, item)
                        y_rows = y_sb[:, bass.ds(sequence(it, "q", 0) * TILES + 4 * w, 4), :].rearrange("p t d -> p (t d)")
                        nc.vector.tensor_tensor(y_rows, ring[:, slot(plan, ("output", pair, w)), :], y_rows, ALU.add).then_inc(done[kind], 1)

            turns(dve, stages)

        @block.gpsimd
        def _(pool):
            start_counts(pool, "scale_weights", "weights_hi", "weights_lo", "scale_out", "out_hi", "out_lo", "times_sin",
                         "rope_add")
            nc.gpsimd.memset(unit[:, 0:1], 1.0).then_inc(unit_ready, 1)
            nc.gpsimd.memset(unit[:, 1:2], SCALE).then_inc(unit_ready, 1)
            pool.wait_ge(unit_ready, 2)
            one, score_scale = unit[:, 0:1], unit[:, 1:2]

            def stages(it, plan):
                for item in plan:
                    kind, *which = item
                    if kind in ("scale_weights", "weights_hi", "weights_lo"):
                        who, n = which
                        source = raw_q[n % 2] if who == "q" else raw[who]
                        w = wq_sb[:, n % 2] if who == "q" else wk_sb if who == "k" else wv_sb
                    if kind == "scale_weights":
                        load = f"load_q{n % 2}"
                        pool.wait_ge(done[load], loaded(it, load, who, n))
                        nc.gpsimd.tensor_tensor(source[:, :, :], source[:, :, :], column(score_scale, source), ALU.mult
                                                ).then_inc(done[kind], 1)
                    if kind == "weights_hi":
                        if who == "q":
                            pool.wait_ge(done["scale_weights"], count(it, "scale_weights", who, n))
                        else:
                            pool.wait_ge(done[f"load_{who}"], loaded(it, f"load_{who}", who, n))
                        wait_stage(pool, it, "project", who, n - (2 if who == "q" else 1))
                        nc.gpsimd.tensor_tensor(w[:, 0], source[:, :, :], column(one, source), ALU.mult).then_inc(done[kind], 1)
                    if kind == "weights_lo":
                        pool.wait_ge(done["weights_hi"], count(it, "weights_hi", who, n))
                        nc.gpsimd.tensor_tensor(w[:, 1], source[:, :, :], w[:, 0].bitcast(F32), ALU.subtract).then_inc(done[kind], 1)
                    if kind == "scale_out":
                        (pair,) = which
                        pool.wait_ge(done["load_o"], loaded(it, "load_o", pair))
                        if it is None or pair == 0:
                            pool.wait_ge(tables_loaded, 3 * 16)
                        scales = head_scale[:, bass.ds(in_sequence(it, "q", 2 * pair), 2)].rearrange("p (h a) -> p h a", a=1)
                        nc.gpsimd.tensor_tensor(raw["o"][:, :, :], raw["o"][:, :, :], scales.broadcast_to([P, 2, D]), ALU.mult
                                                ).then_inc(done[kind], 1)
                    if kind == "out_hi":
                        (pair,) = which
                        pool.wait_ge(done["scale_out"], count(it, "scale_out", pair))
                        wait_stage(pool, it, "output", pair - 1, 1)
                        nc.gpsimd.tensor_tensor(wo_sb[:, 0], raw["o"][:, :, :], column(one, raw["o"]), ALU.mult).then_inc(done[kind], 1)
                    if kind == "out_lo":
                        (pair,) = which
                        pool.wait_ge(done["out_hi"], count(it, "out_hi", pair))
                        nc.gpsimd.tensor_tensor(wo_sb[:, 1], raw["o"][:, :, :], wo_sb[:, 0].bitcast(F32), ALU.subtract
                                                ).then_inc(done[kind], 1)
                    if kind == "times_sin":
                        pool.wait_ge(done["swap"], loaded(it, "swap", *which))
                        if it is None:
                            pool.wait_ge(tables_loaded, 3 * 16)
                        nc.gpsimd.tensor_tensor(rotated[:, :], rotated[:, :], sin_sb[:, :], ALU.mult).then_inc(done[kind], 1)
                    if kind == "rope_add":
                        pool.wait_ge(done["times_cos"], count(it, "times_cos", *which))
                        pool.wait_ge(done["times_sin"], count(it, "times_sin", *which))
                        nc.gpsimd.tensor_tensor(cos_part[:, :], cos_part[:, :], rotated[:, :], ALU.add).then_inc(done[kind], 1)

            turns(pool, stages)


def plan_experts(experts, tiles):
    plan = [(kind,) for kind in ("stats_1", "std_1", "norm_1", "stats_2", "std_2", "affine", "lengths", "unit_rows",
                                 "rows_hi", "rows_lo")]
    for part in range(2):
        for c in range(2):
            plan.extend([("turn_rows", part, c), ("rows_turned", part, c)])

    def fill(e):
        plan.extend([("slot_logits", e), ("slot_max", e), ("slot_exp", e), ("slot_split", e)])

    def turn(kind, copied, *which):
        plan.extend([(kind, *which, 0), (kind, *which, 1), (copied, *which, 0), (copied, *which, 1)])

    fill(0)
    for e in range(experts):
        if e + 1 < experts:
            fill(e + 1)
        for half in range(tiles // 4):
            turn("turn_dispatch", "dispatch_turned", e, half)
        if e % 4 == 3:
            plan.extend([("gather", e // 4), ("gathered", e // 4)])
    for w in range(experts // 4):
        plan.extend([("hidden_layer", w), ("gelu", w)])
    for w in range(experts // 4):
        plan.extend([("output_layer", w), ("slots_hi", w), ("slots_lo", w)])

    def fill_row(t):
        plan.extend([("row_logits", t), ("row_max", t), ("row_exp", t)])

    fill_row(0)
    plan.append(("row_split", 0))
    for t in range(tiles):
        if t + 1 < tiles:
            fill_row(t + 1)
        for quad in range(experts // 4):
            turn("turn_combine", "combine_turned", t, quad)
        if t + 1 < tiles:
            plan.append(("row_split", t + 1))
        plan.extend([("spread", t), ("add_rows", t)])
    plan.extend([("stats_3",), ("std_3",), ("norm_3",)])
    return plan


def soft_experts(nc, y_sb, gamma_d, beta_d, mu_d, scale_d, w1_d, b1_d, w2_d, b2_d, ident_d, out_d):
    B, N, D = out_d.shape
    _, E, S = mu_d.shape
    H = w1_d.shape[2]
    TILES = N // P
    KT = D // P
    ES = E * S
    assert S == P and KT == 2
    plan = plan_experts(E, TILES)
    kinds, at = {}, {}
    for item in plan:
        at[item] = kinds.get(item[0], 0)
        kinds[item[0]] = at[item] + 1

    with ExitStack() as ctx:
        def sb(name, shape, dt=F32):
            return ctx.enter_context(nc.sbuf_tensor(f"ffn_{name}", shape, dt))

        def psum(name, shape, dt=F32):
            return ctx.enter_context(nc.psum_tensor(f"ffn_{name}", shape, dt))

        def sem(name):
            return ctx.enter_context(nc.semaphore(f"ffn_{name}"))

        rows = sb("rows", [P, 2, TILES, D], F32R)
        rowsT = sb("rowsT", [P, 2, KT, N], F32R)
        mu = sb("mu", [P, 2, KT, ES], F32R)
        slots = sb("slots", [P, 2, E, D], F32R)
        exps = sb("exps", [P, 2, ES])
        parts = sb("parts", [P, 2, ES], F32R)
        turned_sb = sb("turned_sb", [P, 2, 2, ES], F32R)
        gathered = sb("gathered", [P, KT, ES])
        hidden = sb("hidden_h", [P, ES])
        w2_sb = exps[0:H + 1, 0, :].rearrange("p (a e d) -> p a e d", a=2, e=4)
        w1_sb = exps[:, 1, :].rearrange("p (c e h) -> p c e h", c=KT, e=E)
        b1_sb = sb("b1_sb", [H, E])
        gamma = sb("gamma", [P, D])
        beta = sb("beta", [P, D])
        scale = sb("scale", [P, 1])
        ident = sb("ident2", [P, P])
        ident_r = sb("ident2_r", [P, P], F32R)
        ones = sb("ones", [P, P])
        moments = sb("moments", [P, TILES, 6])
        mean_var = sb("mean_var", [P, TILES, 2])
        spread_sq = sb("spread_sq", [P, TILES])
        std = sb("std", [P, TILES])
        inv_std = sb("inv_std", [P, TILES])
        neg_max = sb("neg_max2", [P, 2])
        total = sb("total", [P, 2])
        inv_total = sb("inv_total", [P, 2])
        ring = psum("ring2", [P, 4 * BANK])
        turned = psum("turned2", [P, 2, BANK], F32R)
        mix = psum("mix2", [P, 2, BANK])

        done = {kind: sem(f"{kind}_done") for kind in kinds}
        consts_loaded, mu_loaded, w1_loaded = sem("consts2_loaded"), sem("mu_loaded"), sem("w1_loaded")
        w2_loaded = [sem("w2_even_loaded"), sem("w2_odd_loaded")]
        ones_ready, ident_ready, squares_ready, sums_ready, norms_ready, mu_ready = (
            sem("ones_ready"), sem("ident_ready"), sem("squares_ready"), sem("sums_ready"), sem("norms_ready"), sem("mu_ready"))
        ones_row_ready = sem("ones_row_ready")
        dve_step, act_step, stored = sem("dve_step2"), sem("act_step2"), sem("stored")

        def count(b, kind, *which):
            return b * kinds[kind] + at[(kind, *which)] + 1

        block = ctx.enter_context(nc.Block())

        def y_rows(b, t=0, n=TILES):
            return y_sb[:, bass.ds(b * TILES + t, n), :].rearrange("p t d -> p (t d)")

        @block.sync
        def _(sp):
            sp.dma_start(exps[:, :, :], mu_d.rearrange("(c p) e s -> p c (e s)", p=P)).then_inc(mu_loaded, 16)
            sp.dma_start(ident[:, :], ident_d).then_inc(consts_loaded, 16)
            sp.dma_start(gamma[:, :], gamma_d.rearrange("(a d) -> a d", a=1).broadcast_to([P, D])).then_inc(consts_loaded, 16)
            sp.dma_start(beta[:, :], beta_d.rearrange("(a d) -> a d", a=1).broadcast_to([P, D])).then_inc(consts_loaded, 16)
            sp.dma_start(scale[:, :], scale_d.rearrange("(a d) -> a d", a=1).broadcast_to([P, 1])).then_inc(consts_loaded, 16)
            sp.dma_start(b1_sb[:, :], b1_d.rearrange("e h -> h e"), allow_slow_non_contiguous=True).then_inc(consts_loaded, 16)
            for b in range(B):
                sp.wait_ge(done["slot_split"], (b + 1) * kinds["slot_split"])
                for c in range(KT):
                    sp.dma_start(w1_sb[:, c], w1_d[:, c * P:(c + 1) * P, :].rearrange("e p h -> p e h")).then_inc(w1_loaded, 16)
                for w in range(E // 4):
                    if w >= 2:
                        sp.wait_ge(done["output_layer"], count(b, "output_layer", w - 2))
                    else:
                        sp.wait_ge(done["output_layer"], b * kinds["output_layer"])
                    sp.dma_start(w2_sb[0:H, w % 2], w2_d[4 * w:4 * w + 4].rearrange("e h d -> h e d")).then_inc(w2_loaded[w % 2], 16)
                    sp.dma_start(w2_sb[H:H + 1, w % 2], b2_d[4 * w:4 * w + 4].rearrange("(a e) d -> a e d", a=1)
                                 ).then_inc(w2_loaded[w % 2], 16)
                sp.wait_ge(done["norm_3"], b + 1)
                sp.dma_start(out_d[bass.ds(b, 1)].rearrange("a (t p) d -> p (a t) d", p=P),
                             y_sb[:, bass.ds(b * TILES, TILES), :]).then_inc(stored, 16)
            sp.wait_ge(stored, 16 * B)

        @block.tensor
        def _(pe):
            pe.wait_ge(ones_ready, 1)
            pe.wait_ge(squares_ready, 1)
            for q in range(ES // BANK):
                for c in range(KT):
                    last = nc.tensor.matmul(ring[:, q * BANK:(q + 1) * BANK], ones[:, :], gathered[:, c, q * BANK:(q + 1) * BANK],
                                            start=c == 0, stop=c == KT - 1)
            last.then_inc(sums_ready, 1)
            pe.wait_ge(ident_ready, 1)
            pe.wait_ge(mu_ready, 1)
            passes = [(c, a, m) for c in range(KT) for a, m in PARTS]
            for b in range(B):
                for kind, *which in plan:
                    if kind == "turn_rows":
                        part, c = which
                        n = at[(kind, part, c)]
                        if n == 0:
                            pe.wait_ge(done["unit_rows"], b + 1)
                            pe.wait_ge(done["row_exp"], b * kinds["row_exp"])
                        if n >= 2:
                            pe.wait_ge(done["rows_turned"], b * kinds["rows_turned"] + n - 1)
                        unit = parts[:, part, :].rearrange("p (t d) -> p t d", d=D)
                        for t in range(TILES):
                            last = nc.tensor.transpose(ring[:, (n % 2) * N + t * P:(n % 2) * N + (t + 1) * P].bitcast(F32R),
                                                       unit[:, t, c * P:(c + 1) * P], ident_r[:, :])
                        last.then_inc(done[kind], 1)
                    if kind == "slot_logits":
                        (e,) = which
                        if e == 0:
                            pe.wait_ge(done["rows_turned"], (b + 1) * kinds["rows_turned"])
                        if e >= 2:
                            pe.wait_ge(done["slot_exp"], count(b, "slot_exp", e - 2))
                        for half in range(N // BANK):
                            at_col = (e % 2) * N + half * BANK
                            for n, (c, a, m) in enumerate(passes):
                                last = nc.tensor.matmul(ring[:, at_col:at_col + BANK], mu[:, a, c, e * P:(e + 1) * P],
                                                        rowsT[:, m, c, half * BANK:(half + 1) * BANK],
                                                        start=n == 0, stop=n == len(passes) - 1)
                        last.then_inc(done[kind], 1)
                    if kind == "turn_dispatch":
                        e, half, part = which
                        n = at[(kind, *which)]
                        if half == 0 and part == 0:
                            pe.wait_ge(done["slot_split"], count(b, "slot_split", e))
                        if n >= 2:
                            pe.wait_ge(done["dispatch_turned"], b * kinds["dispatch_turned"] + n - 1)
                        else:
                            pe.wait_ge(done["combine_turned"], b * kinds["combine_turned"])
                        for t in range(4):
                            col = (e % 2) * N + (4 * half + t) * P
                            last = nc.tensor.transpose(turned[:, part, t * P:(t + 1) * P], parts[:, part, col:col + P], ident_r[:, :])
                        last.then_inc(done[kind], 1)
                    if kind == "gather":
                        (w,) = which
                        pe.wait_ge(done["dispatch_turned"], count(b, "dispatch_turned", 4 * w + 3, TILES // 4 - 1, 1))
                        pe.wait_ge(done["rows_lo"], b + 1)
                        pe.wait_ge(done["rows_hi"], b + 1)
                        if w:
                            pe.wait_ge(done["gathered"], count(b, "gathered", w - 1))
                        else:
                            pe.wait_ge(done["add_rows"], b * kinds["add_rows"])
                        for c in range(KT):
                            for t in range(TILES):
                                for n, (a, m) in enumerate(PARTS):
                                    last = nc.tensor.matmul(mix[:, c, :], rows[:, a, t, c * P:(c + 1) * P],
                                                            turned_sb[:, 0:2, :, :].rearrange("p a b n -> p a (b n)")[:, m, t * BANK:(t + 1) * BANK],
                                                            start=t == 0 and n == 0, stop=t == TILES - 1 and n == 2)
                        last.then_inc(done[kind], 1)
                    if kind == "hidden_layer":
                        (w,) = which
                        pe.wait_ge(done["gathered"], count(b, "gathered", w))
                        if w == 0:
                            pe.wait_ge(w1_loaded, (b + 1) * (KT * 16))
                            pe.wait_ge(done["slot_exp"], (b + 1) * kinds["slot_exp"])
                        for k in range(4):
                            e = 4 * w + k
                            for c in range(KT):
                                last = nc.tensor.matmul(ring[0:H, e * P:(e + 1) * P], w1_sb[:, c, e, :],
                                                        gathered[:, c, e * P:(e + 1) * P], start=c == 0, stop=c == KT - 1)
                        last.then_inc(done[kind], 1)
                    if kind == "output_layer":
                        (w,) = which
                        pe.wait_ge(done["gelu"], (b + 1) * kinds["gelu"])
                        pe.wait_ge(w2_loaded[w % 2], b * 64 + 32 * (w // 2 + 1))
                        if w >= 2:
                            pe.wait_ge(done["slots_lo"], count(b, "slots_lo", w - 2))
                        for k in range(4):
                            e = 4 * w + k
                            at_col = (w % 2) * 2 * BANK + k * D
                            last = nc.tensor.matmul(ring[:, at_col:at_col + D], hidden[0:H + 1, e * P:(e + 1) * P],
                                                    w2_sb[:, w % 2, k, :], start=True, stop=True)
                        last.then_inc(done[kind], 1)
                    if kind == "row_logits":
                        (t,) = which
                        if t:
                            pe.wait_ge(done["row_exp"], count(b, "row_exp", t - 1))
                        else:
                            pe.wait_ge(done["slots_lo"], (b + 1) * kinds["slots_lo"])
                        for q in range(ES // BANK):
                            for n, (c, a, m) in enumerate(passes):
                                last = nc.tensor.matmul(ring[:, q * BANK:(q + 1) * BANK], rowsT[:, a, c, t * P:(t + 1) * P],
                                                        mu[:, m, c, q * BANK:(q + 1) * BANK], start=n == 0, stop=n == len(passes) - 1)
                        last.then_inc(done[kind], 1)
                    if kind == "turn_combine":
                        t, quad, part = which
                        n = at[(kind, *which)]
                        if quad == 0 and part == 0:
                            pe.wait_ge(done["row_split"], count(b, "row_split", t))
                        if n >= 2:
                            pe.wait_ge(done["combine_turned"], b * kinds["combine_turned"] + n - 1)
                        else:
                            pe.wait_ge(done["dispatch_turned"], (b + 1) * kinds["dispatch_turned"])
                        for k in range(4):
                            col = (4 * quad + k) * P
                            last = nc.tensor.transpose(turned[:, part, k * P:(k + 1) * P], parts[:, part, col:col + P], ident_r[:, :])
                        last.then_inc(done[kind], 1)
                    if kind == "spread":
                        (t,) = which
                        pe.wait_ge(done["combine_turned"], count(b, "combine_turned", t, E // 4 - 1, 1))
                        if t >= 2:
                            pe.wait_ge(done["add_rows"], count(b, "add_rows", t - 2))
                        else:
                            pe.wait_ge(done["gathered"], (b + 1) * kinds["gathered"])
                        for e in range(E):
                            for n, (a, m) in enumerate(PARTS):
                                last = nc.tensor.matmul(mix[:, t % 2, 0:D], turned_sb[:, t % 2, a, e * P:(e + 1) * P],
                                                        slots[:, m, e, :], start=e == 0 and n == 0, stop=e == E - 1 and n == 2)
                        last.then_inc(done[kind], 1)

        @block.scalar
        def _(act):
            act.wait_ge(mu_loaded, 16)
            nc.scalar.activation(gathered[:, :, :], exps[:, :, :], ACT.Square).then_inc(squares_ready, 1)
            act.wait_ge(sums_ready, 1)
            nc.scalar.activation(hidden[:, :], ring[:, :], ACT.Sqrt).then_inc(norms_ready, 1)
            for b in range(B):
                for kind, *which in plan:
                    if kind in ("std_1", "std_2", "std_3"):
                        act.wait_ge(done[kind.replace("std", "stats")], b + 1)
                        nc.scalar.activation(std[:, :], spread_sq[:, :], ACT.Sqrt).then_inc(done[kind], 1)
                    if kind == "lengths":
                        act.wait_ge(done["affine"], b + 1)
                        for t in range(TILES):
                            nc.scalar.activation(exps[:, 1, t * D:(t + 1) * D], exps[:, 0, t * D:(t + 1) * D], ACT.Square,
                                                 accum_out=spread_sq[:, t:t + 1]).then_inc(act_step, 1)
                        act.wait_ge(act_step, (b + 1) * TILES)
                        nc.scalar.activation(std[:, :], spread_sq[:, :], ACT.Sqrt).then_inc(done[kind], 1)
                    if kind == "rows_hi":
                        act.wait_ge(done["gather"], b * kinds["gather"])
                        nc.scalar.activation(rows[:, 0].rearrange("p t d -> p (t d)"), exps[:, 0, :], ACT.Copy).then_inc(done[kind], 1)
                    if kind == "rows_turned":
                        part, c = which
                        n = at[(kind, part, c)]
                        act.wait_ge(done["turn_rows"], count(b, "turn_rows", part, c))
                        nc.scalar.activation(rowsT[:, part, c, :], ring[:, (n % 2) * N:(n % 2 + 1) * N], ACT.Copy).then_inc(done[kind], 1)
                    if kind == "slot_exp":
                        (e,) = which
                        act.wait_ge(done["slot_max"], count(b, "slot_max", e))
                        if e >= 2:
                            act.wait_ge(done["slot_split"], count(b, "slot_split", e - 2))
                        if e == 0:
                            act.wait_ge(done["rows_lo"], b + 1)
                            act.wait_ge(done["unit_rows"], b + 1)
                        nc.scalar.activation(exps[:, e % 2, 0:N], ring[:, (e % 2) * N:(e % 2 + 1) * N], ACT.Exp,
                                             bias=neg_max[:, e % 2:e % 2 + 1], accum_out=total[:, e % 2:e % 2 + 1]
                                             ).then_inc(done[kind], 1)
                    if kind == "dispatch_turned":
                        e, half, part = which
                        act.wait_ge(done["turn_dispatch"], count(b, "turn_dispatch", e, half, part))
                        w = e // 4
                        if e % 4 == 0 and half == 0 and part == 0:
                            if w:
                                act.wait_ge(done["gather"], count(b, "gather", w - 1))
                            else:
                                act.wait_ge(done["spread"], b * kinds["spread"])
                        dst = turned_sb[:, part].rearrange("p a n -> p (a n)").rearrange("p (t n) -> p t n", n=BANK)
                        nc.scalar.activation(dst[:, 4 * half:4 * half + 4, (e % 4) * P:(e % 4 + 1) * P],
                                             turned[:, part, :].bitcast(F32).rearrange("p (t n) -> p t n", n=P),
                                             ACT.Copy).then_inc(done[kind], 1)
                    if kind == "gelu":
                        (w,) = which
                        act.wait_ge(done["hidden_layer"], count(b, "hidden_layer", w))
                        if w == 0:
                            act.wait_ge(ones_row_ready, 1)
                            act.wait_ge(consts_loaded, 5 * 16)
                            act.wait_ge(done["output_layer"], b * kinds["output_layer"])
                        for k in range(4):
                            e = 4 * w + k
                            last = nc.scalar.activation(hidden[0:H, e * P:(e + 1) * P], ring[0:H, e * P:(e + 1) * P], ACT.Gelu,
                                                        bias=b1_sb[:, e:e + 1])
                        last.then_inc(done[kind], 1)
                    if kind == "slots_hi":
                        (w,) = which
                        act.wait_ge(done["output_layer"], count(b, "output_layer", w))
                        if w == 0:
                            act.wait_ge(done["spread"], b * kinds["spread"])
                        nc.scalar.activation(slots[:, 0, 4 * w:4 * w + 4, :].rearrange("p e d -> p (e d)"),
                                             ring[:, (w % 2) * 2 * BANK:(w % 2 + 1) * 2 * BANK], ACT.Copy).then_inc(done[kind], 1)
                    if kind == "row_exp":
                        (t,) = which
                        act.wait_ge(done["row_max"], count(b, "row_max", t))
                        if t >= 2:
                            act.wait_ge(done["row_split"], count(b, "row_split", t - 2))
                            act.wait_ge(done["add_rows"], count(b, "add_rows", t - 2))
                        else:
                            act.wait_ge(done["slot_split"], (b + 1) * kinds["slot_split"])
                        nc.scalar.activation(exps[:, t % 2, :], ring[:, :], ACT.Exp, bias=neg_max[:, t % 2:t % 2 + 1],
                                             accum_out=total[:, t % 2:t % 2 + 1]).then_inc(done[kind], 1)
                    if kind == "combine_turned":
                        t, quad, part = which
                        act.wait_ge(done["turn_combine"], count(b, "turn_combine", t, quad, part))
                        if quad == 0 and part == 0:
                            if t >= 2:
                                act.wait_ge(done["spread"], count(b, "spread", t - 2))
                            else:
                                act.wait_ge(done["gather"], (b + 1) * kinds["gather"])
                        nc.scalar.activation(turned_sb[:, t % 2, part, quad * BANK:(quad + 1) * BANK],
                                             turned[:, part, :].bitcast(F32), ACT.Copy).then_inc(done[kind], 1)

        @block.vector
        def _(dve):
            steps = [0]
            per_sequence = 3 * 2 * TILES + 3 + (TILES + 1) + (3 + TILES) + 2 * E + 2 * TILES

            def step(instruction):
                instruction.then_inc(dve_step, 1)
                steps[0] += 1

            def settle(base):
                dve.wait_ge(dve_step, base + steps[0])

            dve.wait_ge(consts_loaded, 5 * 16)
            nc.vector.tensor_copy(ident_r[:, :], ident[:, :]).then_inc(ident_ready, 1)
            nc.vector.memset(ones[:, :], 1.0).then_inc(ones_ready, 1)
            dve.wait_ge(norms_ready, 1)
            step(nc.vector.tensor_scalar(hidden[:, :], hidden[:, :], L2_EPS, None, ALU.max))
            settle(0)
            step(nc.vector.reciprocal(hidden[:, :], hidden[:, :]))
            settle(0)
            for c in range(KT):
                step(nc.vector.tensor_tensor(exps[:, c, :], exps[:, c, :], hidden[:, :], ALU.mult))
            settle(0)
            step(nc.vector.tensor_copy(mu[:, 0], exps[:, :, :]))
            settle(0)
            nc.vector.tensor_tensor(mu[:, 1], exps[:, :, :], mu[:, 0].bitcast(F32), ALU.subtract).then_inc(mu_ready, 1)
            before = steps[0]
            dve.wait_ge(mu_ready, 1)
            nc.vector.memset(hidden[H:H + 1, :], 1.0).then_inc(ones_row_ready, 1)

            for b in range(B):
                steps[0] = 0
                base = b * per_sequence + before
                for kind, *which in plan:
                    if kind in ("stats_1", "stats_2", "stats_3"):
                        if kind == "stats_1":
                            dve.wait_ge(done["norm_3"], b)
                        elif kind == "stats_2":
                            dve.wait_ge(done["norm_1"], b + 1)
                        else:
                            dve.wait_ge(done["add_rows"], (b + 1) * kinds["add_rows"])
                        for t in range(TILES):
                            step(nc.vector.bn_stats(moments[:, t, :], y_rows(b, t, 1)))
                        settle(base)
                        for t in range(TILES):
                            step(nc.vector.bn_aggr(mean_var[:, t, :], moments[:, t, :]))
                        settle(base)
                        nc.vector.tensor_scalar(spread_sq[:, :], mean_var[:, :, 1:2].rearrange("p t a -> p (t a)"), LN_EPS, None, ALU.add
                                                ).then_inc(done[kind], 1)
                    if kind in ("norm_1", "norm_3"):
                        dve.wait_ge(done["std_1" if kind == "norm_1" else "std_3"], b + 1)
                        step(nc.vector.reciprocal(inv_std[:, :], std[:, :]))
                        settle(base)
                        for t in range(TILES):
                            last = nc.vector.tensor_scalar(y_rows(b, t, 1), y_rows(b, t, 1), mean_var[:, t, 0:1], inv_std[:, t:t + 1],
                                                           ALU.subtract, ALU.mult)
                        last.then_inc(done[kind], 1)
                    if kind == "affine":
                        dve.wait_ge(done["std_2"], b + 1)
                        step(nc.vector.reciprocal(inv_std[:, :], std[:, :]))
                        settle(base)
                        for t in range(TILES):
                            step(nc.vector.tensor_scalar(exps[:, 0, t * D:(t + 1) * D], y_rows(b, t, 1), mean_var[:, t, 0:1],
                                                         inv_std[:, t:t + 1], ALU.subtract, ALU.mult))
                        settle(base)
                        x_ln = exps[:, 0, :].rearrange("p (t d) -> p t d", d=D)
                        every = [P, TILES, D]
                        step(nc.vector.tensor_tensor(x_ln, x_ln, gamma[:, :].rearrange("p (a d) -> p a d", a=1).broadcast_to(every), ALU.mult))
                        settle(base)
                        nc.vector.tensor_tensor(x_ln, x_ln, beta[:, :].rearrange("p (a d) -> p a d", a=1).broadcast_to(every), ALU.add
                                                ).then_inc(done[kind], 1)
                    if kind == "unit_rows":
                        dve.wait_ge(done["lengths"], b + 1)
                        step(nc.vector.tensor_scalar(std[:, :], std[:, :], L2_EPS, None, ALU.max))
                        settle(base)
                        step(nc.vector.reciprocal(inv_std[:, :], std[:, :]))
                        settle(base)
                        step(nc.vector.tensor_scalar(inv_std[:, :], inv_std[:, :], scale[:, 0:1], None, ALU.mult))
                        settle(base)
                        dve.wait_ge(done["turn_combine"], b * kinds["turn_combine"])
                        for t in range(TILES):
                            cols = slice(t * D, (t + 1) * D)
                            step(nc.vector.tensor_scalar(parts[:, 0, cols], exps[:, 0, cols], inv_std[:, t:t + 1], None, ALU.mult))
                        settle(base)
                        for t in range(TILES):
                            cols = slice(t * D, (t + 1) * D)
                            last = nc.vector.scalar_tensor_tensor(parts[:, 1, cols], exps[:, 0, cols], inv_std[:, t:t + 1],
                                                                  parts[:, 0, cols].bitcast(F32), ALU.mult, ALU.subtract)
                        last.then_inc(done[kind], 1)
                    if kind == "rows_lo":
                        dve.wait_ge(done["rows_hi"], b + 1)
                        nc.vector.tensor_tensor(rows[:, 1].rearrange("p t d -> p (t d)"), exps[:, 0, :],
                                                rows[:, 0].rearrange("p t d -> p (t d)").bitcast(F32), ALU.subtract).then_inc(done[kind], 1)
                    if kind == "slot_max":
                        (e,) = which
                        dve.wait_ge(done["slot_logits"], count(b, "slot_logits", e))
                        if e >= 2:
                            dve.wait_ge(done["slot_exp"], count(b, "slot_exp", e - 2))
                        nc.vector.tensor_reduce(neg_max[:, e % 2:e % 2 + 1], ring[:, (e % 2) * N:(e % 2 + 1) * N], AX_X, ALU.max,
                                                negate=True).then_inc(done[kind], 1)
                    if kind == "slot_split":
                        (e,) = which
                        dve.wait_ge(done["slot_exp"], count(b, "slot_exp", e))
                        step(nc.vector.reciprocal(inv_total[:, e % 2:e % 2 + 1], total[:, e % 2:e % 2 + 1]))
                        settle(base)
                        if e >= 2:
                            dve.wait_ge(done["turn_dispatch"], count(b, "turn_dispatch", e - 2, TILES // 4 - 1, 1))
                        else:
                            dve.wait_ge(done["turn_rows"], (b + 1) * kinds["turn_rows"])
                        cols = slice((e % 2) * N, (e % 2 + 1) * N)
                        step(nc.vector.tensor_scalar(parts[:, 0, cols], exps[:, e % 2, 0:N], inv_total[:, e % 2:e % 2 + 1], None, ALU.mult))
                        settle(base)
                        nc.vector.scalar_tensor_tensor(parts[:, 1, cols], exps[:, e % 2, 0:N], inv_total[:, e % 2:e % 2 + 1],
                                                       parts[:, 0, cols].bitcast(F32), ALU.mult, ALU.subtract).then_inc(done[kind], 1)
                    if kind == "gathered":
                        (w,) = which
                        dve.wait_ge(done["gather"], count(b, "gather", w))
                        if w == 0:
                            dve.wait_ge(done["hidden_layer"], b * kinds["hidden_layer"])
                        nc.vector.tensor_copy(gathered[:, :, w * BANK:(w + 1) * BANK], mix[:, :, :]).then_inc(done[kind], 1)
                    if kind == "slots_lo":
                        (w,) = which
                        dve.wait_ge(done["slots_hi"], count(b, "slots_hi", w))
                        nc.vector.tensor_tensor(slots[:, 1, 4 * w:4 * w + 4, :].rearrange("p e d -> p (e d)"),
                                                ring[:, (w % 2) * 2 * BANK:(w % 2 + 1) * 2 * BANK],
                                                slots[:, 0, 4 * w:4 * w + 4, :].rearrange("p e d -> p (e d)").bitcast(F32),
                                                ALU.subtract).then_inc(done[kind], 1)
                    if kind == "row_max":
                        (t,) = which
                        dve.wait_ge(done["row_logits"], count(b, "row_logits", t))
                        if t >= 2:
                            dve.wait_ge(done["row_exp"], count(b, "row_exp", t - 2))
                        else:
                            dve.wait_ge(done["slot_exp"], (b + 1) * kinds["slot_exp"])
                        nc.vector.tensor_reduce(neg_max[:, t % 2:t % 2 + 1], ring[:, :], AX_X, ALU.max, negate=True
                                                ).then_inc(done[kind], 1)
                    if kind == "row_split":
                        (t,) = which
                        dve.wait_ge(done["row_exp"], count(b, "row_exp", t))
                        if t:
                            dve.wait_ge(done["turn_combine"], count(b, "turn_combine", t - 1, E // 4 - 1, 1))
                        else:
                            dve.wait_ge(done["turn_dispatch"], (b + 1) * kinds["turn_dispatch"])
                        step(nc.vector.tensor_copy(parts[:, 0, :], exps[:, t % 2, :]))
                        settle(base)
                        nc.vector.tensor_tensor(parts[:, 1, :], exps[:, t % 2, :], parts[:, 0, :].bitcast(F32), ALU.subtract
                                                ).then_inc(done[kind], 1)
                    if kind == "add_rows":
                        (t,) = which
                        step(nc.vector.reciprocal(inv_total[:, t % 2:t % 2 + 1], total[:, t % 2:t % 2 + 1]))
                        settle(base)
                        dve.wait_ge(done["spread"], count(b, "spread", t))
                        nc.vector.scalar_tensor_tensor(y_rows(b, t, 1), mix[:, t % 2, 0:D], inv_total[:, t % 2:t % 2 + 1],
                                                       y_rows(b, t, 1), ALU.mult, ALU.add).then_inc(done[kind], 1)
                assert steps[0] == per_sequence, (steps[0], per_sequence)


_INS = ["L0_attn_x", "L0_attn_Wq", "L0_attn_Wk", "L0_attn_Wv", "L0_attn_Wo", "L0_attn_head_scale", "L0_ffn_gamma",
        "L0_ffn_beta", "L0_ffn_mu", "L0_ffn_scale", "L0_ffn_W1", "L0_ffn_b1", "L0_ffn_W2", "L0_ffn_b2"]
_OUTS = [((2, 1024, 256), "float32")]


def constants(positions, head, base=10000.0):
    powers = (np.arange(0, head, 2, dtype=np.float32) / np.float32(head)).astype(np.float64)
    inv_freq = (1.0 / np.power(base, powers)).astype(np.float32)
    angles = (inv_freq[:, None] * np.arange(positions, dtype=np.float32)[None, :]).astype(np.float64)
    cos, sin = np.cos(angles).astype(np.float32), np.sin(angles).astype(np.float32)
    later = np.arange(P)[None, :] > np.arange(P)[:, None]
    return {"const_cos": np.concatenate([cos, cos]), "const_sin": np.concatenate([-sin, sin]),
            "const_ident": np.eye(P, dtype=np.float32),
            "const_hidden": np.where(later, np.float32(HIDDEN), np.float32(0.0))}


def program(nc, x, wq, wk, wv, wo, head_scale, gamma, beta, mu, scale, w1, b1, w2, b2, cos, sin, ident, hidden, out):
    B, N, D = x.shape
    with nc.sbuf_tensor("y_sb", [P, B * N // P, D], F32) as y_sb:
        attention(nc, y_sb, x, wq, wk, wv, wo, head_scale, cos, sin, ident, hidden)
        soft_experts(nc, y_sb, gamma, beta, mu, scale, w1, b1, w2, b2, ident, out)


def kernel(**inputs):
    import numpy as _np
    import concourse.bacc as _bacc
    from concourse import mybir as _mybir
    from concourse.bass_utils import run_bass_kernel_spmd as _run

    nc = _bacc.Bacc("TRN2", target_bir_lowering=False, num_devices=1)
    arrays, args = {}, []
    for name in _INS:
        a = _np.ascontiguousarray(inputs[name])
        arrays[f"in_{name}_dram"] = a
        args.append(nc.dram_tensor(f"in_{name}_dram", a.shape, _mybir.dt.from_np(a.dtype), kind="ExternalInput").ap())
    for name, a in constants(1024, 128).items():
        arrays[f"{name}_dram"] = a
        args.append(nc.dram_tensor(f"{name}_dram", a.shape, _mybir.dt.from_np(a.dtype), kind="ExternalInput").ap())
    for i, (shape, dtype) in enumerate(_OUTS):
        dt = _mybir.dt.from_np(_np.dtype(dtype))
        args.append(nc.dram_tensor(f"out_{i}_dram", shape, dt, kind="ExternalOutput").ap())
    program(nc, *args)
    r = _run(nc, [arrays], core_ids=[0])
    got = tuple(r.results[0][f"out_{i}_dram"] for i in range(len(_OUTS)))
    return got[0]
```

```python
from collections import Counter
from contextlib import ExitStack

import concourse.bass as bass
import numpy as np
from concourse import mybir

F32 = mybir.dt.float32
F32R = mybir.dt.float32r
BF16 = mybir.dt.bfloat16
ALU = mybir.AluOpType
ACT = mybir.ActivationFunctionType
AX_X = mybir.AxisListType.X

P = 128
BANK = 512
LN_EPS = 1e-5
L2_EPS = 1e-12
HIDDEN = -(2.0 ** 120)
START = 64
PARTS = ((0, 0), (0, 1), (1, 0))


def plan_heads(part, heads, tiles):
    plan, deferred, later = [], [], []

    def settle():
        plan.extend(deferred)
        deferred[:] = later
        later.clear()

    def rope(who, n):
        plan.append(("project", who, n))
        deferred.extend([("take", who, n), ("swap", who, n)])
        later.extend([(kind, who, n) for kind in ("times_cos", "times_sin", "rope_add")])

    def split_rope(who, n):
        plan.extend([("rope_hi", who, n), ("rope_lo", who, n)])

    def weights(who, n):
        if who == "q":
            plan.extend([(f"load_q{n % 2}", who, n), ("scale_weights", who, n)])
        else:
            plan.append((f"load_{who}", who, n))
        plan.extend([("weights_hi", who, n), ("weights_lo", who, n)])

    def out_weights(pair):
        plan.extend([(kind, pair) for kind in ("load_o", "scale_out", "out_hi", "out_lo")])

    def top(h, i):
        plan.extend([("scores", h, i), ("max", h, i)])
        deferred.append(("sum_exp", h, i))

    def to_columns(h, w):
        plan.extend([(kind, h, w) for kind in ("invert", "columns_hi", "columns_lo")])

    def to_rows(h, w):
        plan.extend([(kind, h, w) for kind in ("turn_columns", "rows_copied")])

    def widen(h, w):
        plan.append(("widen", h, w))
        deferred.append(("widened", h, w))

    def tile(h, w, j):
        plan.extend([(kind, h, w, j) for kind in ("key_scores", "exp", "exp_hi", "exp_lo")])
        settle()

    def weigh(h, w, j):
        plan.append(("weigh", h, w, j))
        if j == 4 * w + 3:
            plan.append(("mixed", h, w))
            deferred.extend([("mixed_hi", h, w), ("mixed_lo", h, w)])

    def output(pair, w):
        plan.extend([("output", pair, w), ("add_output", pair, w)])

    if part == "first":
        for who, n in (("v", 0), ("k", 0), ("q", 0), ("q", 1)):
            weights(who, n)
        plan.extend([(kind, "x", 0, c) for c in range(2) for kind in ("turn_x", "xT_hi", "xT_lo")])
        plan.extend([(kind, "v", 0) for kind in ("project", "take", "turn_v", "v_hi", "v_lo")])
        for who in ("k", "q"):
            rope(who, 0)
            settle()
            settle()
            split_rope(who, 0)
        plan.extend([(kind, "x", 1, c) for c in range(2) for kind in ("turn_x", "xT_hi", "xT_lo")])
        for i in (3, 2, 1, 0, 7, 6, 5, 4):
            top(0, i)
            settle()
            if i == 0:
                rope("q", 1)
            if i == 6:
                to_columns(0, 0)
                to_rows(0, 0)
        split_rope("q", 1)
        return plan

    more = part == "body"
    tops = {1: (3,), 2: (7,), 3: (6,), 4: (2,), 6: (5,), 7: (1,), 8: (0,), 9: (4,)}
    for h in range(heads):
        following = more or h + 1 < heads
        ahead = more or h + 2 < heads
        group_ahead = more or h < 4
        if ahead:
            weights("q", h + 2)
        if h % 4 in (0, 2) and group_ahead:
            weights("kv"[h % 4 // 2], h // 4 + 1)
        if h == 0:
            out_weights(0)
        steps = [(0, j) for j in range(4)] + [(1, j) for j in range(8)]
        for n, step in enumerate(steps):
            tile(h, *step)
            if n >= 2:
                weigh(h, *steps[n - 2])
            if n == 0:
                to_columns(h, 1)
            if n == 9 and following:
                to_columns(h + 1, 0)
            if n == 5 and group_ahead and h % 4 == 2:
                split_rope("k", h // 4 + 1)
            if n == 10 and ahead:
                split_rope("q", h + 2)
            if n == 0 and group_ahead and h % 4 == 3:
                plan.extend([(kind, "v", h // 4 + 1) for kind in ("turn_v", "v_hi", "v_lo")])
            if n == 8:
                if h % 2:
                    output(h // 2, 0)
                elif h:
                    output(h // 2 - 1, 1)
                    out_weights(h // 2)
            if following and (h, n) != (heads - 1, 9):
                for i in tops.get(n, ()):
                    top(h + 1, i)
            if n == 2:
                to_rows(h, 1)
                widen(h, 0)
            if n == 5 and ahead:
                rope("q", h + 2)
            if n == 6:
                widen(h, 1)
            if n == 11 and following:
                to_rows(h + 1, 0)
            if n == 10 and group_ahead and h % 4 == 1:
                rope("k", h // 4 + 1)
            if n == 10 and group_ahead and h % 4 == 2:
                plan.append(("project", "v", h // 4 + 1))
                deferred.append(("take", "v", h // 4 + 1))
        weigh(h, *steps[-2])
        weigh(h, *steps[-1])
    if more:
        top(heads, 4)
    deferred.reverse()
    settle()
    settle()
    output(heads // 2 - 1, 1)
    return plan


def attention(nc, y_sb, slot_vectors, mu_loaded, mu_d, x_d, wq_d, wk_d, wv_d, wo_d, head_scale_d, cos_d, sin_d, ident_d, hidden_d):
    B, N, D = x_d.shape
    DH = P
    HEADS = wq_d.shape[1] // DH
    GROUPS = wk_d.shape[1] // DH
    TILES = N // P
    KT = D // P
    SCALE = DH ** -0.5
    TURN_GROUPS = 2
    TURN_HEADS = TURN_GROUPS * HEADS // GROUPS
    TURNS = B * GROUPS // TURN_GROUPS
    first, body, last_turn = [plan_heads(part, TURN_HEADS, TILES) for part in ("first", "body", "last")]

    def number(plan):
        seen, at = Counter(), {}
        for item in plan:
            at[item] = seen[item[0]]
            seen[item[0]] += 1
        return at, seen

    at_first, in_first = number(first)
    at_body, in_body = number(body)
    at_last, _ = number(last_turn)
    kinds = list(dict.fromkeys(item[0] for item in first + body))
    FILLS = ("turn_x", "project", "turn_v", "scores", "output")
    SMALL_FILLS = ("key_scores", "turn_columns", "widen")
    SMALLS = 3
    HELD = 3
    QUERIES = 4

    def past(it, kind):
        return START if it is None else START + in_first[kind] + it * in_body[kind]

    def count(it, kind, *which):
        at = at_first if it is None else at_last if isinstance(it, int) else at_body
        if (kind, *which) in at:
            return past(it, kind) + at[(kind, *which)] + 1
        if it is None:
            return None
        if which[0] in ("k", "v"):
            item = (kind, which[0], which[1] + TURN_GROUPS, *which[2:])
        elif which[0] == "q":
            item = (kind, "q", which[1] + TURN_HEADS)
        elif "out" in kind:
            item = (kind, which[0] + TURN_HEADS // 2, *which[1:])
        else:
            item = (kind, which[0] + TURN_HEADS, *which[1:])
        return past(it, kind) - in_body[kind] + at_body[item] + 1

    with ExitStack() as ctx:
        def sb(name, shape, dt=F32):
            return ctx.enter_context(nc.sbuf_tensor(name, shape, dt))

        def psum(name, shape, dt=F32):
            return ctx.enter_context(nc.psum_tensor(name, shape, dt))

        def sem(name):
            return ctx.enter_context(nc.semaphore(name))

        xT = sb("xT", [P, 2, B * KT, N], F32R)
        qT = sb("qT", [P, QUERIES, 2, N], F32R)
        kT = sb("kT", [P, 2, 2, N], F32R)
        taken = sb("taken", [P, N])
        v_sb = sb("v_sb", [P, 2, 2, N], F32R)
        exps = sb("exps", [P, 2, BANK])
        exp_parts = sb("exp_parts", [P, HELD, 2, BANK], F32R)
        mix_sb = sb("mix_sb", [P, BANK])
        inv_wide = sb("inv_wide", [P, BANK])
        mixed = sb("mixed", [P, 2, 2, N], F32R)
        cos_sb = sb("cos_sb", [P, N])
        sin_sb = sb("sin_sb", [P, N])
        rotated = sb("rotated", [P, N])
        cos_part = sb("cos_part", [P, N])
        raw_kv, raw_o = sb("raw_kv", [P, KT, DH]), sb("raw_o", [P, 2, D])
        raw_q = [sb(f"raw_q{i}", [P, KT, DH]) for i in range(2)]
        wkv_sb = sb("wkv_sb", [P, 2, KT, DH], F32R)
        wq_sb = sb("wq_sb", [P, 2, 2, KT, DH], F32R)
        wo_sb = sb("wo_sb", [P, 2, 2, D], F32R)
        ident = sb("ident", [P, P])
        ident_r = sb("ident_r", [P, P], F32R)
        ident_b = sb("ident_b", [P, P], BF16)
        hidden = sb("hidden", [P, P])
        hidden_b = sb("hidden_b", [P, P], BF16)
        head_scale = sb("head_scale", [P, HEADS])
        unit = sb("unit", [P, 2])
        pick_max = sb("pick_max", [4, P], F32R)
        pick_inv = sb("pick_inv", [4, P], F32R)
        neg_max = sb("neg_max", [P, 2, TILES])
        row_sum = sb("row_sum", [P, 2, TILES])
        inv_sum = sb("inv_sum", [P, 2, 4])
        columns = sb("columns", [P, 2, 4, 4], F32R)
        rows = sb("rows4", [4, 2, BANK], F32R)
        ring = psum("ring", [P, 2, 2 * BANK])
        small = psum("small", [P, SMALLS, BANK])
        mix = psum("mix", [P, BANK])

        done = {kind: sem(f"{kind}_done") for kind in kinds}
        consts_loaded, tables_loaded, consts_ready, unit_ready = (
            sem("consts_loaded"), sem("tables_loaded"), sem("consts_ready"), sem("unit_ready"))
        x_loaded = [sem(f"x{b}_loaded") for b in range(B)]

        def loaded(it, kind, *which):
            return (count(it, kind, *which) - START) * (32 if kind == "swap" else 16)

        def start_counts(engine, *own):
            for kind in own:
                engine.sem_inc(done[kind], START)

        def wait_stage(engine, it, kind, *which):
            value = count(it, kind, *which)
            if value is not None:
                engine.wait_ge(done[kind], value)

        def before(plan, item, kind):
            return len([1 for other in plan[:plan.index(item)] if other[0] == kind])

        def wait_before(engine, it, kind, plan, item):
            engine.wait_ge(done[kind], past(it, kind) + before(plan, item, kind))

        def turns(engine, stages):
            stages(None, first)
            with engine.Fori(0, TURNS - 1) as it:
                stages(it, body)
            stages(TURNS - 1, last_turn)

        def sequence(it, who, n):
            if it is None:
                return 0
            per_turn, every = (TURN_HEADS, HEADS) if who == "q" else (TURN_GROUPS, GROUPS)
            return (it * per_turn + n) // every

        def in_sequence(it, who, n):
            if it is None:
                return n
            per_turn, every = (TURN_HEADS, HEADS) if who == "q" else (TURN_GROUPS, GROUPS)
            return (it * per_turn + n) % every

        def wait_last_kv(engine, it, kind, who, n):
            if it is None:
                if who == "k":
                    wait_stage(engine, it, kind, "v", 0)
            else:
                wait_stage(engine, it, kind, *(("v", n - 1) if who == "k" else ("k", n)))

        def slot(plan, item):
            return len([1 for other in plan[:plan.index(item)] if other[0] in FILLS]) % 2

        def small_slot(plan, item):
            return len([1 for other in plan[:plan.index(item)] if other[0] in SMALL_FILLS]) % SMALLS

        def column(one, like):
            return one.rearrange("p (a b) -> p a b", b=1).broadcast_to(list(like.shape))

        def seen(w, j):
            return slice((max(4 * w, j) - 4 * w) * P, BANK)

        x_rows = x_d.rearrange("b (t p) d -> b p t d", p=P)
        wq_cols = wq_d.rearrange("(t c) n -> c t n", c=P)
        wk_cols = wk_d.rearrange("(t c) n -> c t n", c=P)
        wv_cols = wv_d.rearrange("(t c) n -> c t n", c=P)
        wo_rows = wo_d.rearrange("(h d) n -> d h n", d=DH)
        block = ctx.enter_context(nc.Block())

        @block.sync
        def _(sp):
            sp.dma_start(y_sb[:, 0:TILES, :], x_rows[0]).then_inc(x_loaded[0], 16)
            sp.dma_start(ident[:, :], ident_d).then_inc(consts_loaded, 16)
            sp.dma_start(hidden[:, :], hidden_d).then_inc(consts_loaded, 16)

            def stages(it, plan):
                def starts(who, unit):
                    per_turn = TURN_HEADS if who == "q" else TURN_GROUPS
                    if it is None:
                        return (0,)
                    values = [in_sequence(it, who, n) * unit for n in (0, per_turn)]
                    return values if isinstance(it, int) else [sp.snap(value) for value in values]

                columns_at = {who: starts(who, DH) for who in ("q", "k")}
                rows_at = starts("q", 1)

                def columns(who, n):
                    per_turn = TURN_HEADS if who == "q" else TURN_GROUPS
                    return bass.ds(columns_at["q" if who == "q" else "k"][n // per_turn] + n % per_turn * DH, DH)

                for item in plan:
                    kind, *which = item
                    if kind in ("load_k", "load_v"):
                        who, n = which
                        source = (wk_cols if who == "k" else wv_cols)[:, :, columns(who, n)]
                        wait_last_kv(sp, it, "weights_lo", who, n)
                        sp.dma_start(raw_kv[:, :, :], source).then_inc(done[kind], 16)
                    if kind in ("load_q0", "load_q1"):
                        _, n = which
                        source = wq_cols[:, :, columns("q", n)]
                        wait_stage(sp, it, "weights_lo", "q", n - 2)
                        sp.dma_start(raw_q[n % 2][:, :, :], source).then_inc(done[kind], 16)
                    if kind == "swap":
                        sp.wait_ge(done["take"], count(it, "take", *which))
                        sp.dma_start(rotated[0:64, :], taken[64:128, :]).then_inc(done[kind], 16)
                        sp.dma_start(rotated[64:128, :], taken[0:64, :]).then_inc(done[kind], 16)
                    if kind == "load_o":
                        (pair,) = which
                        source = wo_rows[:, bass.ds(rows_at[0] + 2 * pair, 2), :]
                        wait_stage(sp, it, "out_lo", pair - 1)
                        sp.dma_start(raw_o[:, :, :], source).then_inc(done[kind], 16)

            stages(None, first)
            sp.dma_start(slot_vectors[:, :, :], mu_d.rearrange("(c p) e s -> p c (e s)", p=P)).then_inc(mu_loaded, 16)
            with sp.Fori(0, TURNS - 1) as it:
                stages(it, body)
            stages(TURNS - 1, last_turn)

        @block.tensor
        def _(pe):
            start_counts(pe, "turn_x", "project", "scores", "turn_v", "turn_columns", "widen", "key_scores", "weigh", "output")
            pe.wait_ge(consts_ready, 5)

            def stages(it, plan):
                entries = [item for item in plan if item[0] in FILLS]
                tiles = [item[1:] for item in plan if item[0] == "exp"]
                small_entries = [item for item in plan if item[0] in SMALL_FILLS]

                def wait_reader(kind, which):
                    reader = {"turn_x": "xT_lo", "project": "take", "turn_v": "v_lo", "scores": "sum_exp", "output": "add_output",
                              "key_scores": "exp", "turn_columns": "rows_copied", "widen": "widened"}[kind]
                    wait_stage(pe, it, reader, *which)

                def free_ring(item):
                    e = entries.index(item)
                    if e >= 2:
                        wait_reader(entries[e - 2][0], entries[e - 2][1:])
                    elif it is not None:
                        pe.wait_ge(done["sum_exp"], past(it, "sum_exp"))
                        pe.wait_ge(done["add_output"], past(it, "add_output"))

                def free_small(item):
                    e = small_entries.index(item)
                    if e >= SMALLS:
                        wait_reader(small_entries[e - SMALLS][0], small_entries[e - SMALLS][1:])
                    elif it is not None:
                        for reader in ("exp", "rows_copied", "widened"):
                            pe.wait_ge(done[reader], past(it, reader))

                for item in plan:
                    kind, *which = item
                    if kind == "turn_x":
                        _, b, c = which
                        pe.wait_ge(x_loaded[b], 16)
                        free_ring(item)
                        for t in range(TILES):
                            last = nc.tensor.transpose(ring[:, slot(plan, item), t * P:(t + 1) * P],
                                                       y_sb[:, b * TILES + t, c * P:(c + 1) * P], ident[:, :])
                        last.then_inc(done[kind], 1)
                    if kind == "project":
                        who, n = which
                        w = wq_sb[:, n % 2, :, :, :] if who == "q" else wkv_sb[:, :, :, :]
                        pe.wait_ge(done["weights_lo"], count(it, "weights_lo", who, n))
                        if it is None:
                            pe.wait_ge(done["xT_lo"], count(it, "xT_lo", "x", 0, KT - 1))
                        free_ring(item)
                        passes = [(c, a, m) for c in range(KT) for a, m in PARTS]
                        for half in range(N // BANK):
                            cols = slice(half * BANK, (half + 1) * BANK)
                            for k, (c, a, m) in enumerate(passes):
                                moving = xT[:, m, bass.ds(sequence(it, who, n) * KT + c, 1), cols].rearrange("p a n -> p (a n)")
                                last = nc.tensor.matmul(ring[:, slot(plan, item), cols], w[:, a, c, :], moving,
                                                        start=k == 0, stop=k == len(passes) - 1)
                        last.then_inc(done[kind], 1)
                    if kind == "scores":
                        h, i = which
                        if i == 3:
                            wait_stage(pe, it, "rope_lo", "q", h)
                        free_ring(item)
                        width = (i + 1) * P
                        q = qT[:, h % QUERIES, :, i * P:(i + 1) * P]
                        for lo in range(0, width, BANK):
                            hi = min(width, lo + BANK)
                            diagonal = hi == width
                            for k, (a, m) in enumerate(PARTS):
                                last = nc.tensor.matmul(ring[:, slot(plan, item), lo:hi], q[:, a, :], kT[:, h // 4 % 2, m, lo:hi],
                                                        start=k == 0, stop=k == 2 and not diagonal)
                            if diagonal:
                                last = nc.tensor.matmul(ring[:, slot(plan, item), width - P:width], ident_b[:, :], hidden_b[:, :],
                                                        start=False, stop=True)
                        last.then_inc(done[kind], 1)
                    if kind == "turn_v":
                        pe.wait_ge(done["take"], count(it, "take", *which))
                        free_ring(item)
                        for t in range(TILES):
                            last = nc.tensor.transpose(ring[:, slot(plan, item), t * P:(t + 1) * P], taken[:, t * P:(t + 1) * P], ident[:, :])
                        last.then_inc(done[kind], 1)
                    if kind == "turn_columns":
                        h, w = which
                        pe.wait_ge(done["columns_lo"], count(it, "columns_lo", h, w))
                        free_small(item)
                        for t in range(4):
                            last = nc.tensor.matmul(small[0:4, small_slot(plan, item), t * P:(t + 1) * P], columns[:, w, t, :],
                                                    ident_r[:, :], start=True, stop=True)
                        last.then_inc(done[kind], 1)
                    if kind == "widen":
                        h, w = which
                        pe.wait_ge(done["rows_copied"], count(it, "rows_copied", h, w))
                        free_small(item)
                        nc.tensor.matmul(small[:, small_slot(plan, item), :], pick_inv[:, :], rows[:, w, :], start=True, stop=True
                                         ).then_inc(done[kind], 1)
                    if kind == "key_scores":
                        h, w, j = which
                        if j == 0:
                            pe.wait_ge(done["rows_copied"], count(it, "rows_copied", h, w))
                        free_small(item)
                        bank = small[:, small_slot(plan, item), :]
                        cols = seen(w, j)
                        queries = slice(max(4 * w, j) * P, (4 * w + 4) * P)
                        for k, (a, m) in enumerate(PARTS):
                            nc.tensor.matmul(bank[:, cols], kT[:, h // 4 % 2, a, j * P:(j + 1) * P], qT[:, h % QUERIES, m, queries],
                                             start=k == 0, stop=False)
                        last = nc.tensor.matmul(bank[:, cols], pick_max[:, :], rows[:, w, cols], start=False, stop=j < 4 * w)
                        if j >= 4 * w:
                            last = nc.tensor.matmul(bank[:, cols.start:cols.start + P], hidden_b[:, :], ident_b[:, :],
                                                    start=False, stop=True)
                        last.then_inc(done[kind], 1)
                    if kind == "weigh":
                        h, w, j = which
                        pe.wait_ge(done["exp_lo"], count(it, "exp_lo", h, w, j))
                        if j == 0:
                            wait_stage(pe, it, "mixed", *((h, 0) if w else (h - 1, 1)))
                            wait_stage(pe, it, "v_lo", "v", h // 4)
                        for k, (a, m) in enumerate(PARTS):
                            last = nc.tensor.matmul(mix[:, seen(w, j)], v_sb[:, h // 4 % 2, a, j * P:(j + 1) * P],
                                                    exp_parts[:, tiles.index((h, w, j)) % HELD, m, seen(w, j)],
                                                    start=j == 0 and k == 0, stop=j == 4 * w + 3 and k == 2)
                        last.then_inc(done[kind], 1)
                    if kind == "output":
                        pair, w = which
                        pe.wait_ge(done["mixed_hi"], count(it, "mixed_hi", 2 * pair + 1, w))
                        pe.wait_ge(done["mixed_lo"], count(it, "mixed_lo", 2 * pair + 1, w))
                        pe.wait_ge(done["out_lo"], count(it, "out_lo", pair))
                        free_ring(item)
                        passes = [(hh, a, m) for hh in range(2) for a, m in PARTS]
                        for t in range(4):
                            for k, (hh, a, m) in enumerate(passes):
                                last = nc.tensor.matmul(ring[:, slot(plan, item), t * D:(t + 1) * D],
                                                        mixed[:, hh, a, (4 * w + t) * P:(4 * w + t + 1) * P],
                                                        wo_sb[:, m, hh, :], start=k == 0, stop=k == len(passes) - 1)
                        last.then_inc(done[kind], 1)

            turns(pe, stages)

        @block.scalar
        def _(act):
            act.dma_start(cos_sb[:, :], cos_d).then_inc(tables_loaded, 16)
            act.dma_start(sin_sb[:, :], sin_d).then_inc(tables_loaded, 16)
            act.dma_start(head_scale[:, :], head_scale_d.rearrange("a h b c -> (a b c) h").broadcast_to([P, HEADS])).then_inc(tables_loaded, 16)
            act.dma_start(y_sb[:, TILES:2 * TILES, :], x_rows[1]).then_inc(x_loaded[1], 16)
            start_counts(act, "xT_hi", "take", "rope_hi", "v_hi", "sum_exp", "exp", "exp_hi", "widened", "mixed_hi")

            def stages(it, plan):
                tiles = [item[1:] for item in plan if item[0] == "exp"]
                for item in plan:
                    kind, *which = item
                    if kind == "xT_hi":
                        _, b, c = which
                        act.wait_ge(done["turn_x"], count(it, "turn_x", *which))
                        nc.scalar.activation(xT[:, 0, b * KT + c, :], ring[:, slot(plan, ("turn_x", *which)), :], ACT.Copy
                                             ).then_inc(done[kind], 1)
                    if kind == "take":
                        who, n = which
                        act.wait_ge(done["project"], count(it, "project", *which))
                        wait_before(act, it, "rope_add", plan, item)
                        wait_before(act, it, "turn_v", plan, item)
                        nc.scalar.activation(taken[:, :], ring[:, slot(plan, ("project", *which)), :], ACT.Copy).then_inc(done[kind], 1)
                    if kind == "v_hi":
                        _, g = which
                        act.wait_ge(done["turn_v"], count(it, "turn_v", *which))
                        wait_stage(act, it, "weigh", 4 * g - 5, 1, 7)
                        nc.scalar.activation(v_sb[:, g % 2, 0, :], ring[:, slot(plan, ("turn_v", *which)), :], ACT.Copy
                                             ).then_inc(done[kind], 1)
                    if kind == "rope_hi":
                        who, n = which
                        dst = kT[:, n % 2] if who == "k" else qT[:, n % QUERIES]
                        act.wait_ge(done["rope_add"], count(it, "rope_add", who, n))
                        wait_stage(act, it, "key_scores", 4 * n - 5 if who == "k" else n - QUERIES, 1, 7)
                        nc.scalar.activation(dst[:, 0, :], cos_part[:, :], ACT.Copy).then_inc(done[kind], 1)
                    if kind == "sum_exp":
                        h, i = which
                        act.wait_ge(done["max"], count(it, "max", h, i))
                        if i % 4 == 3:
                            wait_stage(act, it, "invert", h - 2, i // 4)
                        tile = ring[:, slot(plan, ("scores", h, i)), 0:(i + 1) * P]
                        nc.scalar.activation(tile, tile, ACT.Exp,
                                             bias=neg_max[:, h % 2, i:i + 1], accum_out=row_sum[:, h % 2, i:i + 1]
                                             ).then_inc(done[kind], 1)
                    if kind == "exp":
                        h, w, j = which
                        n = tiles.index((h, w, j))
                        act.wait_ge(done["key_scores"], count(it, "key_scores", h, w, j))
                        if n >= 2:
                            act.wait_ge(done["exp_lo"], count(it, "exp_lo", *tiles[n - 2]))
                        else:
                            act.wait_ge(done["exp_lo"], past(it, "exp_lo"))
                        nc.scalar.activation(exps[:, n % 2, seen(w, j)], small[:, small_slot(plan, ("key_scores", h, w, j)), seen(w, j)],
                                             ACT.Exp).then_inc(done[kind], 1)
                    if kind == "exp_hi":
                        h, w, j = which
                        n = tiles.index((h, w, j))
                        act.wait_ge(done["exp"], count(it, "exp", h, w, j))
                        if n >= HELD:
                            act.wait_ge(done["weigh"], count(it, "weigh", *tiles[n - HELD]))
                        else:
                            act.wait_ge(done["weigh"], past(it, "weigh"))
                        nc.scalar.activation(exp_parts[:, n % HELD, 0, seen(w, j)], exps[:, n % 2, seen(w, j)], ACT.Copy
                                             ).then_inc(done[kind], 1)
                    if kind == "widened":
                        h, w = which
                        act.wait_ge(done["widen"], count(it, "widen", h, w))
                        wait_stage(act, it, "mixed", *((h, 0) if w else (h - 1, 1)))
                        nc.scalar.activation(inv_wide[:, :], small[:, small_slot(plan, ("widen", h, w)), :], ACT.Copy
                                             ).then_inc(done[kind], 1)
                    if kind == "mixed_hi":
                        h, w = which
                        act.wait_ge(done["mixed"], count(it, "mixed", h, w))
                        wait_stage(act, it, "output", h // 2 - 1, w)
                        nc.scalar.activation(mixed[:, h % 2, 0, w * BANK:(w + 1) * BANK], mix_sb[:, :], ACT.Copy).then_inc(done[kind], 1)

            turns(act, stages)

        @block.vector
        def _(dve):
            start_counts(dve, "xT_lo", "v_lo", "max", "invert", "columns_hi", "columns_lo", "rows_copied", "exp_lo", "mixed",
                         "times_cos", "rope_lo", "mixed_lo", "add_output")
            dve.wait_ge(consts_loaded, 2 * 16)
            nc.vector.tensor_copy(ident_r[:, :], ident[:, :]).then_inc(consts_ready, 1)
            nc.vector.tensor_copy(ident_b[:, :], ident[:, :]).then_inc(consts_ready, 1)
            nc.vector.tensor_copy(hidden_b[:, :], hidden[:, :]).then_inc(consts_ready, 1)
            for picked, row in ((pick_max, 0), (pick_inv, 2)):
                nc.vector.tensor_tensor(picked[:, :], ident[0:4, row:row + 1].broadcast_to([4, P]),
                                        ident[0:4, row + 1:row + 2].broadcast_to([4, P]), ALU.add).then_inc(consts_ready, 1)

            def stages(it, plan):
                tiles = [item[1:] for item in plan if item[0] == "exp"]
                for item in plan:
                    kind, *which = item
                    if kind == "xT_lo":
                        _, b, c = which
                        dve.wait_ge(done["xT_hi"], count(it, "xT_hi", *which))
                        nc.vector.tensor_tensor(xT[:, 1, b * KT + c, :], ring[:, slot(plan, ("turn_x", *which)), :],
                                                xT[:, 0, b * KT + c, :].bitcast(F32), ALU.subtract).then_inc(done[kind], 1)
                    if kind == "v_lo":
                        _, g = which
                        dve.wait_ge(done["v_hi"], count(it, "v_hi", *which))
                        nc.vector.tensor_tensor(v_sb[:, g % 2, 1, :], ring[:, slot(plan, ("turn_v", *which)), :],
                                                v_sb[:, g % 2, 0, :].bitcast(F32), ALU.subtract).then_inc(done[kind], 1)
                    if kind == "max":
                        h, i = which
                        dve.wait_ge(done["scores"], count(it, "scores", h, i))
                        nc.vector.tensor_reduce(neg_max[:, h % 2, i:i + 1], ring[:, slot(plan, ("scores", h, i)), 0:(i + 1) * P],
                                                AX_X, ALU.max, negate=True).then_inc(done[kind], 1)
                    if kind == "invert":
                        h, w = which
                        dve.wait_ge(done["sum_exp"], count(it, "sum_exp", h, 4 * w))
                        nc.vector.reciprocal(inv_sum[:, w, :], row_sum[:, h % 2, 4 * w:4 * w + 4]).then_inc(done[kind], 1)
                    if kind in ("columns_hi", "columns_lo"):
                        h, w = which
                        values = (neg_max[:, h % 2, 4 * w:4 * w + 4], inv_sum[:, w, :])
                    if kind == "columns_hi":
                        dve.wait_ge(done["invert"], count(it, "invert", h, w))
                        wait_stage(dve, it, "turn_columns", h - 1, w)
                        for k, value in enumerate(values):
                            last = nc.vector.tensor_copy(columns[:, w, :, 2 * k:2 * k + 1], value.rearrange("p (t a) -> p t a", a=1))
                        last.then_inc(done[kind], 1)
                    if kind == "columns_lo":
                        dve.wait_ge(done["columns_hi"], count(it, "columns_hi", h, w))
                        for k, value in enumerate(values):
                            last = nc.vector.tensor_tensor(columns[:, w, :, 2 * k + 1:2 * k + 2], value.rearrange("p (t a) -> p t a", a=1),
                                                           columns[:, w, :, 2 * k:2 * k + 1].bitcast(F32), ALU.subtract)
                        last.then_inc(done[kind], 1)
                    if kind == "rows_copied":
                        h, w = which
                        dve.wait_ge(done["turn_columns"], count(it, "turn_columns", h, w))
                        nc.vector.tensor_copy(rows[:, w, :], small[0:4, small_slot(plan, ("turn_columns", h, w)), :]
                                              ).then_inc(done[kind], 1)
                    if kind == "exp_lo":
                        h, w, j = which
                        n = tiles.index((h, w, j))
                        dve.wait_ge(done["exp_hi"], count(it, "exp_hi", h, w, j))
                        nc.vector.tensor_tensor(exp_parts[:, n % HELD, 1, seen(w, j)], exps[:, n % 2, seen(w, j)],
                                                exp_parts[:, n % HELD, 0, seen(w, j)].bitcast(F32), ALU.subtract).then_inc(done[kind], 1)
                    if kind == "mixed":
                        h, w = which
                        dve.wait_ge(done["weigh"], count(it, "weigh", h, w, 4 * w + 3))
                        dve.wait_ge(done["widened"], count(it, "widened", h, w))
                        wait_before(dve, it, "mixed_lo", plan, item)
                        nc.vector.tensor_tensor(mix_sb[:, :], mix[:, :], inv_wide[:, :], ALU.mult).then_inc(done[kind], 1)
                    if kind == "times_cos":
                        dve.wait_ge(done["take"], count(it, "take", *which))
                        if it is None:
                            dve.wait_ge(tables_loaded, 3 * 16)
                        wait_before(dve, it, "rope_lo", plan, item)
                        nc.vector.tensor_tensor(cos_part[:, :], taken[:, :], cos_sb[:, :], ALU.mult).then_inc(done[kind], 1)
                    if kind == "rope_lo":
                        who, n = which
                        dst = kT[:, n % 2] if who == "k" else qT[:, n % QUERIES]
                        dve.wait_ge(done["rope_hi"], count(it, "rope_hi", who, n))
                        nc.vector.tensor_tensor(dst[:, 1, :], cos_part[:, :], dst[:, 0, :].bitcast(F32), ALU.subtract
                                                ).then_inc(done[kind], 1)

                    if kind == "mixed_lo":
                        h, w = which
                        cols = slice(w * BANK, (w + 1) * BANK)
                        dve.wait_ge(done["mixed_hi"], count(it, "mixed_hi", h, w))
                        nc.vector.tensor_tensor(mixed[:, h % 2, 1, cols], mix_sb[:, :], mixed[:, h % 2, 0, cols].bitcast(F32), ALU.subtract
                                                ).then_inc(done[kind], 1)
                    if kind == "add_output":
                        pair, w = which
                        dve.wait_ge(done["output"], count(it, "output", pair, w))
                        wait_before(dve, it, "add_output", plan, item)
                        y_rows = y_sb[:, bass.ds(sequence(it, "q", 0) * TILES + 4 * w, 4), :].rearrange("p t d -> p (t d)")
                        nc.vector.tensor_tensor(y_rows, ring[:, slot(plan, ("output", pair, w)), :], y_rows, ALU.add).then_inc(done[kind], 1)

            turns(dve, stages)

        @block.gpsimd
        def _(pool):
            start_counts(pool, "scale_weights", "weights_hi", "weights_lo", "scale_out", "out_hi", "out_lo", "times_sin",
                         "rope_add")
            nc.gpsimd.memset(unit[:, 0:1], 1.0).then_inc(unit_ready, 1)
            nc.gpsimd.memset(unit[:, 1:2], SCALE).then_inc(unit_ready, 1)
            pool.wait_ge(unit_ready, 2)
            one, score_scale = unit[:, 0:1], unit[:, 1:2]

            def stages(it, plan):
                for item in plan:
                    kind, *which = item
                    if kind in ("scale_weights", "weights_hi", "weights_lo"):
                        who, n = which
                        source = raw_q[n % 2] if who == "q" else raw_kv
                        w = wq_sb[:, n % 2] if who == "q" else wkv_sb
                    if kind == "scale_weights":
                        load = f"load_q{n % 2}"
                        pool.wait_ge(done[load], loaded(it, load, who, n))
                        nc.gpsimd.tensor_tensor(source[:, :, :], source[:, :, :], column(score_scale, source), ALU.mult
                                                ).then_inc(done[kind], 1)
                    if kind == "weights_hi":
                        if who == "q":
                            pool.wait_ge(done["scale_weights"], count(it, "scale_weights", who, n))
                        else:
                            pool.wait_ge(done[f"load_{who}"], loaded(it, f"load_{who}", who, n))
                        if who == "q":
                            wait_stage(pool, it, "project", "q", n - 2)
                        else:
                            wait_last_kv(pool, it, "project", who, n)
                        nc.gpsimd.tensor_tensor(w[:, 0], source[:, :, :], column(one, source), ALU.mult).then_inc(done[kind], 1)
                    if kind == "weights_lo":
                        pool.wait_ge(done["weights_hi"], count(it, "weights_hi", who, n))
                        nc.gpsimd.tensor_tensor(w[:, 1], source[:, :, :], w[:, 0].bitcast(F32), ALU.subtract).then_inc(done[kind], 1)
                    if kind == "scale_out":
                        (pair,) = which
                        pool.wait_ge(done["load_o"], loaded(it, "load_o", pair))
                        if it is None or pair == 0:
                            pool.wait_ge(tables_loaded, 3 * 16)
                        scales = head_scale[:, bass.ds(in_sequence(it, "q", 2 * pair), 2)].rearrange("p (h a) -> p h a", a=1)
                        nc.gpsimd.tensor_tensor(raw_o[:, :, :], raw_o[:, :, :], scales.broadcast_to([P, 2, D]), ALU.mult
                                                ).then_inc(done[kind], 1)
                    if kind == "out_hi":
                        (pair,) = which
                        pool.wait_ge(done["scale_out"], count(it, "scale_out", pair))
                        wait_stage(pool, it, "output", pair - 1, 1)
                        nc.gpsimd.tensor_tensor(wo_sb[:, 0], raw_o[:, :, :], column(one, raw_o), ALU.mult).then_inc(done[kind], 1)
                    if kind == "out_lo":
                        (pair,) = which
                        pool.wait_ge(done["out_hi"], count(it, "out_hi", pair))
                        nc.gpsimd.tensor_tensor(wo_sb[:, 1], raw_o[:, :, :], wo_sb[:, 0].bitcast(F32), ALU.subtract
                                                ).then_inc(done[kind], 1)
                    if kind == "times_sin":
                        pool.wait_ge(done["swap"], loaded(it, "swap", *which))
                        if it is None:
                            pool.wait_ge(tables_loaded, 3 * 16)
                        nc.gpsimd.tensor_tensor(rotated[:, :], rotated[:, :], sin_sb[:, :], ALU.mult).then_inc(done[kind], 1)
                    if kind == "rope_add":
                        pool.wait_ge(done["times_cos"], count(it, "times_cos", *which))
                        pool.wait_ge(done["times_sin"], count(it, "times_sin", *which))
                        nc.gpsimd.tensor_tensor(cos_part[:, :], cos_part[:, :], rotated[:, :], ALU.add).then_inc(done[kind], 1)

            turns(pool, stages)


def plan_experts(experts, tiles):
    plan = [(kind,) for kind in ("stats_1", "std_1", "norm_1", "stats_2", "std_2", "affine", "lengths", "unit_scale",
                                 "rows_hi", "rows_lo", "unit_rows")]
    for part in range(2):
        for c in range(2):
            plan.extend([("turn_rows", part, c), ("rows_turned", part, c)])

    def turn(kind, copied, *which):
        plan.extend([(kind, *which, 0), (kind, *which, 1), (copied + "_hi", *which), (copied + "_lo", *which)])

    def gather(w, piece):
        plan.append(("gather", w, piece))
        if piece % 2:
            plan.append(("gathered", w, piece // 2))

    plan.extend([("slot_logits", 0), ("slot_max", 0), ("slot_exp", 0), ("slot_split", 0)])
    for e in range(experts):
        if e + 1 < experts:
            plan.extend([("slot_logits", e + 1), ("slot_max", e + 1)])
        turn("turn_dispatch", "dispatched", e, 0)
        if e + 1 < experts:
            plan.append(("slot_exp", e + 1))
        if e >= 4:
            gather(e // 4 - 1, e % 4)
        turn("turn_dispatch", "dispatched", e, 1)
        if e + 1 < experts:
            plan.append(("slot_split", e + 1))
    for piece in range(4):
        gather(experts // 4 - 1, piece)
    for w in range(experts // 4):
        plan.extend([("hidden_layer", w), ("gelu", w)])
    for w in range(experts // 4):
        plan.extend([("output_layer", w), ("slots_hi", w), ("slots_lo", w)])

    def split_row(t, half):
        plan.extend([("row_hi", t, half), ("row_lo", t, half)])

    plan.extend([(kind, 0, half) for half in range(2) for kind in ("row_logits", "row_max")])
    plan.extend([("row_peak", 0), ("row_exp", 0, 0), ("row_exp", 0, 1)])
    split_row(0, 0)
    split_row(0, 1)
    for t in range(tiles):
        following = t + 1 < tiles
        for quad in range(4):
            if following and quad < 2:
                plan.extend([("row_logits", t + 1, quad), ("row_max", t + 1, quad)])
            turn("turn_combine", "combined", t, quad)
            if quad:
                plan.append(("spread", t, quad - 1))
            if following and quad == 1:
                plan.extend([("row_peak", t + 1), ("row_exp", t + 1, 0)])
            if following and quad == 2:
                plan.append(("row_exp", t + 1, 1))
            if following and quad == 3:
                split_row(t + 1, 0)
        plan.append(("spread", t, 3))
        if following:
            split_row(t + 1, 1)
        plan.append(("add_rows", t))
    plan.extend([("stats_3",), ("std_3",), ("norm_3",)])
    return plan


def order_sequences(sequences, plan):
    front = [item for item in plan[:plan.index(("unit_rows",))]]
    tail = plan[-3:]
    middle = plan[len(front):-3]
    between = {0: front[0:2], 1: front[2:3], 2: front[3:5], 3: front[5:6], 4: front[6:8], 5: front[8:]}
    order = [(0, item) for item in front]
    for b in range(sequences):
        for item in middle:
            order.append((b, item))
            if item[0] == "add_rows" and b + 1 < sequences:
                order.extend((b + 1, other) for other in between.get(item[1], ()))
            if item == ("slot_split", 2) and b:
                order.extend((b - 1, other) for other in tail)
    return order + [(sequences - 1, item) for item in tail]


def soft_experts(nc, y_sb, exps, mu_loaded, gamma_d, beta_d, mu_d, scale_d, w1_d, b1_d, w2_d, b2_d, ident_d, out_d):
    B, N, D = out_d.shape
    _, E, S = mu_d.shape
    H = w1_d.shape[2]
    TILES = N // P
    KT = D // P
    ES = E * S
    assert S == P and KT == 2
    plan = plan_experts(E, TILES)
    order = order_sequences(B, plan)
    kinds, at = {}, {}
    for item in plan:
        at[item] = kinds.get(item[0], 0)
        kinds[item[0]] = at[item] + 1

    with ExitStack() as ctx:
        def sb(name, shape, dt=F32):
            return ctx.enter_context(nc.sbuf_tensor(f"ffn_{name}", shape, dt))

        def psum(name, shape, dt=F32):
            return ctx.enter_context(nc.psum_tensor(f"ffn_{name}", shape, dt))

        def sem(name):
            return ctx.enter_context(nc.semaphore(f"ffn_{name}"))

        rows = sb("rows", [P, 2, TILES, D], F32R)
        rowsT = sb("rowsT", [P, 2, KT, N], F32R)
        mu = sb("mu", [P, 2, KT, ES], F32R)
        slots = sb("slots", [P, 2, E, D], F32R)
        parts = sb("parts", [P, 2, ES], F32R)
        turned_sb = sb("turned_sb", [P, 2, 2, ES], F32R)
        gathered = sb("gathered", [P, KT, ES])
        hidden = sb("hidden_h", [P, ES])
        w2_sb = exps[0:H + 1, 0, :].rearrange("p (a e d) -> p a e d", a=2, e=4)
        w1_sb = exps[:, 1, :].rearrange("p (c e h) -> p c e h", c=KT, e=E)
        b1_sb = sb("b1_sb", [H, E])
        gamma = sb("gamma", [P, D])
        beta = sb("beta", [P, D])
        scale = sb("scale", [P, 1])
        ident = sb("ident2", [P, P])
        ident_r = sb("ident2_r", [P, P], F32R)
        ones = sb("ones", [P, P])
        moments = sb("moments", [P, TILES, 6])
        mean_var = sb("mean_var", [P, TILES, 2])
        spread_sq = sb("spread_sq", [P, TILES])
        std = sb("std", [P, TILES])
        row_scale = sb("row_scale", [P, TILES])
        inv_std = sb("inv_std", [P, TILES])
        neg_max = sb("neg_max2", [P, 2])
        half_max = sb("half_max", [P, 2, 2])
        total = sb("total", [P, 2, 2])
        inv_total = sb("inv_total", [P, 2])
        ring = psum("ring2", [P, 4 * BANK])
        turned = psum("turned2", [P, 2, BANK], F32R)
        mix = psum("mix2", [P, 2, BANK])

        done = {kind: sem(f"{kind}_done") for kind in kinds}
        consts_loaded, w1_loaded = sem("consts2_loaded"), sem("w1_loaded")
        w2_loaded = [sem("w2_even_loaded"), sem("w2_odd_loaded")]
        ones_ready, ident_ready, squares_ready, sums_ready, norms_ready, mu_ready = (
            sem("ones_ready"), sem("ident_ready"), sem("squares_ready"), sem("sums_ready"), sem("norms_ready"), sem("mu_ready"))
        ones_row_ready, inv_ready, mu_scaled, mu_hi_ready = sem("ones_row_ready"), sem("inv_ready"), sem("mu_scaled"), sem("mu_hi_ready")
        dve_step, act_step, stored = sem("dve_step2"), sem("act_step2"), sem("stored")

        def count(b, kind, *which):
            return b * kinds[kind] + at[(kind, *which)] + 1

        def dispatch_sb(w, part):
            flat = slots[:, part].rearrange("p e d -> p (e d)") if w % 2 else turned_sb[:, part].rearrange("p a n -> p (a n)")
            return flat.rearrange("p (t n) -> p t n", n=BANK)

        block = ctx.enter_context(nc.Block())

        def free_dispatch(engine, b, e, half):
            if e % 4 == 0 and half == 0:
                if e >= 8:
                    engine.wait_ge(done["gather"], count(b, "gather", e // 4 - 2, 3))
                else:
                    engine.wait_ge(done["spread"], b * kinds["spread"])

        def free_combine(engine, b, t, quad):
            if t >= 2:
                engine.wait_ge(done["spread"], count(b, "spread", t - 2, quad))
            else:
                engine.wait_ge(done["gather"], (b + 1) * kinds["gather"])

        def y_rows(b, t=0, n=TILES):
            return y_sb[:, bass.ds(b * TILES + t, n), :].rearrange("p t d -> p (t d)")

        @block.sync
        def _(sp):
            sp.dma_start(ident[:, :], ident_d).then_inc(consts_loaded, 16)
            sp.dma_start(gamma[:, :], gamma_d.rearrange("(a d) -> a d", a=1).broadcast_to([P, D])).then_inc(consts_loaded, 16)
            sp.dma_start(beta[:, :], beta_d.rearrange("(a d) -> a d", a=1).broadcast_to([P, D])).then_inc(consts_loaded, 16)
            sp.dma_start(scale[:, :], scale_d.rearrange("(a d) -> a d", a=1).broadcast_to([P, 1])).then_inc(consts_loaded, 16)
            sp.dma_start(b1_sb[:, :], b1_d.rearrange("e h -> h e"), allow_slow_non_contiguous=True).then_inc(consts_loaded, 16)
            for b in range(B):
                sp.wait_ge(done["slot_split"], (b + 1) * kinds["slot_split"])
                for c in range(KT):
                    sp.dma_start(w1_sb[:, c], w1_d[:, c * P:(c + 1) * P, :].rearrange("e p h -> p e h")).then_inc(w1_loaded, 16)
                for w in range(E // 4):
                    if w >= 2:
                        sp.wait_ge(done["output_layer"], count(b, "output_layer", w - 2))
                    else:
                        sp.wait_ge(done["output_layer"], b * kinds["output_layer"])
                    sp.dma_start(w2_sb[0:H, w % 2], w2_d[4 * w:4 * w + 4].rearrange("e h d -> h e d")).then_inc(w2_loaded[w % 2], 16)
                    sp.dma_start(w2_sb[H:H + 1, w % 2], b2_d[4 * w:4 * w + 4].rearrange("(a e) d -> a e d", a=1)
                                 ).then_inc(w2_loaded[w % 2], 16)
                sp.wait_ge(done["norm_3"], b + 1)
                sp.dma_start(out_d[bass.ds(b, 1)].rearrange("a (t p) d -> p (a t) d", p=P),
                             y_sb[:, bass.ds(b * TILES, TILES), :]).then_inc(stored, 16)
            sp.wait_ge(stored, 16 * B)

        @block.tensor
        def _(pe):
            pe.wait_ge(ones_ready, 1)
            pe.wait_ge(squares_ready, 1)
            for q in range(ES // BANK):
                for c in range(KT):
                    last = nc.tensor.matmul(ring[:, q * BANK:(q + 1) * BANK], ones[:, :], gathered[:, c, q * BANK:(q + 1) * BANK],
                                            start=c == 0, stop=c == KT - 1)
            last.then_inc(sums_ready, 1)
            pe.wait_ge(ident_ready, 1)
            passes = [(c, a, m) for c in range(KT) for a, m in PARTS]
            for b, (kind, *which) in order:
                if kind == "turn_rows":
                    part, c = which
                    n = at[(kind, part, c)]
                    if n == 0:
                        pe.wait_ge(done["unit_rows"], b + 1)
                        pe.wait_ge(done["row_exp"], b * kinds["row_exp"])
                    if n >= 2:
                        pe.wait_ge(done["rows_turned"], b * kinds["rows_turned"] + n - 1)
                    unit = parts[:, part, :].rearrange("p (t d) -> p t d", d=D)
                    for t in range(TILES):
                        last = nc.tensor.transpose(ring[:, (n % 2) * N + t * P:(n % 2) * N + (t + 1) * P].bitcast(F32R),
                                                   unit[:, t, c * P:(c + 1) * P], ident_r[:, :])
                    last.then_inc(done[kind], 1)
                if kind == "slot_logits":
                    (e,) = which
                    if e == 0:
                        pe.wait_ge(mu_ready, 1)
                        pe.wait_ge(done["rows_turned"], (b + 1) * kinds["rows_turned"])
                    if e >= 2:
                        pe.wait_ge(done["slot_exp"], count(b, "slot_exp", e - 2))
                    for half in range(N // BANK):
                        at_col = (e % 2) * N + half * BANK
                        for n, (c, a, m) in enumerate(passes):
                            last = nc.tensor.matmul(ring[:, at_col:at_col + BANK], mu[:, a, c, e * P:(e + 1) * P],
                                                    rowsT[:, m, c, half * BANK:(half + 1) * BANK],
                                                    start=n == 0, stop=n == len(passes) - 1)
                    last.then_inc(done[kind], 1)
                if kind == "turn_dispatch":
                    e, half, part = which
                    n = at[(kind, *which)]
                    if half == 0 and part == 0:
                        pe.wait_ge(done["slot_split"], count(b, "slot_split", e))
                    copied = "lo" if part else "hi"
                    if n >= 2:
                        pe.wait_ge(done[f"dispatched_{copied}"], b * kinds["dispatched_hi"] + n // 2)
                    else:
                        pe.wait_ge(done[f"combined_{copied}"], b * kinds["combined_hi"])
                    for t in range(4):
                        col = (e % 2) * N + (4 * half + t) * P
                        last = nc.tensor.transpose(turned[:, part, t * P:(t + 1) * P], parts[:, part, col:col + P], ident_r[:, :])
                    last.then_inc(done[kind], 1)
                if kind == "gather":
                    w, piece = which
                    c = piece // 2
                    if piece == 0:
                        pe.wait_ge(done["dispatched_hi"], count(b, "dispatched_hi", 4 * w + 3, 1))
                        pe.wait_ge(done["dispatched_lo"], count(b, "dispatched_lo", 4 * w + 3, 1))
                        pe.wait_ge(done["rows_lo"], b + 1)
                    if w:
                        pe.wait_ge(done["gathered"], count(b, "gathered", w - 1, c))
                    else:
                        pe.wait_ge(done["add_rows"], b * kinds["add_rows"])
                    for t in range(4 * (piece % 2), 4 * (piece % 2) + 4):
                        for n, (a, m) in enumerate(PARTS):
                            last = nc.tensor.matmul(mix[:, c, :], rows[:, a, t, c * P:(c + 1) * P], dispatch_sb(w, m)[:, t, :],
                                                    start=t == 0 and n == 0, stop=t == TILES - 1 and n == 2)
                    last.then_inc(done[kind], 1)
                if kind == "hidden_layer":
                    (w,) = which
                    pe.wait_ge(done["gathered"], count(b, "gathered", w, 1))
                    if w == 0:
                        pe.wait_ge(w1_loaded, (b + 1) * (KT * 16))
                        pe.wait_ge(done["slot_exp"], (b + 1) * kinds["slot_exp"])
                    for k in range(4):
                        e = 4 * w + k
                        for c in range(KT):
                            last = nc.tensor.matmul(ring[0:H, e * P:(e + 1) * P], w1_sb[:, c, e, :],
                                                    gathered[:, c, e * P:(e + 1) * P], start=c == 0, stop=c == KT - 1)
                    last.then_inc(done[kind], 1)
                if kind == "output_layer":
                    (w,) = which
                    pe.wait_ge(done["gelu"], (b + 1) * kinds["gelu"])
                    pe.wait_ge(w2_loaded[w % 2], b * 64 + 32 * (w // 2 + 1))
                    if w >= 2:
                        pe.wait_ge(done["slots_lo"], count(b, "slots_lo", w - 2))
                    for k in range(4):
                        e = 4 * w + k
                        at_col = (w % 2) * 2 * BANK + k * D
                        last = nc.tensor.matmul(ring[:, at_col:at_col + D], hidden[0:H + 1, e * P:(e + 1) * P],
                                                w2_sb[:, w % 2, k, :], start=True, stop=True)
                    last.then_inc(done[kind], 1)
                if kind == "row_logits":
                    t, half = which
                    if t:
                        pe.wait_ge(done["row_exp"], count(b, "row_exp", t - 1, half))
                    else:
                        pe.wait_ge(done["slots_lo"], (b + 1) * kinds["slots_lo"])
                    for q in (2 * half, 2 * half + 1):
                        for n, (c, a, m) in enumerate(passes):
                            last = nc.tensor.matmul(ring[:, q * BANK:(q + 1) * BANK], rowsT[:, a, c, t * P:(t + 1) * P],
                                                    mu[:, m, c, q * BANK:(q + 1) * BANK], start=n == 0, stop=n == len(passes) - 1)
                    last.then_inc(done[kind], 1)
                if kind == "turn_combine":
                    t, quad, part = which
                    n = at[(kind, *which)]
                    if quad % 2 == 0 and part == 0:
                        pe.wait_ge(done["row_lo"], count(b, "row_lo", t, quad // 2))
                    copied = "lo" if part else "hi"
                    if n >= 2:
                        pe.wait_ge(done[f"combined_{copied}"], b * kinds["combined_hi"] + n // 2)
                    else:
                        pe.wait_ge(done[f"dispatched_{copied}"], (b + 1) * kinds["dispatched_hi"])
                    for k in range(4):
                        col = (4 * quad + k) * P
                        last = nc.tensor.transpose(turned[:, part, k * P:(k + 1) * P], parts[:, part, col:col + P], ident_r[:, :])
                    last.then_inc(done[kind], 1)
                if kind == "spread":
                    t, quad = which
                    pe.wait_ge(done["combined_hi"], count(b, "combined_hi", t, quad))
                    pe.wait_ge(done["combined_lo"], count(b, "combined_lo", t, quad))
                    if quad == 0:
                        if t >= 2:
                            pe.wait_ge(done["add_rows"], count(b, "add_rows", t - 2))
                        else:
                            pe.wait_ge(done["gathered"], (b + 1) * kinds["gathered"])
                    for e in range(4 * quad, 4 * quad + 4):
                        for n, (a, m) in enumerate(PARTS):
                            last = nc.tensor.matmul(mix[:, t % 2, 0:D], turned_sb[:, t % 2, a, e * P:(e + 1) * P],
                                                    slots[:, m, e, :], start=e == 0 and n == 0, stop=e == E - 1 and n == 2)
                    last.then_inc(done[kind], 1)

        @block.scalar
        def _(act):
            act.wait_ge(mu_loaded, 16)
            nc.scalar.activation(gathered[:, :, :], exps[:, :, :], ACT.Square).then_inc(squares_ready, 1)
            for b, (kind, *which) in order:
                if kind in ("std_1", "std_2", "std_3"):
                    act.wait_ge(done[kind.replace("std", "stats")], b + 1)
                    nc.scalar.activation(std[:, :], spread_sq[:, :], ACT.Sqrt).then_inc(done[kind], 1)
                if kind == "std_2" and b == 0:
                    act.wait_ge(sums_ready, 1)
                    nc.scalar.activation(hidden[:, :], ring[:, :], ACT.Sqrt).then_inc(norms_ready, 1)
                if kind == "lengths":
                    act.wait_ge(done["affine"], b + 1)
                    for t in range(TILES):
                        nc.scalar.activation(gathered[:, 1, t * D:(t + 1) * D], gathered[:, 0, t * D:(t + 1) * D], ACT.Square,
                                             accum_out=spread_sq[:, t:t + 1]).then_inc(act_step, 1)
                    act.wait_ge(act_step, (b + 1) * TILES)
                    nc.scalar.activation(std[:, :], spread_sq[:, :], ACT.Sqrt).then_inc(done[kind], 1)
                if kind == "rows_hi":
                    act.wait_ge(done["gather"], b * kinds["gather"])
                    nc.scalar.activation(rows[:, 0].rearrange("p t d -> p (t d)"), gathered[:, 0, :], ACT.Copy).then_inc(done[kind], 1)
                if kind == "rows_hi" and b == 0:
                    act.wait_ge(mu_scaled, 1)
                    nc.scalar.activation(mu[:, 0], exps[:, :, :], ACT.Copy).then_inc(mu_hi_ready, 1)
                if kind == "rows_turned":
                    part, c = which
                    n = at[(kind, part, c)]
                    act.wait_ge(done["turn_rows"], count(b, "turn_rows", part, c))
                    nc.scalar.activation(rowsT[:, part, c, :], ring[:, (n % 2) * N:(n % 2 + 1) * N], ACT.Copy).then_inc(done[kind], 1)
                if kind == "slot_exp":
                    (e,) = which
                    act.wait_ge(done["slot_max"], count(b, "slot_max", e))
                    if e >= 2:
                        act.wait_ge(done["slot_split"], count(b, "slot_split", e - 2))
                    if e == 0:
                        act.wait_ge(mu_ready, 1)
                    nc.scalar.activation(exps[:, e % 2, 0:N], ring[:, (e % 2) * N:(e % 2 + 1) * N], ACT.Exp,
                                         bias=neg_max[:, e % 2:e % 2 + 1], accum_out=total[:, e % 2, 0:1]
                                         ).then_inc(done[kind], 1)
                if kind == "dispatched_hi":
                    e, half = which
                    act.wait_ge(done["turn_dispatch"], count(b, "turn_dispatch", e, half, 0))
                    free_dispatch(act, b, e, half)
                    nc.scalar.activation(dispatch_sb(e // 4, 0)[:, 4 * half:4 * half + 4, (e % 4) * P:(e % 4 + 1) * P],
                                         turned[:, 0, :].bitcast(F32).rearrange("p (t n) -> p t n", n=P), ACT.Copy
                                         ).then_inc(done[kind], 1)
                if kind == "gelu":
                    (w,) = which
                    act.wait_ge(done["hidden_layer"], count(b, "hidden_layer", w))
                    if w == 0:
                        act.wait_ge(ones_row_ready, 1)
                        act.wait_ge(consts_loaded, 5 * 16)
                        act.wait_ge(done["output_layer"], b * kinds["output_layer"])
                    for k in range(4):
                        e = 4 * w + k
                        last = nc.scalar.activation(hidden[0:H, e * P:(e + 1) * P], ring[0:H, e * P:(e + 1) * P], ACT.Gelu,
                                                    bias=b1_sb[:, e:e + 1])
                    last.then_inc(done[kind], 1)
                if kind == "slots_hi":
                    (w,) = which
                    act.wait_ge(done["output_layer"], count(b, "output_layer", w))
                    if w == 0:
                        act.wait_ge(done["gather"], (b + 1) * kinds["gather"])
                    nc.scalar.activation(slots[:, 0, 4 * w:4 * w + 4, :].rearrange("p e d -> p (e d)"),
                                         ring[:, (w % 2) * 2 * BANK:(w % 2 + 1) * 2 * BANK], ACT.Copy).then_inc(done[kind], 1)
                if kind == "row_exp":
                    t, half = which
                    act.wait_ge(done["row_peak"], count(b, "row_peak", t))
                    if t >= 2:
                        act.wait_ge(done["row_lo"], count(b, "row_lo", t - 2, half))
                        act.wait_ge(done["add_rows"], count(b, "add_rows", t - 2))
                    else:
                        act.wait_ge(done["slot_split"], (b + 1) * kinds["slot_split"])
                    cols = slice(half * (ES // 2), (half + 1) * (ES // 2))
                    nc.scalar.activation(exps[:, t % 2, cols], ring[:, cols], ACT.Exp, bias=neg_max[:, t % 2:t % 2 + 1],
                                         accum_out=total[:, t % 2, half:half + 1]).then_inc(done[kind], 1)
                if kind == "row_hi":
                    t, half = which
                    act.wait_ge(done["row_exp"], count(b, "row_exp", t, half))
                    if t:
                        act.wait_ge(done["turn_combine"], count(b, "turn_combine", t - 1, 2 * half + 1, 1))
                    else:
                        act.wait_ge(done["turn_dispatch"], (b + 1) * kinds["turn_dispatch"])
                    cols = slice(half * (ES // 2), (half + 1) * (ES // 2))
                    nc.scalar.activation(parts[:, 0, cols], exps[:, t % 2, cols], ACT.Copy).then_inc(done[kind], 1)
                if kind == "combined_hi":
                    t, quad = which
                    act.wait_ge(done["turn_combine"], count(b, "turn_combine", t, quad, 0))
                    free_combine(act, b, t, quad)
                    nc.scalar.activation(turned_sb[:, t % 2, 0, quad * BANK:(quad + 1) * BANK], turned[:, 0, :].bitcast(F32),
                                         ACT.Copy).then_inc(done[kind], 1)

        @block.vector
        def _(dve):
            steps = [0]

            def step(instruction):
                instruction.then_inc(dve_step, 1)
                steps[0] += 1

            def settle():
                dve.wait_ge(dve_step, steps[0])

            nc.vector.memset(ones[:, :], 1.0).then_inc(ones_ready, 1)

            for b, (kind, *which) in order:
                if kind == "affine" and b == 0:
                    dve.wait_ge(consts_loaded, 5 * 16)
                    nc.vector.tensor_copy(ident_r[:, :], ident[:, :]).then_inc(ident_ready, 1)
                    dve.wait_ge(norms_ready, 1)
                    step(nc.vector.tensor_scalar(hidden[:, :], hidden[:, :], L2_EPS, None, ALU.max))
                    settle()
                    nc.vector.reciprocal(hidden[:, :], hidden[:, :]).then_inc(inv_ready, 1)
                if kind in ("stats_1", "stats_2", "stats_3"):
                    if kind == "stats_2":
                        dve.wait_ge(done["norm_1"], b + 1)
                    elif kind == "stats_3":
                        dve.wait_ge(done["add_rows"], (b + 1) * kinds["add_rows"])
                    for t in range(TILES):
                        step(nc.vector.bn_stats(moments[:, t, :], y_rows(b, t, 1)))
                    settle()
                    for t in range(TILES):
                        step(nc.vector.bn_aggr(mean_var[:, t, :], moments[:, t, :]))
                    settle()
                    nc.vector.tensor_scalar(spread_sq[:, :], mean_var[:, :, 1:2].rearrange("p t a -> p (t a)"), LN_EPS, None, ALU.add
                                            ).then_inc(done[kind], 1)
                if kind in ("norm_1", "norm_3"):
                    dve.wait_ge(done["std_1" if kind == "norm_1" else "std_3"], b + 1)
                    step(nc.vector.reciprocal(inv_std[:, :], std[:, :]))
                    settle()
                    for t in range(TILES):
                        last = nc.vector.tensor_scalar(y_rows(b, t, 1), y_rows(b, t, 1), mean_var[:, t, 0:1], inv_std[:, t:t + 1],
                                                       ALU.subtract, ALU.mult)
                    last.then_inc(done[kind], 1)
                if kind == "affine":
                    dve.wait_ge(done["hidden_layer"], b * kinds["hidden_layer"])
                    dve.wait_ge(sums_ready, 1)
                    dve.wait_ge(done["std_2"], b + 1)
                    step(nc.vector.reciprocal(inv_std[:, :], std[:, :]))
                    settle()
                    for t in range(TILES):
                        step(nc.vector.tensor_scalar(gathered[:, 0, t * D:(t + 1) * D], y_rows(b, t, 1), mean_var[:, t, 0:1],
                                                     inv_std[:, t:t + 1], ALU.subtract, ALU.mult))
                    settle()
                    x_ln = gathered[:, 0, :].rearrange("p (t d) -> p t d", d=D)
                    every = [P, TILES, D]
                    step(nc.vector.tensor_tensor(x_ln, x_ln, gamma[:, :].rearrange("p (a d) -> p a d", a=1).broadcast_to(every), ALU.mult))
                    settle()
                    nc.vector.tensor_tensor(x_ln, x_ln, beta[:, :].rearrange("p (a d) -> p a d", a=1).broadcast_to(every), ALU.add
                                            ).then_inc(done[kind], 1)
                if kind == "unit_scale":
                    dve.wait_ge(done["lengths"], b + 1)
                    step(nc.vector.tensor_scalar(std[:, :], std[:, :], L2_EPS, None, ALU.max))
                    settle()
                    step(nc.vector.reciprocal(inv_std[:, :], std[:, :]))
                    settle()
                    nc.vector.tensor_scalar(row_scale[:, :], inv_std[:, :], scale[:, 0:1], None, ALU.mult).then_inc(done[kind], 1)
                if kind == "unit_rows":
                    dve.wait_ge(done["unit_scale"], b + 1)
                    dve.wait_ge(done["turn_combine"], b * kinds["turn_combine"])
                    for t in range(TILES):
                        cols = slice(t * D, (t + 1) * D)
                        step(nc.vector.tensor_scalar(parts[:, 0, cols], gathered[:, 0, cols], row_scale[:, t:t + 1], None, ALU.mult))
                    settle()
                    for t in range(TILES):
                        cols = slice(t * D, (t + 1) * D)
                        last = nc.vector.scalar_tensor_tensor(parts[:, 1, cols], gathered[:, 0, cols], row_scale[:, t:t + 1],
                                                              parts[:, 0, cols].bitcast(F32), ALU.mult, ALU.subtract)
                    last.then_inc(done[kind], 1)
                if kind == "unit_rows" and b == 0:
                    dve.wait_ge(mu_scaled, 1)
                    nc.vector.memset(hidden[H:H + 1, :], 1.0).then_inc(ones_row_ready, 1)
                if kind == "rows_lo":
                    dve.wait_ge(done["rows_hi"], b + 1)
                    nc.vector.tensor_tensor(rows[:, 1].rearrange("p t d -> p (t d)"), gathered[:, 0, :],
                                            rows[:, 0].rearrange("p t d -> p (t d)").bitcast(F32), ALU.subtract).then_inc(done[kind], 1)
                if kind == "slot_max":
                    (e,) = which
                    dve.wait_ge(done["slot_logits"], count(b, "slot_logits", e))
                    if e >= 2:
                        dve.wait_ge(done["slot_exp"], count(b, "slot_exp", e - 2))
                    nc.vector.tensor_reduce(neg_max[:, e % 2:e % 2 + 1], ring[:, (e % 2) * N:(e % 2 + 1) * N], AX_X, ALU.max,
                                            negate=True).then_inc(done[kind], 1)
                if kind == "slot_split":
                    (e,) = which
                    dve.wait_ge(done["slot_exp"], count(b, "slot_exp", e))
                    step(nc.vector.reciprocal(inv_total[:, e % 2:e % 2 + 1], total[:, e % 2, 0:1]))
                    settle()
                    if e >= 2:
                        dve.wait_ge(done["turn_dispatch"], count(b, "turn_dispatch", e - 2, TILES // 4 - 1, 1))
                    else:
                        dve.wait_ge(done["turn_rows"], (b + 1) * kinds["turn_rows"])
                    cols = slice((e % 2) * N, (e % 2 + 1) * N)
                    step(nc.vector.tensor_scalar(parts[:, 0, cols], exps[:, e % 2, 0:N], inv_total[:, e % 2:e % 2 + 1], None, ALU.mult))
                    settle()
                    nc.vector.scalar_tensor_tensor(parts[:, 1, cols], exps[:, e % 2, 0:N], inv_total[:, e % 2:e % 2 + 1],
                                                   parts[:, 0, cols].bitcast(F32), ALU.mult, ALU.subtract).then_inc(done[kind], 1)
                if kind == "gathered":
                    w, c = which
                    dve.wait_ge(done["gather"], count(b, "gather", w, 2 * c + 1))
                    if w == 0:
                        dve.wait_ge(done["rows_hi"], b + 1)
                    nc.vector.tensor_copy(gathered[:, c, w * BANK:(w + 1) * BANK], mix[:, c, :]).then_inc(done[kind], 1)
                if kind == "dispatched_lo":
                    e, half = which
                    dve.wait_ge(done["turn_dispatch"], count(b, "turn_dispatch", e, half, 1))
                    free_dispatch(dve, b, e, half)
                    nc.vector.tensor_copy(dispatch_sb(e // 4, 1)[:, 4 * half:4 * half + 4, (e % 4) * P:(e % 4 + 1) * P],
                                          turned[:, 1, :].bitcast(F32).rearrange("p (t n) -> p t n", n=P)).then_inc(done[kind], 1)
                if kind == "slots_lo":
                    (w,) = which
                    dve.wait_ge(done["slots_hi"], count(b, "slots_hi", w))
                    nc.vector.tensor_tensor(slots[:, 1, 4 * w:4 * w + 4, :].rearrange("p e d -> p (e d)"),
                                            ring[:, (w % 2) * 2 * BANK:(w % 2 + 1) * 2 * BANK],
                                            slots[:, 0, 4 * w:4 * w + 4, :].rearrange("p e d -> p (e d)").bitcast(F32),
                                            ALU.subtract).then_inc(done[kind], 1)
                if kind == "row_max":
                    t, half = which
                    cols = slice(half * (ES // 2), (half + 1) * (ES // 2))
                    dve.wait_ge(done["row_logits"], count(b, "row_logits", t, half))
                    nc.vector.tensor_reduce(half_max[:, t % 2, half:half + 1], ring[:, cols], AX_X, ALU.max, negate=True
                                            ).then_inc(done[kind], 1)
                if kind == "row_peak":
                    (t,) = which
                    dve.wait_ge(done["row_max"], count(b, "row_max", t, 1))
                    if t >= 2:
                        dve.wait_ge(done["row_exp"], count(b, "row_exp", t - 2, 1))
                    else:
                        dve.wait_ge(done["slot_exp"], (b + 1) * kinds["slot_exp"])
                    nc.vector.tensor_tensor(neg_max[:, t % 2:t % 2 + 1], half_max[:, t % 2, 0:1], half_max[:, t % 2, 1:2], ALU.min
                                            ).then_inc(done[kind], 1)
                if kind == "row_lo":
                    t, half = which
                    cols = slice(half * (ES // 2), (half + 1) * (ES // 2))
                    dve.wait_ge(done["row_hi"], count(b, "row_hi", t, half))
                    nc.vector.tensor_tensor(parts[:, 1, cols], exps[:, t % 2, cols], parts[:, 0, cols].bitcast(F32), ALU.subtract
                                            ).then_inc(done[kind], 1)
                if kind == "combined_lo":
                    t, quad = which
                    dve.wait_ge(done["turn_combine"], count(b, "turn_combine", t, quad, 1))
                    free_combine(dve, b, t, quad)
                    nc.vector.tensor_copy(turned_sb[:, t % 2, 1, quad * BANK:(quad + 1) * BANK], turned[:, 1, :].bitcast(F32)
                                          ).then_inc(done[kind], 1)
                if kind == "add_rows":
                    (t,) = which
                    dve.wait_ge(done["row_exp"], count(b, "row_exp", t, 1))
                    step(nc.vector.tensor_tensor(inv_total[:, t % 2:t % 2 + 1], total[:, t % 2, 0:1], total[:, t % 2, 1:2], ALU.add))
                    settle()
                    step(nc.vector.reciprocal(inv_total[:, t % 2:t % 2 + 1], inv_total[:, t % 2:t % 2 + 1]))
                    settle()
                    dve.wait_ge(done["spread"], count(b, "spread", t, 3))
                    nc.vector.scalar_tensor_tensor(y_rows(b, t, 1), mix[:, t % 2, 0:D], inv_total[:, t % 2:t % 2 + 1],
                                                   y_rows(b, t, 1), ALU.mult, ALU.add).then_inc(done[kind], 1)

        @block.gpsimd
        def _(pool):
            pool.wait_ge(inv_ready, 1)
            for c in range(KT):
                last = nc.gpsimd.tensor_tensor(exps[:, c, :], exps[:, c, :], hidden[:, :], ALU.mult)
            last.then_inc(mu_scaled, 1)
            pool.wait_ge(mu_hi_ready, 1)
            nc.gpsimd.tensor_tensor(mu[:, 1], exps[:, :, :], mu[:, 0].bitcast(F32), ALU.subtract).then_inc(mu_ready, 1)


_INS = ["L0_attn_x", "L0_attn_Wq", "L0_attn_Wk", "L0_attn_Wv", "L0_attn_Wo", "L0_attn_head_scale", "L0_ffn_gamma",
        "L0_ffn_beta", "L0_ffn_mu", "L0_ffn_scale", "L0_ffn_W1", "L0_ffn_b1", "L0_ffn_W2", "L0_ffn_b2"]
_OUTS = [((2, 1024, 256), "float32")]


def constants(positions, head, base=10000.0):
    powers = (np.arange(0, head, 2, dtype=np.float32) / np.float32(head)).astype(np.float64)
    inv_freq = (1.0 / np.power(base, powers)).astype(np.float32)
    angles = (inv_freq[:, None] * np.arange(positions, dtype=np.float32)[None, :]).astype(np.float64)
    cos, sin = np.cos(angles).astype(np.float32), np.sin(angles).astype(np.float32)
    later = np.arange(P)[None, :] > np.arange(P)[:, None]
    return {"const_cos": np.concatenate([cos, cos]), "const_sin": np.concatenate([-sin, sin]),
            "const_ident": np.eye(P, dtype=np.float32),
            "const_hidden": np.where(later, np.float32(HIDDEN), np.float32(0.0))}


def program(nc, x, wq, wk, wv, wo, head_scale, gamma, beta, mu, scale, w1, b1, w2, b2, cos, sin, ident, hidden, out):
    B, N, D = x.shape
    with (nc.sbuf_tensor("y_sb", [P, B * N // P, D], F32) as y_sb,
          nc.sbuf_tensor("exps_and_mu", [P, D // P, mu.shape[1] * mu.shape[2]], F32) as exps, nc.semaphore("mu_loaded") as mu_loaded):
        attention(nc, y_sb, exps, mu_loaded, mu, x, wq, wk, wv, wo, head_scale, cos, sin, ident, hidden)
        soft_experts(nc, y_sb, exps, mu_loaded, gamma, beta, mu, scale, w1, b1, w2, b2, ident, out)


def kernel(**inputs):
    import numpy as _np
    import concourse.bacc as _bacc
    from concourse import mybir as _mybir
    from concourse.bass_utils import run_bass_kernel_spmd as _run

    nc = _bacc.Bacc("TRN2", target_bir_lowering=False, num_devices=1)
    arrays, args = {}, []
    for name in _INS:
        a = _np.ascontiguousarray(inputs[name])
        arrays[f"in_{name}_dram"] = a
        args.append(nc.dram_tensor(f"in_{name}_dram", a.shape, _mybir.dt.from_np(a.dtype), kind="ExternalInput").ap())
    for name, a in constants(1024, 128).items():
        arrays[f"{name}_dram"] = a
        args.append(nc.dram_tensor(f"{name}_dram", a.shape, _mybir.dt.from_np(a.dtype), kind="ExternalInput").ap())
    for i, (shape, dtype) in enumerate(_OUTS):
        dt = _mybir.dt.from_np(_np.dtype(dtype))
        args.append(nc.dram_tensor(f"out_{i}_dram", shape, dt, kind="ExternalOutput").ap())
    program(nc, *args)
    r = _run(nc, [arrays], core_ids=[0])
    got = tuple(r.results[0][f"out_{i}_dram"] for i in range(len(_OUTS)))
    return got[0]
```
